# Optimizing a Trainium2 kernel written in Bass

```python
import numpy as np
import jax
import jax.numpy as jnp

def _softmax(x, axis=-1):
    return jax.nn.softmax(x, axis=axis)

def _gelu(x):
    return jax.nn.gelu(x, approximate=True)

def _silu(x):
    return jax.nn.silu(x)

def _sigmoid(x):
    return jax.nn.sigmoid(x)

def _layernorm(x, axis=-1, eps=1e-05):
    m = jnp.mean(x, axis=axis, keepdims=True)
    v = jnp.var(x, axis=axis, keepdims=True)
    return (x - m) / jnp.sqrt(v + eps)

def _scatter_add(tgt, idx, src, axis=0):
    return tgt.at[idx].add(src)

def _segment_sum(src, seg, n):
    return jax.ops.segment_sum(src, seg, n)
kernel_name = 'mk_adaln_ffn_d2_seqx_r8_5ba528'

def setup_inputs(seed: int=0):
    np.random.seed(seed)
    _w = jnp.asarray

    def _rec_inputs():
        import jax
        import jax.numpy as jnp
        _rk = jax.random.key(seed)
        x = -0.000125 + 0.9999 * jax.random.normal(jax.random.fold_in(_rk, 1), (32, 128, 128), jnp.float32)
        _lenS = 128 - jax.random.randint(jax.random.fold_in(_rk, 7), (32,), 0, max(1, 128 // 4) + 1, jnp.int32)
        _lenS2 = 128 - jax.random.randint(jax.random.fold_in(_rk, 8), (32,), 0, max(1, 128 // 4) + 1, jnp.int32)
        cond_1024 = -0.00493535 + 1.00056 * jax.random.normal(jax.random.fold_in(_rk, 11), (32, 128), jnp.float32)
        return (x, cond_1024)
    x, cond_1024 = _rec_inputs()

    def _L0_cond_setup():
        import jax, jax.numpy as jnp
        import numpy as np
        INPUT_DIM = 128
        HIDDEN_DIM = 128
        CHUNK_SIZE = 4

        def _linear_params(key, fan_in, fan_out):
            kw, kb = jax.random.split(key)
            bound = 1.0 / np.sqrt(fan_in)
            W = jax.random.uniform(kw, (fan_in, fan_out), jnp.float32, -bound, bound)
            b = jax.random.uniform(kb, (fan_out,), jnp.float32, -bound, bound)
            return (W, b)

        def _gru_forward(x, h0, Wz, bz, Wr, br, Wh, bh, Wp, bp):
            B, T, D = x.shape
            t = jnp.arange(T)
            do_prop = ((t + 1) % CHUNK_SIZE == 0) & (t < T - 1)
            xs = jnp.transpose(x, (1, 0, 2))

            def step(h, inp):
                x_t, prop = inp
                comb = jnp.concatenate([x_t, h], axis=-1)
                z = jax.nn.sigmoid(comb @ Wz + bz)
                r = jax.nn.sigmoid(comb @ Wr + br)
                comb2 = jnp.concatenate([x_t, r * h], axis=-1)
                h_cand = jnp.tanh(comb2 @ Wh + bh)
                h_new = (1.0 - z) * h + z * h_cand
                h_next = jnp.where(prop, jnp.tanh(h_new @ Wp + bp), h_new)
                return (h_next, h_new)
            _, ys = jax.lax.scan(step, h0, (xs, do_prop))
            return jnp.transpose(ys, (1, 0, 2))
        key = jax.random.key(seed)
        ks = jax.random.split(key, 6)
        x = jax.random.normal(ks[0], (64, 64, INPUT_DIM), jnp.float32)
        h0 = jax.random.normal(ks[1], (64, HIDDEN_DIM), jnp.float32)
        Wz, bz = _linear_params(ks[2], INPUT_DIM + HIDDEN_DIM, HIDDEN_DIM)
        Wr, br = _linear_params(ks[3], INPUT_DIM + HIDDEN_DIM, HIDDEN_DIM)
        Wh, bh = _linear_params(ks[4], INPUT_DIM + HIDDEN_DIM, HIDDEN_DIM)
        Wp, bp = _linear_params(ks[5], HIDDEN_DIM, HIDDEN_DIM)
        return {'x': x, 'h0': h0, 'Wz': Wz, 'bz': bz, 'Wr': Wr, 'br': br, 'Wh': Wh, 'bh': bh, 'Wp': Wp, 'bp': bp}
    _L0_cond_all = _L0_cond_setup()
    _L0_cond_in = {k: v for k, v in _L0_cond_all.items() if k in ('Wz', 'bz', 'Wr', 'br', 'Wh', 'bh', 'Wp', 'bp')}
    del _L0_cond_all

    def _L0_ffn_setup():
        import jax, jax.numpy as jnp
        import numpy as np
        D = 128
        E = 12
        HS = 2 * D
        HR = 3 * D
        TAU = 1.5

        def _geglu(h):
            a, g = jnp.split(h, 2, axis=-1)
            return a * jax.nn.gelu(g, approximate=False)
        key = jax.random.key(seed)
        ks = jax.random.split(key, 12)

        def xavier(k, shape):
            fan_in, fan_out = (shape[-2], shape[-1])
            lim = jnp.sqrt(6.0 / (fan_in + fan_out))
            return jax.random.uniform(k, shape, jnp.float32, -lim, lim)
        x = jax.random.normal(ks[0], (2, 128, D), jnp.float32)
        Ws1 = xavier(ks[1], (D, 2 * HS))
        bs1 = jnp.zeros((2 * HS,), jnp.float32)
        Ws2 = xavier(ks[2], (HS, D))
        bs2 = jnp.zeros((D,), jnp.float32)
        We1 = xavier(ks[3], (E, D, 2 * HR))
        be1 = jnp.zeros((E, 2 * HR), jnp.float32)
        We2 = xavier(ks[4], (E, HR, D))
        be2 = jnp.zeros((E, D), jnp.float32)
        Wr = xavier(ks[5], (D, E))
        br = jnp.zeros((E,), jnp.float32)
        return {'x': x, 'Ws1': Ws1, 'bs1': bs1, 'Ws2': Ws2, 'bs2': bs2, 'We1': We1, 'be1': be1, 'We2': We2, 'be2': be2, 'Wr': Wr, 'br': br}
    _L0_ffn_all = _L0_ffn_setup()
    _L0_ffn_in = {k: v for k, v in _L0_ffn_all.items() if k in ('Ws1', 'bs1', 'Ws2', 'bs2', 'We1', 'be1', 'We2', 'be2', 'Wr', 'br')}
    del _L0_ffn_all

    def _L1_cond_setup():
        import jax, jax.numpy as jnp
        import numpy as np
        import math
        N, T, D, H = (64, 64, 128, 128)
        key = jax.random.key(seed)
        k1, k2, k3, k4 = jax.random.split(key, 4)
        x = jax.random.normal(k1, (N, T, D), dtype=jnp.float32)
        h0 = jax.random.normal(k2, (N, H), dtype=jnp.float32)
        Wx = jax.random.normal(k3, (D, H), dtype=jnp.float32) / math.sqrt(D)
        Wh = jax.random.normal(k4, (H, H), dtype=jnp.float32) / math.sqrt(H)
        b = jnp.zeros((H,), dtype=jnp.float32)
        return {'x': x, 'h0': h0, 'Wx': Wx, 'Wh': Wh, 'b': b}
    _L1_cond_all = _L1_cond_setup()
    _L1_cond_in = {k: v for k, v in _L1_cond_all.items() if k in ('Wx', 'Wh', 'b')}
    del _L1_cond_all

    def _L1_ffn_setup():
        import jax, jax.numpy as jnp
        import numpy as np
        EPS = 1e-05

        def layernorm(x, w, b):
            mu = jnp.mean(x, axis=-1, keepdims=True)
            var = jnp.mean(jnp.square(x - mu), axis=-1, keepdims=True)
            return (x - mu) * jax.lax.rsqrt(var + EPS) * w + b

        def act_quant_fake(x):
            scale = 127.0 / jnp.clip(jnp.max(jnp.abs(x), axis=-1, keepdims=True), EPS, None)
            return jnp.clip(jnp.round(x * scale), -128.0, 127.0) / scale

        def weight_quant_fake(w):
            scale = 1.0 / jnp.clip(jnp.mean(jnp.abs(w)), EPS, None)
            return jnp.clip(jnp.round(w * scale), -1.0, 1.0) / scale

        def bitlinear(x, w, b):
            dqx = x + jax.lax.stop_gradient(act_quant_fake(x) - x)
            dqw = w + jax.lax.stop_gradient(weight_quant_fake(w) - w)
            return jnp.einsum('btd,hd->bth', dqx, dqw) + b
        key = jax.random.key(seed)
        ks = jax.random.split(key, 5)
        dim, hidden = (128, 512)
        B, T = (8, 256)
        return {'x': jax.random.normal(ks[0], (B, T, dim), dtype=jnp.float32), 'ln1_w': jnp.ones((dim,), jnp.float32), 'ln1_b': jnp.zeros((dim,), jnp.float32), 'w1': jax.random.normal(ks[1], (hidden, dim), jnp.float32) * (1.0 / np.sqrt(dim)), 'b1': jax.random.normal(ks[2], (hidden,), jnp.float32) * 0.01, 'ln2_w': jnp.ones((hidden,), jnp.float32), 'ln2_b': jnp.zeros((hidden,), jnp.float32), 'w2': jax.random.normal(ks[3], (dim, hidden), jnp.float32) * (1.0 / np.sqrt(hidden)), 'b2': jax.random.normal(ks[4], (dim,), jnp.float32) * 0.01}
    _L1_ffn_all = _L1_ffn_setup()
    _L1_ffn_in = {k: v for k, v in _L1_ffn_all.items() if k in ('ln1_w', 'ln1_b', 'w1', 'b1', 'ln2_w', 'ln2_b', 'w2', 'b2')}
    del _L1_ffn_all
    return {'x': x, 'cond_1024': cond_1024, 'L0_cond_Wz': _L0_cond_in['Wz'], 'L0_cond_bz': _L0_cond_in['bz'], 'L0_cond_Wr': _L0_cond_in['Wr'], 'L0_cond_br': _L0_cond_in['br'], 'L0_cond_Wh': _L0_cond_in['Wh'], 'L0_cond_bh': _L0_cond_in['bh'], 'L0_cond_Wp': _L0_cond_in['Wp'], 'L0_cond_bp': _L0_cond_in['bp'], 'L0_ffn_Ws1': _L0_ffn_in['Ws1'], 'L0_ffn_bs1': _L0_ffn_in['bs1'], 'L0_ffn_Ws2': _L0_ffn_in['Ws2'], 'L0_ffn_bs2': _L0_ffn_in['bs2'], 'L0_ffn_We1': _L0_ffn_in['We1'], 'L0_ffn_be1': _L0_ffn_in['be1'], 'L0_ffn_We2': _L0_ffn_in['We2'], 'L0_ffn_be2': _L0_ffn_in['be2'], 'L0_ffn_Wr': _L0_ffn_in['Wr'], 'L0_ffn_br': _L0_ffn_in['br'], 'L1_cond_Wx': _L1_cond_in['Wx'], 'L1_cond_Wh': _L1_cond_in['Wh'], 'L1_cond_b': _L1_cond_in['b'], 'L1_ffn_ln1_w': _L1_ffn_in['ln1_w'], 'L1_ffn_ln1_b': _L1_ffn_in['ln1_b'], 'L1_ffn_w1': _L1_ffn_in['w1'], 'L1_ffn_b1': _L1_ffn_in['b1'], 'L1_ffn_ln2_w': _L1_ffn_in['ln2_w'], 'L1_ffn_ln2_b': _L1_ffn_in['ln2_b'], 'L1_ffn_w2': _L1_ffn_in['w2'], 'L1_ffn_b2': _L1_ffn_in['b2']}

def reference(x, cond_1024, L0_cond_Wz, L0_cond_bz, L0_cond_Wr, L0_cond_br, L0_cond_Wh, L0_cond_bh, L0_cond_Wp, L0_cond_bp, L0_ffn_Ws1, L0_ffn_bs1, L0_ffn_Ws2, L0_ffn_bs2, L0_ffn_We1, L0_ffn_be1, L0_ffn_We2, L0_ffn_be2, L0_ffn_Wr, L0_ffn_br, L1_cond_Wx, L1_cond_Wh, L1_cond_b, L1_ffn_ln1_w, L1_ffn_ln1_b, L1_ffn_w1, L1_ffn_b1, L1_ffn_ln2_w, L1_ffn_ln2_b, L1_ffn_w2, L1_ffn_b2):
    import jax
    import jax.numpy as jnp

    def _L0_cond_ref(x, h0, Wz, bz, Wr, br, Wh, bh, Wp, bp):
        import jax, jax.numpy as jnp
        import numpy as np
        INPUT_DIM = 128
        HIDDEN_DIM = 128
        CHUNK_SIZE = 4

        def _linear_params(key, fan_in, fan_out):
            kw, kb = jax.random.split(key)
            bound = 1.0 / np.sqrt(fan_in)
            W = jax.random.uniform(kw, (fan_in, fan_out), jnp.float32, -bound, bound)
            b = jax.random.uniform(kb, (fan_out,), jnp.float32, -bound, bound)
            return (W, b)

        def _gru_forward(x, h0, Wz, bz, Wr, br, Wh, bh, Wp, bp):
            B, T, D = x.shape
            t = jnp.arange(T)
            do_prop = ((t + 1) % CHUNK_SIZE == 0) & (t < T - 1)
            xs = jnp.transpose(x, (1, 0, 2))

            def step(h, inp):
                x_t, prop = inp
                comb = jnp.concatenate([x_t, h], axis=-1)
                z = jax.nn.sigmoid(comb @ Wz + bz)
                r = jax.nn.sigmoid(comb @ Wr + br)
                comb2 = jnp.concatenate([x_t, r * h], axis=-1)
                h_cand = jnp.tanh(comb2 @ Wh + bh)
                h_new = (1.0 - z) * h + z * h_cand
                h_next = jnp.where(prop, jnp.tanh(h_new @ Wp + bp), h_new)
                return (h_next, h_new)
            _, ys = jax.lax.scan(step, h0, (xs, do_prop))
            return jnp.transpose(ys, (1, 0, 2))
        return _gru_forward(x, h0, Wz, bz, Wr, br, Wh, bh, Wp, bp)

    def _L0_ffn_ref(x, Ws1, bs1, Ws2, bs2, We1, be1, We2, be2, Wr, br):
        import jax, jax.numpy as jnp
        import numpy as np
        D = 128
        E = 12
        HS = 2 * D
        HR = 3 * D
        TAU = 1.5

        def _geglu(h):
            a, g = jnp.split(h, 2, axis=-1)
            return a * jax.nn.gelu(g, approximate=False)
        B, T, Dm = x.shape
        xf = x.reshape(-1, Dm)
        ys = _geglu(xf @ Ws1 + bs1) @ Ws2 + bs2
        logits = (xf @ Wr + br) / TAU
        top_val, top_idx = jax.lax.top_k(logits, 2)
        top_w = jax.nn.softmax(top_val, axis=-1)
        onehot = jax.nn.one_hot(top_idx, E, dtype=x.dtype)
        w = jnp.einsum('nke,nk->ne', onehot, top_w)
        h = jnp.einsum('nd,edh->enh', xf, We1) + be1[:, None, :]
        act = _geglu(h)
        yE = jnp.einsum('enh,ehd->end', act, We2) + be2[:, None, :]
        yr = jnp.einsum('end,ne->nd', yE, w)
        return (ys + yr).reshape(B, T, Dm)

    def _L1_cond_ref(x, h0, Wx, Wh, b):
        import jax, jax.numpy as jnp
        import numpy as np
        import math
        N, T, D, H = (64, 64, 128, 128)
        xW = jnp.einsum('ntd,dh->nth', x, Wx) + b

        def step(prev_h, xw_t):
            next_h = jnp.tanh(prev_h @ Wh + xw_t)
            return (next_h, next_h)
        _, hs = jax.lax.scan(step, h0, jnp.swapaxes(xW, 0, 1))
        return jnp.swapaxes(hs, 0, 1)

    def _L1_ffn_ref(x, ln1_w, ln1_b, w1, b1, ln2_w, ln2_b, w2, b2):
        import jax, jax.numpy as jnp
        import numpy as np
        EPS = 1e-05

        def layernorm(x, w, b):
            mu = jnp.mean(x, axis=-1, keepdims=True)
            var = jnp.mean(jnp.square(x - mu), axis=-1, keepdims=True)
            return (x - mu) * jax.lax.rsqrt(var + EPS) * w + b

        def act_quant_fake(x):
            scale = 127.0 / jnp.clip(jnp.max(jnp.abs(x), axis=-1, keepdims=True), EPS, None)
            return jnp.clip(jnp.round(x * scale), -128.0, 127.0) / scale

        def weight_quant_fake(w):
            scale = 1.0 / jnp.clip(jnp.mean(jnp.abs(w)), EPS, None)
            return jnp.clip(jnp.round(w * scale), -1.0, 1.0) / scale

        def bitlinear(x, w, b):
            dqx = x + jax.lax.stop_gradient(act_quant_fake(x) - x)
            dqw = w + jax.lax.stop_gradient(weight_quant_fake(w) - w)
            return jnp.einsum('btd,hd->bth', dqx, dqw) + b
        h = layernorm(x, ln1_w, ln1_b)
        h = bitlinear(h, w1, b1)
        h = jax.nn.gelu(h, approximate=False)
        h = layernorm(h, ln2_w, ln2_b)
        out = bitlinear(h, w2, b2)
        return out
    x = x + _L0_ffn_ref(_L0_cond_ref(x, cond_1024, L0_cond_Wz, L0_cond_bz, L0_cond_Wr, L0_cond_br, L0_cond_Wh, L0_cond_bh, L0_cond_Wp, L0_cond_bp), L0_ffn_Ws1, L0_ffn_bs1, L0_ffn_Ws2, L0_ffn_bs2, L0_ffn_We1, L0_ffn_be1, L0_ffn_We2, L0_ffn_be2, L0_ffn_Wr, L0_ffn_br)
    x = x + _L1_ffn_ref(_L1_cond_ref(x, cond_1024, L1_cond_Wx, L1_cond_Wh, L1_cond_b), L1_ffn_ln1_w, L1_ffn_ln1_b, L1_ffn_w1, L1_ffn_b1, L1_ffn_ln2_w, L1_ffn_ln2_b, L1_ffn_w2, L1_ffn_b2)
    return x

_drawn_inputs = setup_inputs


def setup_inputs(seed=0):
    import zlib

    import numpy as np

    out = dict(_drawn_inputs(seed))
    spreads = {'L0_ffn_bs1': (0.0, 0.491),
     'L0_ffn_bs2': (0.0, 0.1),
     'L0_ffn_be1': (0.0, 0.62),
     'L0_ffn_be2': (0.0, 0.1),
     'L0_ffn_br': (0.0, 0.1),
     'L1_cond_b': (0.0, 0.331),
     'L1_ffn_ln1_w': (1.0, 0.2),
     'L1_ffn_ln1_b': (0.0, 0.1),
     'L1_ffn_ln2_w': (1.0, 0.2),
     'L1_ffn_ln2_b': (0.0, 0.1)}
    factors = {'L0_cond_bz': 5.453,
     'L0_cond_Wr': 5.211,
     'L0_cond_br': 8.0,
     'L0_cond_bp': 2.767,
     'L0_ffn_Ws1': 2.921,
     'L0_ffn_Ws2': 2.821,
     'L0_ffn_We1': 4.434,
     'L0_ffn_We2': 4.135,
     'L1_ffn_b1': 4.78,
     'L1_ffn_b2': 6.817}
    for name, (base, spread) in spreads.items():
        noise = np.random.default_rng([zlib.crc32(name.encode()), seed]).standard_normal(out[name].shape)
        drawn = base * np.exp(spread * noise) if base else spread * noise
        out[name] = jnp.asarray(drawn.astype(out[name].dtype))
    for name, factor in factors.items():
        out[name] = (out[name] * factor).astype(out[name].dtype)
    return out
```

```python
from contextlib import ExitStack

import concourse.bass as bass
from concourse import mybir

F32 = mybir.dt.float32
BF16 = mybir.dt.bfloat16
I32 = mybir.dt.int32
U32 = mybir.dt.uint32
ALU = mybir.AluOpType
ACT = mybir.ActivationFunctionType
AX_X = mybir.AxisListType.X

P = 128
BATCH, STEPS, D = 32, 128, 128
TOKENS = BATCH * STEPS
QUAD = 4
QUADS = STEPS // QUAD
E = 12
HS, HR = 2 * D, 3 * D
TAU = 1.5
HID = 512
EPS = 1e-5
MAGIC = 12582912.0
N_SLOT_TILES = 2 * TOKENS // P + E
N_SLOT_TILES += N_SLOT_TILES % 2
N_SLOTS = N_SLOT_TILES * P
B1_AT, B2_AT = 0, E * 2 * HR
BS1_AT = B2_AT + E * D
BS2_AT = BS1_AT + 2 * HS
N_BIAS = BS2_AT + D
BIAS_ROWS = N_BIAS // P
ds = bass.ds


def valid(q, lo=0, hi=QUADS):
    return lo <= q < hi if isinstance(q, int) else True


def build(nc, x_t, x_tok, h0_t, gru_w, gru_b, gru_wp, gru_bp, we1, we2, ws1, ws2, wr, br, bias,
          rnn_wx, rnn_wh, rnn_b, w1_t, w2_t, ln1_w, ln1_b, b1, ln2_w, ln2_b, b2, out):
    with ExitStack() as ctx:
        def sb(name, shape, dt=F32):
            return ctx.enter_context(nc.sbuf_tensor(name, shape, dt))

        def sem(name):
            return ctx.enter_context(nc.semaphore(name))

        bank = [ctx.enter_context(nc.psum_tensor(f"bank{i}", [P, 512], F32)) for i in range(8)]

        slots_in = nc.dram_tensor("slots_in", (N_SLOTS, D), F32, kind="Internal").ap()
        slots_out = nc.dram_tensor("slots_out", (N_SLOTS, D), F32, kind="Internal").ap()

        ident = sb("ident", [P, P])
        ident_b = sb("ident_b", [P, P], BF16)
        ones_b = sb("ones_b", [P, P], BF16)
        ones_f = sb("ones_f", [P, P])
        before = sb("before", [P, P], BF16)
        iota_e = sb("iota_e", [P, E])
        iota_t = sb("iota_t", [1, N_SLOT_TILES])
        zeros = sb("zeros", [P, D])
        g_w = sb("g_w", [P, 2, 3, P])
        g_b = sb("g_b", [1, 3, P])
        wh_half = sb("wh_half", [P, 3, P])
        wh_nhalf = sb("wh_nhalf", [P, 2, P])
        wh_nquart = sb("wh_nquart", [P, 2, P])
        wc_quart = sb("wc_quart", [P, P])
        wp_sb = sb("wp_sb", [P, P])
        wp_half = sb("wp_half", [P, P])
        wp_nquart = sb("wp_nquart", [P, P])
        bp_sb = sb("bp_sb", [P, 1])
        we1_sb = sb("we1_sb", [P, E * 2 * HR])
        we2_sb = sb("we2_sb", [P, E * HR])
        ws1_sb = sb("ws1_sb", [P, 2 * HS])
        ws2_sb = sb("ws2_sb", [P, 2, D])
        wr_sb = sb("wr_sb", [P, E])
        br_sb = sb("br_sb", [1, E])
        bias_in = sb("bias_in", [BIAS_ROWS, P])
        bias_r = sb("bias_r", [BIAS_ROWS, 2, P])
        bias_p = sb("bias_p", [BIAS_ROWS, 3, P], BF16)
        bias3 = sb("bias3", [3, N_BIAS], BF16)
        wx_sb = sb("wx_sb", [P, P])
        rwh_sb = sb("rwh_sb", [P, P])
        rb_sb = sb("rb_sb", [P, 1])
        w1_raw = sb("w1_raw", [P, HID])
        w2_raw = sb("w2_raw", [P, HID])
        w1_q = sb("w1_q", [P, HID], BF16)
        w2_q = sb("w2_q", [P, HID], BF16)
        wq_tmp = sb("wq_tmp", [P, 2, HID])
        w_abs = sb("w_abs", [P, 2])
        w_mean = sb("w_mean", [P, 2])
        w_inv = sb("w_inv", [P, 2])
        w_step = sb("w_step", [P, 2])
        ln1w_sb = sb("ln1w_sb", [P, D])
        ln1b_sb = sb("ln1b_sb", [P, D])
        b1_sb = sb("b1_sb", [P, HID])
        ln2w_sb = sb("ln2w_sb", [P, HID])
        ln2b_sb = sb("ln2b_sb", [P, HID])
        b2_sb = sb("b2_sb", [P, D])

        xt_sb = sb("xt_sb", [P, TOKENS])
        res = sb("res", [P, QUADS, D])
        h_tok = sb("h_tok", [P, QUADS, D])

        h_prev = sb("h_prev", [P, BATCH])
        g_zr = sb("g_zr", [P, 2, BATCH])
        g_rh = sb("g_rh", [P, BATCH])
        g_na = sb("g_na", [P, BATCH])
        g_c = sb("g_c", [P, BATCH])
        g_e = sb("g_e", [P, BATCH])
        h2 = [sb(f"h2_{p}", [P, QUAD, BATCH]) for p in range(2)]

        lg = [sb(f"lg{p}", [P, E]) for p in range(2)]
        top = [sb(f"top{p}", [P, 8]) for p in range(2)]
        tix = [sb(f"tix{p}", [P, 8], U32) for p in range(2)]
        top_v = sb("top_v", [P, QUADS, 2])
        top_i = sb("top_i", [P, QUADS, 2])
        s_gl = sb("s_gl", [P, HS])
        s_act = sb("s_act", [P, HS])
        s_at = sb("s_at", [P, HS])

        hot = sb("hot", [P, 2, QUADS, E], BF16)
        hot_any = sb("hot_any", [P, QUADS, E], BF16)
        cnt = sb("cnt", [P, 4, E])
        ones_e = sb("ones_e", [P, E])
        ends = sb("ends", [P, E])
        base = sb("base", [P, E])
        where_e = sb("where_e", [P, QUADS, E])
        picked = sb("picked", [P, 2, QUADS, E])
        slot_f = sb("slot_f", [P, 2, QUADS])
        slot = sb("slot", [P, 2, QUADS], U32)
        past = sb("past", [1, N_SLOT_TILES, E])
        eid_f = sb("eid_f", [1, N_SLOT_TILES])
        eid_m = sb("eid_m", [1, N_SLOT_TILES])
        eid = sb("eid", [1, N_SLOT_TILES], I32)
        dv = sb("dv", [P, QUADS])
        th = sb("th", [P, QUADS])
        pick_w = sb("pick_w", [P, 2, QUADS])

        xg = [sb(f"xg{p}", [P, D]) for p in range(2)]
        xg_t = [sb(f"xg_t{p}", [P, P]) for p in range(2)]
        e_gl = [sb(f"e_gl{p}", [P, HR]) for p in range(2)]
        e_act = [sb(f"e_act{p}", [P, HR]) for p in range(2)]
        e_at = [sb(f"e_at{p}", [P, HR]) for p in range(2)]
        e_y = [sb(f"e_y{p}", [P, D]) for p in range(2)]

        late = [xt_sb[:, i * HID:(i + 1) * HID] for i in range(8)]
        hid, gel, n2, ln2 = late[0:2], late[2:4], late[4], late[5]
        qm2 = xt_sb[:, 6 * HID:8 * HID].rearrange("q (a n) -> q a n", a=2)

        y_got = [[sb(f"y{k}_{p}", [P, D]) for p in range(2)] for k in range(2)]
        y_sum = sb("y_sum", [P, D])
        x1 = [sb(f"x1_{p}", [P, D]) for p in range(2)]
        x1_t = [sb(f"x1_t{p}", [P, P]) for p in range(2)]
        r_t = [sb(f"r_t{p}", [P, QUAD, BATCH]) for p in range(2)]
        r_start = sb("r_start", [P, BATCH])
        touched = sb("touched", [P, 2])
        st1 = sb("st1", [P, 6])
        mv = sb("mv", [P, 2, 2])
        var_e = sb("var_e", [P, 2])
        half_bits = sb("half_bits", [P, 2], I32)
        rsq = [sb(f"rsq{i}", [P, 2]) for i in range(4)]
        rsq_t = sb("rsq_t", [P, 2, 2])
        n1 = sb("n1", [P, D])
        ln1 = sb("ln1", [P, D])
        am1 = sb("am1", [P, 2])
        sc1 = sb("sc1", [P, 2])
        dq1 = [sb(f"dq1_{p}", [P, 1]) for p in range(2)]
        qm1 = sb("qm1", [P, 2, D])
        q1 = [sb(f"q1_{p}", [P, D], BF16) for p in range(2)]
        q1_t = sb("q1_t", [P, P], BF16)
        st2 = sb("st2", [P, 6])
        am2 = sb("am2", [P, 2])
        sc2 = sb("sc2", [P, 2])
        dq2 = [sb(f"dq2_{p}", [P, 1]) for p in range(2)]
        q2 = [sb(f"q2_{p}", [P, HID], BF16) for p in range(2)]
        q2_t = sb("q2_t", [P, HID], BF16)
        fo = sb("fo", [P, D])
        o_sb = [sb(f"o_sb{p}", [P, D]) for p in range(2)]

        gru_in = sem("gru_in")
        gru_x = sem("gru_x")
        ffn_in = sem("ffn_in")
        exp_in = sem("exp_in")
        l1_in = sem("l1_in")
        bias_loaded = sem("bias_loaded")
        bias_moved = sem("bias_moved")
        consts = sem("consts")
        consts_c = sem("consts_c")
        zeroed = sem("zeroed")
        w_scaled = sem("w_scaled")
        bias_chain = sem("bias_chain")
        bias_split = sem("bias_split")
        h0_in = sem("h0_in")
        zr_done = sem("zr_done")
        zr_tanh = sem("zr_tanh")
        rh_ready = sem("rh_ready")
        na_ready = sem("na_ready")
        c_done = sem("c_done")
        c_tanh = sem("c_tanh")
        e_ready = sem("e_ready")
        h_ready = sem("h_ready")
        prop_done = sem("prop_done")
        prop_tanh = sem("prop_tanh")
        hT_done = sem("hT_done")
        h_tok_ready = sem("h_tok_ready")
        lg_done = sem("lg_done")
        lg_read = sem("lg_read")
        rt = sem("rt")
        sh_done = sem("sh_done")
        s_gelu = sem("s_gelu")
        s_act_ready = sem("s_act_ready")
        sT_done = sem("sT_done")
        s_at_ready = sem("s_at_ready")
        sy_done = sem("sy_done")
        res_ready = sem("res_ready")
        sl = sem("sl")
        th_ready = sem("th_ready")
        rank_done = sem("rank_done")
        eid_ready = sem("eid_ready")
        slot_ready = sem("slot_ready")
        pw_ready = sem("pw_ready")
        scattered = sem("scattered")
        xg_in = [sem(f"xg_in{p}") for p in range(2)]
        xgT_done = sem("xgT_done")
        xg_t_ready = sem("xg_t_ready")
        up_done = sem("up_done")
        e_gelu = sem("e_gelu")
        e_act_ready = sem("e_act_ready")
        eT_done = sem("eT_done")
        e_at_ready = sem("e_at_ready")
        ey_done = sem("ey_done")
        e_y_ready = sem("e_y_ready")
        e_y_out = [sem(f"e_y_out{p}") for p in range(2)]
        gathered = [sem(f"gathered{p}") for p in range(2)]
        ysum_ready = sem("ysum_ready")
        x1_ready = sem("x1_ready")
        x1_kept = sem("x1_kept")
        x1T_done = sem("x1T_done")
        x1_t_ready = sem("x1_t_ready")
        r_done = sem("r_done")
        r_tanh = sem("r_tanh")
        rT_done = sem("rT_done")
        f1 = sem("f1")
        rq = sem("rq")
        mv_init = sem("mv_init")
        f1_norm = sem("f1_norm")
        q1_ready = sem("q1_ready")
        q1T_done = sem("q1T_done")
        q1_t_ready = sem("q1_t_ready")
        m1_done = sem("m1_done")
        hid_ready = sem("hid_ready")
        gel_ready = sem("gel_ready")
        f2 = sem("f2")
        q2m_ready = sem("q2m_ready")
        q2_ready = sem("q2_ready")
        q2T_done = sem("q2T_done")
        q2_t_ready = sem("q2_t_ready")
        m2_done = sem("m2_done")
        fo_ready = sem("fo_ready")
        o_ready = sem("o_ready")
        o_out = [sem(f"o_out{p}") for p in range(2)]
        wq = sem("wq")
        wsum_ready = sem("wsum_ready")
        wsum_done = sem("wsum_done")
        wq_ready = sem("wq_ready")

        ROUTER_STEPS = 3
        LN1_STEPS = 9
        LN2_STEPS = 9
        RSQRT_STEPS = 12

        zr_ps, c_ps = bank[0:2], bank[2:4]
        t_ps, a_ps, y_ps, l_ps = bank[4], bank[5], bank[6], bank[7]
        ea_ps, eg_ps = bank[0:2], bank[2:4]
        ex_ps, et_ps, ey_ps = bank[4], bank[5], bank[6]
        rank_ps = bank[7]
        rx_ps = bank[0:2]
        x1t_ps, rt_ps, q1t_ps, m1_ps, q2t_ps, m2_ps = bank[2], bank[3], bank[4], bank[5], bank[6], bank[7]

        def zr(p, s):
            return zr_ps[p][:, s * 64:s * 64 + 64]

        def gate(p, g):
            return zr_ps[p][:, 0:256].rearrange("q (s g b) -> q s g b", s=QUAD, g=2)[:, :, g, :]

        prop_cols = slice(256, 256 + BATCH)

        block = ctx.enter_context(nc.Block())

        @block.sync
        def _(sp):
            first = 4 * P
            sp.dma_start(g_w[:, :, :, :], gru_w.rearrange("k (i g n) -> k i g n", i=2, g=3)).then_inc(gru_in, 16)
            sp.dma_start(xt_sb[:, 0:first], x_t[:, 0:first]).then_inc(gru_in, 16)
            sp.dma_start(g_b[:, :, :], gru_b.rearrange("k (g n) -> k g n", g=3)).then_inc(gru_in, 16)
            sp.dma_start(wp_sb[:, :], gru_wp).then_inc(gru_in, 16)
            sp.dma_start(bp_sb[:, :], gru_bp).then_inc(gru_in, 16)
            sp.dma_start(h_prev[:, :], h0_t).then_inc(h0_in, 16)
            sp.dma_start(r_start[:, :], h0_t).then_inc(h0_in, 16)
            sp.dma_start(ws1_sb[:, :], ws1).then_inc(ffn_in, 16)
            sp.dma_start(ws2_sb[:, :, :], ws2.rearrange("k (c n) -> k c n", c=2)).then_inc(ffn_in, 16)
            sp.dma_start(wr_sb[:, :], wr).then_inc(ffn_in, 16)
            sp.dma_start(br_sb[:, :], br).then_inc(ffn_in, 16)
            sp.dma_start(bias_in[:, :], bias).then_inc(bias_loaded, 16)
            sp.dma_start(xt_sb[:, first:TOKENS], x_t[:, first:TOKENS]).then_inc(gru_x, 16)
            sp.dma_start(res[:, :, :], x_tok.rearrange("q (i n) -> q i n", i=QUADS)).then_inc(ffn_in, 16)
            sp.wait_ge(bias_split, 3)
            for part in range(3):
                sp.dma_start(bias3[part:part + 1, :].rearrange("a (r n) -> a r n", n=P),
                             bias_p[:, part, :]).then_inc(bias_moved, 16)
            sp.dma_start(we1_sb[:, :], we1).then_inc(exp_in, 16)
            sp.dma_start(we2_sb[:, :], we2).then_inc(exp_in, 16)
            for dst, src in ((wx_sb, rnn_wx), (rwh_sb, rnn_wh), (rb_sb, rnn_b), (w1_raw, w1_t), (w2_raw, w2_t)):
                sp.dma_start(dst[:, :], src).then_inc(l1_in, 16)
            for dst, src in ((ln1w_sb, ln1_w), (ln1b_sb, ln1_b), (b1_sb, b1), (ln2w_sb, ln2_w),
                             (ln2b_sb, ln2_b), (b2_sb, b2)):
                sp.dma_start(dst[:, :], src.to_broadcast([P, src.shape[1]])).then_inc(l1_in, 16)
            sp.wait_ge(consts, 7)
            for i in range(4):
                n = N_SLOTS // 4
                sp.dma_start(slots_in[i * n:(i + 1) * n, :].rearrange("(i p) d -> p i d", p=P),
                             zeros[:, :].unsqueeze(1).to_broadcast([P, n // P, D])).then_inc(zeroed, 16)

            sp.wait_ge(scattered, 16 * 2 * QUADS)
            for p in range(2):
                sp.dma_start(xg[p][:, :], slots_in[ds(p * P, P), :]).then_inc(xg_in[p], 16)

            def expert_io(k, p):
                i = 2 * k + p
                if valid(i + 2, 0, N_SLOT_TILES):
                    sp.wait_ge(xgT_done, i + 1)
                    sp.dma_start(xg[p][:, :], slots_in[ds((i + 2) * P, P), :]).then_inc(xg_in[p], 16)
                if valid(i - 2, 0, N_SLOT_TILES):
                    sp.wait_ge(e_y_ready, i - 1)
                    sp.dma_start(slots_out[ds((i - 2) * P, P), :], e_y[p][:, :]).then_inc(e_y_out[p], 16)

            expert_io(0, 0)
            expert_io(0, 1)
            with sp.Fori(1, N_SLOT_TILES // 2 - 1) as k:
                expert_io(k, 0)
                expert_io(k, 1)
            for i in range(N_SLOT_TILES - 2, N_SLOT_TILES + 2):
                expert_io(i // 2, i % 2)

            def store(k, p):
                i = 2 * k + p
                sp.wait_ge(o_ready, i + 1)
                sp.dma_start(out[ds(i * P, P), :], o_sb[p][:, :]).then_inc(o_out[p], 16)

            with sp.Fori(0, QUADS // 2) as k:
                store(k, 0)
                store(k, 1)
            for p in range(2):
                sp.wait_ge(o_out[p], 16 * (QUADS // 2))

        @block.gpsimd
        def _(pool):
            pool.memset(ident[:, :], 0.0).then_inc(consts_c, 1)
            pool.memset(ident_b[:, :], 0.0).then_inc(consts_c, 1)
            pool.memset(before[:, :], 0.0).then_inc(consts_c, 1)
            pool.memset(ones_f[:, :], 1.0).then_inc(consts, 1)
            pool.memset(ones_b[:, :], 1.0).then_inc(consts, 1)
            pool.memset(zeros[:, :], 0.0).then_inc(consts, 1)
            pool.memset(ones_e[:, :], 1.0).then_inc(consts, 1)
            pool.wait_ge(consts_c, 3)
            for m in (ident, ident_b):
                pool.affine_select(out=m[:, :], in_=m[:, :], compare_op=ALU.not_equal, fill=1.0, base=0,
                                   pattern=[[-1, P]], channel_multiplier=1).then_inc(consts, 1)
            pool.affine_select(out=before[:, :], in_=before[:, :], compare_op=ALU.is_ge, fill=1.0, base=0,
                               pattern=[[-1, P]], channel_multiplier=1).then_inc(consts, 1)
            pool.wait_ge(gru_in, 16 * 5)
            pool.tensor_scalar(wc_quart[:, :], g_w[:, 1, 2, :], 0.25, None, ALU.mult).then_inc(w_scaled, 1)
            pool.tensor_scalar(wh_half[:, :, :], g_w[:, 1, :, :], 0.5, None, ALU.mult).then_inc(w_scaled, 1)
            pool.tensor_scalar(wh_nhalf[:, :, :], g_w[:, 1, 0:2, :], -0.5, None, ALU.mult).then_inc(w_scaled, 1)
            pool.tensor_scalar(wh_nquart[:, :, :], g_w[:, 1, 0:2, :], -0.25, None, ALU.mult).then_inc(w_scaled, 1)
            pool.tensor_scalar(wp_half[:, :], wp_sb[:, :], 0.5, None, ALU.mult).then_inc(w_scaled, 1)
            pool.tensor_scalar(wp_nquart[:, :], wp_sb[:, :], -0.25, None, ALU.mult).then_inc(w_scaled, 1)
            pool.iota(iota_e[:, :], [[1, E]], base=0, channel_multiplier=0,
                      allow_small_or_imprecise_dtypes=True).then_inc(consts, 1)
            pool.iota(iota_t[:, :], [[1, N_SLOT_TILES]], base=0, channel_multiplier=0,
                      allow_small_or_imprecise_dtypes=True).then_inc(consts, 1)
            pool.wait_ge(ffn_in, 16 * 5)
            pool.tensor_scalar(ws1_sb[:, :], ws1_sb[:, :], 0.5, None, ALU.mult).then_inc(w_scaled, 1)
            pool.tensor_scalar(wr_sb[:, :], wr_sb[:, :], 0.5, None, ALU.mult).then_inc(w_scaled, 1)

            pool.wait_ge(zeroed, 64)
            pool.wait_ge(slot_ready, 1)
            pool.wait_ge(h_tok_ready, QUADS)
            for j in range(QUADS):
                for k in range(2):
                    pool.indirect_dma_start(
                        out=slots_in, out_offset=bass.IndirectOffsetOnAxis(ap=slot[:, k, j:j + 1], axis=0),
                        in_=h_tok[:, j, :], in_offset=None).then_inc(scattered, 16)
            for p in range(2):
                pool.wait_ge(e_y_out[p], 16 * (N_SLOT_TILES // 2))
            for j in range(QUADS):
                p = j % 2
                if j >= 2:
                    pool.wait_ge(x1_ready, j - 1)
                for k in range(2):
                    pool.indirect_dma_start(
                        out=y_got[k][p][:, :], out_offset=None, in_=slots_out,
                        in_offset=bass.IndirectOffsetOnAxis(ap=slot[:, k, j:j + 1], axis=0)).then_inc(gathered[p], 16)
                if j >= 1:
                    pool.wait_ge(x1_ready, j)
                    pool.tensor_copy(res[:, j - 1, :], x1[1 - p][:, :]).then_inc(x1_kept, 1)
            pool.wait_ge(x1_ready, QUADS)
            pool.tensor_copy(res[:, QUADS - 1, :], x1[1][:, :]).then_inc(x1_kept, 1)

        @block.tensor
        def _(pe):
            pe.wait_ge(consts, 9)
            pe.wait_ge(gru_in, 16 * 5)
            pe.wait_ge(w_scaled, 8)

            def x_part(q, p, g):
                dst = gate(p, g) if g < 2 else c_ps[p][:, 0:P].rearrange("q (s b) -> q s b", s=QUAD)
                pe.matmul(dst, g_w[:, 0, g, :], xt_sb[:, ds(q * P, P)].rearrange("q (s b) -> q s b", s=QUAD),
                          start=(g != 1), stop=False, skip_group_check=True)
                pe.matmul(dst, g_b[:, g, :], ones_f[0:1, :].rearrange("q (s b) -> q s b", s=QUAD),
                          start=False, stop=False, skip_group_check=True)

            def add(dst, w, v):
                return pe.matmul(dst, w, v, start=False, stop=False, skip_group_check=True)

            def shared_up(p, half):
                pe.matmul(a_ps[:, half * HS:(half + 1) * HS], h2[p][:, :, :], ws1_sb[:, half * HS:(half + 1) * HS],
                          start=(half == 0), stop=False, skip_group_check=True)

            def gru_quad(k, p, last=False):
                q = 2 * k + p
                side = valid(q - 1)
                o = 1 - p
                for s in range(QUAD):
                    z_at, r_at = zr(p, s)[:, 0:BATCH], zr(p, s)[:, BATCH:2 * BATCH]
                    if s == 0:
                        pe.wait_ge(prop_tanh, q)
                        add(r_at, g_w[:, 1, 1, :], h_prev[:, :])
                        add(z_at, g_w[:, 1, 0, :], h_prev[:, :]).then_inc(zr_done, 1)
                    else:
                        wn = wh_nhalf if s == 1 else wh_nquart
                        pe.wait_ge(na_ready, 4 * q + s)
                        add(r_at, wn[:, 1, :], g_na[:, :])
                        add(z_at, wn[:, 0, :], g_na[:, :])
                        pe.wait_ge(e_ready, 4 * q + s)
                        add(r_at, wh_half[:, 1, :], g_e[:, :])
                        add(z_at, wh_half[:, 0, :], g_e[:, :]).then_inc(zr_done, 1)
                    if s == 0 and side:
                        pe.wait_ge(h_ready, 4 * q)
                        pe.transpose(t_ps[:, 0:P], h2[o][:, :, :], ident[:, :]).then_inc(hT_done, 1)
                    if s == 1 and side:
                        shared_up(o, 0)
                    if s == 2 and valid(q + 1):
                        x_part(q + 1, o, 0)
                    if s == 3 and valid(q + 1):
                        x_part(q + 1, o, 2)
                    pe.wait_ge(rh_ready, 4 * q + s + 1)
                    add(c_ps[p][:, s * BATCH:(s + 1) * BATCH], wh_half[:, 2, :] if s == 0 else wc_quart[:, :],
                        g_rh[:, :]).then_inc(c_done, 1)
                    if s == 0 and side:
                        pe.matmul(l_ps[:, 0:E], h2[o][:, :, :], wr_sb[:, :], start=True, stop=False)
                        pe.matmul(l_ps[:, 0:E], ones_f[0:1, :], br_sb[:, :], start=False,
                                  stop=True).then_inc(lg_done, 1)
                    if s == 1 and side:
                        shared_up(o, 1)
                        add(a_ps[:, 0:2 * HS], ones_b[0:3, :], bias3[:, BS1_AT:BS1_AT + 2 * HS]).then_inc(sh_done, 1)
                    if s == 2 and valid(q + 1):
                        x_part(q + 1, o, 1)
                    if s == 3 and side:
                        shared_turn(q - 1)
                if not last:
                    pe.wait_ge(na_ready, 4 * q + 4)
                    add(zr_ps[p][:, prop_cols], wp_nquart[:, :], g_na[:, :])
                    pe.wait_ge(e_ready, 4 * q + 4)
                    add(zr_ps[p][:, prop_cols], wp_half[:, :], g_e[:, :]).then_inc(prop_done, 1)
                if side:
                    shared_down(q - 1)

            def shared_turn(j):
                pe.wait_ge(s_act_ready, j + 1)
                pe.wait_ge(h_tok_ready, j + 1)
                pe.transpose(t_ps[:, 0:P], s_act[:, 0:P], ident[:, :])
                pe.transpose(t_ps[:, P:2 * P], s_act[:, P:2 * P], ident[:, :]).then_inc(sT_done, 1)

            def shared_down(j):
                pe.wait_ge(s_at_ready, j + 1)
                if valid(j, 1):
                    pe.wait_ge(res_ready, j)
                pe.matmul(y_ps[:, 0:D], s_at[:, 0:P], ws2_sb[:, 0, :], start=True, stop=False)
                pe.matmul(y_ps[:, 0:D], s_at[:, P:2 * P], ws2_sb[:, 1, :], start=False, stop=False)
                pe.matmul(y_ps[:, 0:D], ones_b[0:3, :], bias3[:, BS2_AT:BS2_AT + D], start=False,
                          stop=True).then_inc(sy_done, 1)

            for g in range(3):
                x_part(0, 0, g)
            pe.wait_ge(h0_in, 32)
            pe.wait_ge(gru_x, 16)
            gru_quad(0, 0)
            pe.wait_ge(bias_moved, 48)
            gru_quad(0, 1)
            with pe.Fori(1, QUADS // 2 - 1) as k:
                gru_quad(k, 0)
                gru_quad(k, 1)
            gru_quad(QUADS // 2 - 1, 0)
            gru_quad(QUADS // 2 - 1, 1, last=True)
            o = 1
            pe.wait_ge(h_ready, 4 * QUADS)
            pe.transpose(t_ps[:, 0:P], h2[o][:, :, :], ident[:, :]).then_inc(hT_done, 1)
            pe.wait_ge(lg_read, QUADS - 1)
            pe.matmul(l_ps[:, 0:E], h2[o][:, :, :], wr_sb[:, :], start=True, stop=False)
            pe.matmul(l_ps[:, 0:E], ones_f[0:1, :], br_sb[:, :], start=False, stop=True).then_inc(lg_done, 1)
            pe.wait_ge(s_act_ready, QUADS - 1)
            shared_up(o, 0)
            shared_up(o, 1)
            add(a_ps[:, 0:2 * HS], ones_b[0:3, :], bias3[:, BS1_AT:BS1_AT + 2 * HS]).then_inc(sh_done, 1)
            shared_turn(QUADS - 1)
            shared_down(QUADS - 1)

            pe.wait_ge(sl, 3)
            pe.matmul(rank_ps[:, 0:QUADS * E], before[:, :], hot_any[:, :, :], start=True, stop=False,
                      skip_group_check=True)
            for j in range(QUADS):
                n = QUADS - j
                mm = pe.matmul(rank_ps[:, (j + 1) * E:(QUADS + 1) * E].rearrange("q (n e) -> q n e", e=E), ones_b[:, :],
                               hot_any[:, j:j + 1, :].to_broadcast([P, n, E]), start=False, stop=(j == QUADS - 1),
                               skip_group_check=True)
            mm.then_inc(rank_done, 1)
            pe.wait_ge(wsum_ready, 2)
            pe.matmul(y_ps[:, 256:258], ones_f[:, :], w_abs[:, :], start=True, stop=True).then_inc(wsum_done, 1)

            pe.wait_ge(exp_in, 32)
            pe.wait_ge(eid_ready, 1)

            def turn_in(k, p):
                i = 2 * k + p
                pe.wait_ge(xg_in[p], 16 * (k + 1))
                if valid(i, 1):
                    pe.wait_ge(xg_t_ready, i)
                pe.transpose(ex_ps[:, 0:P], xg[p][:, :], ident[:, :]).then_inc(xgT_done, 1)

            def expert(k, p):
                i = 2 * k + p
                if valid(i + 1, 0, N_SLOT_TILES):
                    turn_in(k + p, 1 - p)
                if valid(i - 2, 0, N_SLOT_TILES):
                    pe.wait_ge(e_act_ready, i - 1)
                    if valid(i - 3, 0, N_SLOT_TILES):
                        pe.wait_ge(e_at_ready, i - 2)
                    for c in range(3):
                        mm = pe.transpose(et_ps[:, c * P:(c + 1) * P], e_act[p][:, c * P:(c + 1) * P], ident[:, :])
                    mm.then_inc(eT_done, 1)
                if valid(i, 0, N_SLOT_TILES):
                    e = pe.value_load(eid[0:1, ds(i, 1)], min_val=0, max_val=E - 1)
                    pe.wait_ge(xg_t_ready, i + 1)
                    for half, ps in enumerate((eg_ps, ea_ps)):
                        at = (1 - half) * HR
                        pe.matmul(ps[p][:, 0:HR], xg_t[p][:, :], we1_sb[:, ds(e * (2 * HR) + at, HR)],
                                  start=True, stop=False)
                        mm = pe.matmul(ps[p][:, 0:HR], ones_b[0:3, :], bias3[:, ds(e * (2 * HR) + (B1_AT + at), HR)],
                                       start=False, stop=True)
                        mm.then_inc(up_done, 1)
                if valid(i - 2, 0, N_SLOT_TILES):
                    e = pe.value_load(eid[0:1, ds(i - 2, 1)], min_val=0, max_val=E - 1)
                    pe.wait_ge(e_at_ready, i - 1)
                    if valid(i - 3, 0, N_SLOT_TILES):
                        pe.wait_ge(e_y_ready, i - 2)
                    for c in range(3):
                        pe.matmul(ey_ps[:, 0:D], e_at[p][:, c * P:(c + 1) * P],
                                  we2_sb[:, ds(e * HR + c * D, D)], start=(c == 0), stop=False)
                    pe.matmul(ey_ps[:, 0:D], ones_b[0:3, :], bias3[:, ds(e * D + B2_AT, D)], start=False,
                              stop=True).then_inc(ey_done, 1)

            turn_in(0, 0)
            expert(0, 0)
            expert(0, 1)
            expert(1, 0)
            expert(1, 1)
            with pe.Fori(2, N_SLOT_TILES // 2 - 1) as k:
                expert(k, 0)
                expert(k, 1)
            for i in range(N_SLOT_TILES - 2, N_SLOT_TILES + 2):
                expert(i // 2, i % 2)

            pe.wait_ge(l1_in, 16 * 11)
            pe.wait_ge(h0_in, 32)
            pe.wait_ge(wq_ready, 2)

            def turn_x1(j, p):
                pe.wait_ge(x1_ready, j + 1)
                if valid(j, 1):
                    pe.wait_ge(x1_t_ready, j)
                pe.transpose(x1t_ps[:, 0:P], x1[p][:, :], ident[:, :]).then_inc(x1T_done, 1)

            def rnn_x(j, p):
                pe.wait_ge(x1_t_ready, j + 1)
                pe.matmul(rx_ps[p][:, 0:P], wx_sb[:, :], x1_t[p][:, :], start=True, stop=False, skip_group_check=True)

            def layer1(k, p):
                q = 2 * k + p
                o = 1 - p
                for s in range(QUAD):
                    if valid(q):
                        if s == 0:
                            prev = r_start[:, :] if isinstance(q, int) and q == 0 else r_t[o][:, QUAD - 1, :]
                        else:
                            prev = r_t[p][:, s - 1, :]
                        if valid(q, 1) or s > 0:
                            pe.wait_ge(r_tanh, 4 * q + s)
                        pe.matmul(rx_ps[p][:, s * BATCH:(s + 1) * BATCH], rwh_sb[:, :], prev, start=False, stop=False,
                                  skip_group_check=True).then_inc(r_done, 1)
                    if s == 0:
                        if valid(q + 2):
                            turn_x1(q + 2, p)
                        if valid(q - 1):
                            pe.wait_ge(r_tanh, 4 * q)
                            if valid(q - 1, 1):
                                pe.wait_ge(f1_norm, q - 1)
                            pe.transpose(rt_ps[:, 0:P], r_t[o][:, :, :], ident[:, :]).then_inc(rT_done, 1)
                    if s == 1:
                        if valid(q + 1):
                            rnn_x(q + 1, o)
                        if valid(q - 2):
                            pe.wait_ge(q1_ready, q - 1)
                            pe.transpose(q1t_ps[:, 0:P // 2].bitcast(BF16), q1[p][:, :], ident_b[:, :]).then_inc(q1T_done, 1)
                    if s == 2 and valid(q - 4):
                        pe.wait_ge(q2_ready, q - 3)
                        for c in range(4):
                            mm = pe.transpose(q2t_ps[:, c * P // 2:(c + 1) * P // 2].bitcast(BF16),
                                              q2[p][:, c * P:(c + 1) * P], ident_b[:, :])
                        mm.then_inc(q2T_done, 1)
                    if s == 3 and valid(q - 2):
                        pe.wait_ge(q1_t_ready, q - 1)
                        if valid(q - 3):
                            pe.wait_ge(hid_ready, q - 2)
                        pe.matmul(m1_ps[:, 0:HID], q1_t[:, :], w1_q[:, :], start=True, stop=True).then_inc(m1_done, 1)
                if valid(q - 4):
                    pe.wait_ge(q2_t_ready, q - 3)
                    if valid(q - 5):
                        pe.wait_ge(fo_ready, q - 4)
                    for c in range(4):
                        mm = pe.matmul(m2_ps[:, 0:D], q2_t[:, c * P:(c + 1) * P], w2_q[:, c * P:(c + 1) * P],
                                       start=(c == 0), stop=(c == 3))
                    mm.then_inc(m2_done, 1)

            turn_x1(0, 0)
            rnn_x(0, 0)
            turn_x1(1, 1)
            for q in range(6):
                layer1(q // 2, q % 2)
            with pe.Fori(3, QUADS // 2 - 1) as k:
                layer1(k, 0)
                layer1(k, 1)
            for q in range(QUADS - 2, QUADS + 4):
                layer1(q // 2, q % 2)

        @block.scalar
        def _(act):
            act.wait_ge(gru_in, 16 * 5)

            def gru_quad(k, p, last=False):
                q = 2 * k + p
                side = valid(q - 1)
                for s in range(QUAD):
                    act.wait_ge(zr_done, 4 * q + s + 1)
                    act.activation(g_zr[:, :, :], zr(p, s).rearrange("q (g b) -> q g b", g=2), ACT.Tanh,
                                   scale=0.5).then_inc(zr_tanh, 1)
                    act.wait_ge(c_done, 4 * q + s + 1)
                    act.activation(g_c[:, :], c_ps[p][:, s * BATCH:(s + 1) * BATCH], ACT.Tanh).then_inc(c_tanh, 1)
                    if s == 0 and side:
                        keep_h(q - 1)
                    if s == 1 and side:
                        shared_gelu(q - 1)
                    if s == 3 and side:
                        shared_copy(q - 1)
                if not last:
                    act.wait_ge(prop_done, q + 1)
                    act.activation(h_prev[:, :], zr_ps[p][:, prop_cols], ACT.Tanh,
                                   bias=bp_sb[:, :]).then_inc(prop_tanh, 1)

            def keep_h(j):
                act.wait_ge(hT_done, j + 1)
                act.activation(h_tok[:, ds(j, 1), :].rearrange("q a n -> q (a n)"), t_ps[:, 0:P], ACT.Copy,
                               scale=0.5).then_inc(h_tok_ready, 1)

            def shared_gelu(j):
                act.wait_ge(sh_done, j + 1)
                act.activation(s_gl[:, :], a_ps[:, HS:2 * HS], ACT.Gelu).then_inc(s_gelu, 1)

            def shared_copy(j):
                act.wait_ge(sT_done, j + 1)
                act.activation(s_at[:, :], t_ps[:, 0:HS], ACT.Copy).then_inc(s_at_ready, 1)

            gru_quad(0, 0)
            gru_quad(0, 1)
            with act.Fori(1, QUADS // 2 - 1) as k:
                gru_quad(k, 0)
                gru_quad(k, 1)
            gru_quad(QUADS // 2 - 1, 0)
            gru_quad(QUADS // 2 - 1, 1, last=True)
            keep_h(QUADS - 1)
            shared_gelu(QUADS - 1)
            shared_copy(QUADS - 1)
            act.wait_ge(sl, 4)
            act.activation(th[:, :], dv[:, :], ACT.Tanh, scale=0.5).then_inc(th_ready, 1)

            def copy_in(i, p):
                act.wait_ge(xgT_done, i + 1)
                act.activation(xg_t[p][:, :], ex_ps[:, 0:P], ACT.Copy).then_inc(xg_t_ready, 1)

            def expert(k, p):
                i = 2 * k + p
                if valid(i + 1, 0, N_SLOT_TILES):
                    if valid(i - 1, 0, N_SLOT_TILES):
                        act.wait_ge(up_done, 2 * i)
                    copy_in(i + 1, 1 - p)
                if valid(i - 2, 0, N_SLOT_TILES):
                    act.wait_ge(eT_done, i - 1)
                    if valid(i - 4, 0, N_SLOT_TILES):
                        act.wait_ge(ey_done, i - 3)
                    act.activation(e_at[p][:, :], et_ps[:, 0:HR], ACT.Copy).then_inc(e_at_ready, 1)
                if valid(i, 0, N_SLOT_TILES):
                    act.wait_ge(up_done, 2 * i + 1)
                    act.activation(e_gl[p][:, :], eg_ps[p][:, 0:HR], ACT.Gelu).then_inc(e_gelu, 1)

            copy_in(0, 0)
            for i in range(4):
                expert(i // 2, i % 2)
            with act.Fori(2, N_SLOT_TILES // 2 - 1) as k:
                expert(k, 0)
                expert(k, 1)
            for i in range(N_SLOT_TILES - 2, N_SLOT_TILES + 2):
                expert(i // 2, i % 2)

            act.wait_ge(l1_in, 16 * 11)

            def copy_x1(j, p):
                act.wait_ge(x1T_done, j + 1)
                act.activation(x1_t[p][:, :], x1t_ps[:, 0:P], ACT.Copy).then_inc(x1_t_ready, 1)

            def layer1(k, p):
                q = 2 * k + p
                for s in range(QUAD):
                    if valid(q):
                        act.wait_ge(r_done, 4 * q + s + 1)
                        if s == 0 and valid(q, 2):
                            act.wait_ge(rT_done, q - 1)
                        act.activation(r_t[p][:, s, :], rx_ps[p][:, s * BATCH:(s + 1) * BATCH], ACT.Tanh,
                                       bias=rb_sb[:, :]).then_inc(r_tanh, 1)
                    if s == 0 and valid(q + 2):
                        copy_x1(q + 2, p)
                    if s == 1 and valid(q - 2):
                        act.wait_ge(q1T_done, q - 1)
                        act.activation(q1_t[:, :], q1t_ps[:, 0:P // 2].bitcast(BF16), ACT.Copy).then_inc(q1_t_ready, 1)
                    if s == 2 and valid(q - 4):
                        act.wait_ge(q2T_done, q - 3)
                        act.activation(q2_t[:, :], q2t_ps[:, 0:HID // 2].bitcast(BF16), ACT.Copy).then_inc(q2_t_ready, 1)
                if valid(q - 2):
                    act.wait_ge(hid_ready, q - 1)
                    act.activation(gel[p][:, :], hid[p][:, :], ACT.Gelu).then_inc(gel_ready, 1)
                if valid(q - 3):
                    act.wait_ge(q2m_ready, q - 2)
                    act.activation(q2[1 - p][:, :], qm2[:, 1, :], ACT.Copy, bias=-MAGIC).then_inc(q2_ready, 1)

            copy_x1(0, 0)
            copy_x1(1, 1)
            for q in range(6):
                layer1(q // 2, q % 2)
            with act.Fori(3, QUADS // 2 - 1) as k:
                layer1(k, 0)
                layer1(k, 1)
            for q in range(QUADS - 2, QUADS + 4):
                layer1(q // 2, q % 2)

        @block.vector
        def _(dve):
            dve.wait_ge(bias_loaded, 16)
            dve.tensor_copy(bias_p[:, 0, :], bias_in[:, :]).then_inc(bias_split, 1)
            dve.wait_ge(bias_split, 1)
            dve.tensor_tensor(bias_r[:, 0, :], bias_in[:, :], bias_p[:, 0, :], ALU.subtract).then_inc(bias_chain, 1)
            dve.wait_ge(bias_chain, 1)
            dve.tensor_copy(bias_p[:, 1, :], bias_r[:, 0, :]).then_inc(bias_split, 1)
            dve.wait_ge(bias_split, 2)
            dve.tensor_tensor(bias_r[:, 1, :], bias_r[:, 0, :], bias_p[:, 1, :], ALU.subtract).then_inc(bias_chain, 1)
            dve.wait_ge(bias_chain, 2)
            dve.tensor_copy(bias_p[:, 2, :], bias_r[:, 1, :]).then_inc(bias_split, 1)
            dve.memset(mv[:, :, :], 1.0).then_inc(mv_init, 1)

            def gru_quad(k, p):
                q = 2 * k + p
                side = valid(q - 1)
                for s in range(QUAD):
                    prev = h_prev[:, :] if s == 0 else h2[p][:, s - 1, :]
                    dve.wait_ge(zr_tanh, 4 * q + s + 1)
                    if s == 0:
                        dve.wait_ge(prop_tanh, q)
                    dve.wait_ge(h_ready, 4 * q + s)
                    dve.scalar_tensor_tensor(g_rh[:, :], g_zr[:, 1, :], 1.0, prev, ALU.add, ALU.mult).then_inc(rh_ready, 1)
                    dve.scalar_tensor_tensor(g_na[:, :], g_zr[:, 0, :], 1.0, prev, ALU.subtract, ALU.mult)\
                       .then_inc(na_ready, 1)
                    if s == 1 and side:
                        router(q - 1, 1 - p, 0)
                    dve.wait_ge(c_tanh, 4 * q + s + 1)
                    dve.scalar_tensor_tensor(g_e[:, :], g_zr[:, 0, :], 1.0, g_c[:, :], ALU.add, ALU.mult)\
                       .then_inc(e_ready, 1)
                    dve.wait_ge(e_ready, 4 * q + s + 1)
                    dve.wait_ge(na_ready, 4 * q + s + 1)
                    if s == 0 and valid(q - 2):
                        dve.wait_ge(sh_done, q - 1)
                        dve.wait_ge(lg_done, q - 1)
                        dve.wait_ge(hT_done, q - 1)
                    dve.scalar_tensor_tensor(h2[p][:, s, :], g_na[:, :], -1.0 if s == 0 else -0.5, g_e[:, :],
                                             ALU.mult, ALU.add).then_inc(h_ready, 1)
                    if s == 1 and side:
                        router(q - 1, 1 - p, 1)
                    if s == 2 and side:
                        shared_act(q - 1)
                    if s == 0 and valid(q - 2):
                        add_shared(q - 2)

            def router(j, p, part):
                n = ROUTER_STEPS * j
                if part == 0:
                    dve.wait_ge(lg_done, j + 1)
                    dve.tensor_scalar(lg[p][:, :], l_ps[:, 0:E], 1.0 / TAU, None, ALU.mult).then_inc(lg_read, 1)
                    dve.wait_ge(lg_read, j + 1)
                    dve.tensor_copy(touched[:, 0:1], lg[p][:, 0:1])
                    dve.max(top[p][:, :], lg[p][:, :]).then_inc(rt, 1)
                else:
                    dve.wait_ge(rt, n + 1)
                    dve.tensor_copy(top_v[:, ds(j, 1), :].rearrange("q a n -> q (a n)"), top[p][:, 0:2])
                    dve.max_index(tix[p][:, :], top[p][:, :], lg[p][:, :]).then_inc(rt, 1)
                    dve.wait_ge(rt, n + 2)
                    dve.tensor_copy(top_i[:, ds(j, 1), :].rearrange("q a n -> q (a n)"), tix[p][:, 0:2]).then_inc(rt, 1)

            def shared_act(j):
                dve.wait_ge(s_gelu, j + 1)
                if valid(j, 1):
                    dve.wait_ge(sT_done, j)
                dve.tensor_tensor(s_act[:, :], a_ps[:, 0:HS], s_gl[:, :], ALU.mult).then_inc(s_act_ready, 1)

            def add_shared(j):
                dve.wait_ge(sy_done, j + 1)
                r = res[:, ds(j, 1), :].rearrange("q a n -> q (a n)")
                dve.tensor_tensor(r, r, y_ps[:, 0:D], ALU.add).then_inc(res_ready, 1)

            dve.wait_ge(ffn_in, 16 * 5)
            dve.wait_ge(h0_in, 32)
            gru_quad(0, 0)
            gru_quad(0, 1)
            with dve.Fori(1, QUADS // 2) as k:
                gru_quad(k, 0)
                gru_quad(k, 1)
            add_shared(QUADS - 2)
            router(QUADS - 1, 1, 0)
            router(QUADS - 1, 1, 1)
            shared_act(QUADS - 1)
            add_shared(QUADS - 1)

            dve.wait_ge(consts, 9)
            dve.wait_ge(rt, ROUTER_STEPS * QUADS)
            for k in range(2):
                dve.tensor_tensor(hot[:, k, :, :], iota_e[:, :].unsqueeze(1).to_broadcast([P, QUADS, E]),
                                  top_i[:, :, k:k + 1].to_broadcast([P, QUADS, E]), ALU.is_equal).then_inc(sl, 1)
            dve.wait_ge(sl, 2)
            dve.tensor_tensor(hot_any[:, :, :], hot[:, 0, :, :], hot[:, 1, :, :], ALU.add).then_inc(sl, 1)
            dve.tensor_tensor(dv[:, :], top_v[:, :, 0], top_v[:, :, 1], ALU.subtract).then_inc(sl, 1)
            dve.wait_ge(rank_done, 1)
            dve.tensor_scalar(cnt[:, 0, :], rank_ps[:, QUADS * E:(QUADS + 1) * E], 1.0 / P, 0.5 - 0.5 / P,
                              ALU.mult, ALU.add).then_inc(sl, 1)
            dve.wait_ge(sl, 5)
            dve.tensor_scalar(cnt[:, 1, :], cnt[:, 0, :], MAGIC, None, ALU.add).then_inc(sl, 1)
            dve.wait_ge(sl, 6)
            dve.tensor_scalar(cnt[:, 2, :], cnt[:, 1, :], MAGIC, None, ALU.subtract).then_inc(sl, 1)
            dve.wait_ge(sl, 7)
            dve.tensor_tensor_scan(ends[:, :], ones_e[:, :], cnt[:, 2, :], 0.0, ALU.mult, ALU.add).then_inc(sl, 1)
            dve.wait_ge(sl, 8)
            dve.tensor_tensor(cnt[:, 3, :], ends[:, :], cnt[:, 2, :], ALU.subtract).then_inc(sl, 1)
            dve.wait_ge(sl, 9)
            dve.tensor_scalar(base[:, :], cnt[:, 3, :], float(P), None, ALU.mult).then_inc(sl, 1)
            dve.wait_ge(sl, 10)
            dve.tensor_tensor(where_e[:, :, :], rank_ps[:, 0:QUADS * E].rearrange("q (j e) -> q j e", e=E),
                              base[:, :].unsqueeze(1).to_broadcast([P, QUADS, E]), ALU.add).then_inc(sl, 1)
            dve.wait_ge(sl, 11)
            for k in range(2):
                dve.tensor_tensor(picked[:, k, :, :], hot[:, k, :, :], where_e[:, :, :], ALU.mult).then_inc(sl, 1)
            dve.wait_ge(sl, 13)
            dve.tensor_reduce(slot_f[:, :, :], picked[:, :, :, :], AX_X, ALU.add).then_inc(sl, 1)
            dve.wait_ge(sl, 14)
            dve.tensor_copy(slot[:, :, :], slot_f[:, :, :]).then_inc(slot_ready, 1)
            dve.tensor_tensor(past[:, :, :], ends[0:1, :].unsqueeze(1).to_broadcast([1, N_SLOT_TILES, E]),
                              iota_t[:, :].unsqueeze(2).to_broadcast([1, N_SLOT_TILES, E]), ALU.is_le).then_inc(sl, 1)
            dve.wait_ge(sl, 15)
            dve.tensor_reduce(eid_f[:, :], past[:, :, :], AX_X, ALU.add).then_inc(sl, 1)
            dve.wait_ge(sl, 16)
            dve.tensor_scalar(eid_m[:, :], eid_f[:, :], float(E - 1), None, ALU.min).then_inc(sl, 1)
            dve.wait_ge(sl, 17)
            dve.tensor_copy(eid[:, :], eid_m[:, :]).then_inc(eid_ready, 1)
            dve.wait_ge(th_ready, 1)
            dve.tensor_scalar(pick_w[:, 0, :], th[:, :], 0.5, 0.5, ALU.mult, ALU.add).then_inc(pw_ready, 1)
            dve.tensor_scalar(pick_w[:, 1, :], th[:, :], -0.5, 0.5, ALU.mult, ALU.add).then_inc(pw_ready, 1)

            dve.wait_ge(l1_in, 16 * 11)
            for n, w in enumerate((w1_raw, w2_raw)):
                dve.tensor_reduce(w_abs[:, n:n + 1], w[:, :], AX_X, ALU.add, apply_absolute_value=True)\
                   .then_inc(wsum_ready, 1)
            dve.wait_ge(wsum_done, 1)
            dve.tensor_scalar(w_mean[:, :], y_ps[:, 256:258], 1.0 / (D * HID), EPS, ALU.mult, ALU.max).then_inc(wq, 1)
            dve.wait_ge(wq, 1)
            dve.reciprocal(w_inv[:, :], w_mean[:, :]).then_inc(wq, 1)
            dve.tensor_scalar(w_step[:, :], w_mean[:, :], 1.0 / 127.0, None, ALU.mult).then_inc(wq, 1)
            for n, (w, wq_out) in enumerate(((w1_raw, w1_q), (w2_raw, w2_q))):
                dve.wait_ge(wq, 3 + 2 * n)
                dve.tensor_scalar(wq_tmp[:, 0, :], w[:, :], w_inv[:, n:n + 1], MAGIC, ALU.mult, ALU.add).then_inc(wq, 1)
                dve.wait_ge(wq, 4 + 2 * n)
                dve.tensor_scalar(wq_tmp[:, 1, :], wq_tmp[:, 0, :], MAGIC + 1.0, MAGIC - 1.0, ALU.min, ALU.max)\
                   .then_inc(wq, 1)
                dve.wait_ge(wq, 5 + 2 * n)
                dve.tensor_scalar(wq_out[:, :], wq_tmp[:, 1, :], MAGIC, None, ALU.subtract).then_inc(wq_ready, 1)

            def expert(k, p):
                i = 2 * k + p
                if valid(i, 0, N_SLOT_TILES):
                    dve.wait_ge(e_gelu, i + 1)
                    dve.wait_ge(up_done, 2 * i + 2)
                    if valid(i - 2, 0, N_SLOT_TILES):
                        dve.wait_ge(eT_done, i - 1)
                    dve.tensor_tensor(e_act[p][:, :], ea_ps[p][:, 0:HR], e_gl[p][:, :], ALU.mult).then_inc(e_act_ready, 1)
                if valid(i - 2, 0, N_SLOT_TILES):
                    dve.wait_ge(ey_done, i - 1)
                    if valid(i - 4, 0, N_SLOT_TILES):
                        dve.wait_ge(e_y_out[p], 16 * (k - 1))
                    dve.tensor_copy(e_y[p][:, :], ey_ps[:, 0:D]).then_inc(e_y_ready, 1)

            for i in range(4):
                expert(i // 2, i % 2)
            with dve.Fori(2, N_SLOT_TILES // 2) as k:
                expert(k, 0)
                expert(k, 1)
            for i in range(N_SLOT_TILES, N_SLOT_TILES + 2):
                expert(i // 2, i % 2)

            dve.wait_ge(pw_ready, 2)
            dve.wait_ge(mv_init, 1)
            dve.wait_ge(res_ready, QUADS)

            def combine(k, p):
                j = 2 * k + p
                dve.wait_ge(gathered[p], 32 * (k + 1))
                if valid(j, 1):
                    dve.wait_ge(x1_ready, j)
                dve.scalar_tensor_tensor(y_sum[:, :], y_got[0][p][:, :], pick_w[:, 0, ds(j, 1)],
                                         res[:, ds(j, 1), :].rearrange("q a n -> q (a n)"), ALU.mult, ALU.add)\
                   .then_inc(ysum_ready, 1)
                dve.wait_ge(ysum_ready, j + 1)
                if valid(j, 2):
                    dve.wait_ge(x1T_done, j - 1)
                    dve.wait_ge(x1_kept, j - 1)
                dve.scalar_tensor_tensor(x1[p][:, :], y_got[1][p][:, :], pick_w[:, 1, ds(j, 1)], y_sum[:, :],
                                         ALU.mult, ALU.add).then_inc(x1_ready, 1)

            def quantise(v, scr, am, sc, dq, n, chain, at):
                dve.tensor_reduce(am[:, 0:1], v, AX_X, ALU.max, apply_absolute_value=True).then_inc(chain, 1)
                dve.wait_ge(chain, at + 1)
                dve.tensor_scalar(am[:, 1:2], am[:, 0:1], EPS, None, ALU.max).then_inc(chain, 1)
                dve.wait_ge(chain, at + 2)
                dve.reciprocal(sc[:, 0:1], am[:, 1:2]).then_inc(chain, 1)
                dve.tensor_scalar(dq, am[:, 1:2], w_step[:, n:n + 1], None, ALU.mult)
                dve.wait_ge(chain, at + 3)
                dve.tensor_scalar(sc[:, 1:2], sc[:, 0:1], 127.0, None, ALU.mult).then_inc(chain, 1)
                dve.wait_ge(chain, at + 4)
                dve.tensor_scalar(scr[:, 0, :], v, sc[:, 1:2], MAGIC, ALU.mult, ALU.add).then_inc(chain, 1)
                dve.wait_ge(chain, at + 5)
                return dve.tensor_scalar(scr[:, 1, :], scr[:, 0, :], MAGIC + 127.0, MAGIC - 128.0, ALU.min, ALU.max)

            def norm_stats(v, st, n, chain, at):
                dve.bn_stats(st[:, :], v).then_inc(chain, 1)
                dve.wait_ge(chain, at + 1)
                dve.tensor_copy(touched[:, 1:2], st[:, 0:1])
                dve.bn_aggr(mv[:, n, :], st[:, :]).then_inc(chain, 1)

            def rsqrts(i):
                at = RSQRT_STEPS * i
                dve.tensor_scalar(var_e[:, :], mv[:, :, 1], EPS, None, ALU.add).then_inc(rq, 1)
                dve.wait_ge(rq, at + 1)
                dve.tensor_scalar(half_bits[:, :], var_e[:, :].bitcast(I32), 1, None, ALU.logical_shift_right).then_inc(rq, 1)
                dve.wait_ge(rq, at + 2)
                dve.tensor_scalar(rsq[0][:, :].bitcast(I32), half_bits[:, :], -1.0, float(0x5F3759DF), ALU.mult, ALU.add)\
                   .then_inc(rq, 1)
                for n in range(3):
                    y = rsq[n][:, :]
                    dve.wait_ge(rq, at + 3 * n + 3)
                    dve.tensor_tensor(rsq_t[:, 0, :], y, y, ALU.mult).then_inc(rq, 1)
                    dve.wait_ge(rq, at + 3 * n + 4)
                    dve.scalar_tensor_tensor(rsq_t[:, 1, :], rsq_t[:, 0, :], -0.5, var_e[:, :], ALU.mult, ALU.mult)\
                       .then_inc(rq, 1)
                    dve.wait_ge(rq, at + 3 * n + 5)
                    dve.scalar_tensor_tensor(rsq[n + 1][:, :], rsq_t[:, 1, :], 1.5, y, ALU.add, ALU.mult).then_inc(rq, 1)
                dve.wait_ge(rq, at + RSQRT_STEPS)

            def norm1_stats(j):
                dve.wait_ge(rT_done, j + 1)
                norm_stats(rt_ps[:, 0:P], st1, 0, f1, LN1_STEPS * j)

            def norm1(j, p):
                at = LN1_STEPS * j
                dve.wait_ge(f1, at + 2)
                dve.scalar_tensor_tensor(n1[:, :], rt_ps[:, 0:P], mv[:, 0, 0:1], ln1w_sb[:, :], ALU.subtract,
                                         ALU.mult).then_inc(f1_norm, 1)
                dve.wait_ge(f1_norm, j + 1)
                dve.scalar_tensor_tensor(ln1[:, :], n1[:, :], rsq[3][:, 0:1], ln1b_sb[:, :], ALU.mult,
                                         ALU.add).then_inc(f1, 1)
                dve.wait_ge(f1, at + 3)
                if valid(j, 1):
                    dve.wait_ge(q1_ready, j)
                quantise(ln1[:, :], qm1, am1, sc1, dq1[p][:, :], 0, f1, at + 3).then_inc(f1, 1)
                dve.wait_ge(f1, at + LN1_STEPS)
                if valid(j, 2):
                    dve.wait_ge(q1T_done, j - 1)
                dve.tensor_scalar(q1[p][:, :], qm1[:, 1, :], MAGIC, None, ALU.subtract).then_inc(q1_ready, 1)

            def hidden(j, p):
                dve.wait_ge(m1_done, j + 1)
                if valid(j, 2):
                    dve.wait_ge(gel_ready, j - 1)
                dve.scalar_tensor_tensor(hid[p][:, :], m1_ps[:, :], dq1[p][:, 0:1], b1_sb[:, :], ALU.mult,
                                         ALU.add).then_inc(hid_ready, 1)

            def norm2_stats(j, p):
                dve.wait_ge(gel_ready, j + 1)
                norm_stats(gel[p][:, :], st2, 1, f2, LN2_STEPS * j)

            def norm2(j, p):
                at = LN2_STEPS * j
                dve.wait_ge(f2, at + 2)
                dve.scalar_tensor_tensor(n2[:, :], gel[p][:, :], mv[:, 1, 0:1], ln2w_sb[:, :], ALU.subtract,
                                         ALU.mult).then_inc(f2, 1)
                dve.wait_ge(f2, at + 3)
                dve.scalar_tensor_tensor(ln2[:, :], n2[:, :], rsq[3][:, 1:2], ln2b_sb[:, :], ALU.mult, ALU.add)\
                   .then_inc(f2, 1)
                dve.wait_ge(f2, at + 4)
                if valid(j, 1):
                    dve.wait_ge(q2_ready, j)
                quantise(ln2[:, :], qm2, am2, sc2, dq2[p][:, :], 1, f2, at + 4).then_inc(q2m_ready, 1)

            def finish(j, p):
                dve.wait_ge(m2_done, j + 1)
                if valid(j, 1):
                    dve.wait_ge(o_ready, j)
                dve.scalar_tensor_tensor(fo[:, :], m2_ps[:, 0:D], dq2[p][:, 0:1], b2_sb[:, :], ALU.mult,
                                         ALU.add).then_inc(fo_ready, 1)
                dve.wait_ge(fo_ready, j + 1)
                dve.wait_ge(x1_kept, j + 1)
                if valid(j, 2):
                    dve.wait_ge(o_out[p], 8 * (j - p))
                dve.tensor_tensor(o_sb[p][:, :], fo[:, :], res[:, ds(j, 1), :].rearrange("q a n -> q (a n)"),
                                  ALU.add).then_inc(o_ready, 1)

            def layer1(k, p):
                q = 2 * k + p
                o = 1 - p
                if valid(q + 2):
                    combine(k + 1, p)
                if valid(q - 1):
                    norm1_stats(q - 1)
                if valid(q - 3):
                    norm2_stats(q - 3, o)
                if valid(q - 1):
                    dve.wait_ge(f1, LN1_STEPS * (q - 1) + 2)
                if valid(q - 3):
                    dve.wait_ge(f2, LN2_STEPS * (q - 3) + 2)
                if valid(q - 1) or valid(q - 3):
                    rsqrts(q - 1)
                if valid(q - 1):
                    norm1(q - 1, o)
                if valid(q - 2):
                    hidden(q - 2, p)
                if valid(q - 3):
                    norm2(q - 3, o)
                if valid(q - 4):
                    finish(q - 4, p)

            combine(0, 0)
            combine(0, 1)
            for q in range(6):
                layer1(q // 2, q % 2)
            with dve.Fori(3, QUADS // 2 - 1) as k:
                layer1(k, 0)
                layer1(k, 1)
            for q in range(QUADS - 2, QUADS + 4):
                layer1(q // 2, q % 2)



def kernel(**inputs):
    import numpy as np
    import concourse.bacc as bacc
    from concourse import mybir as _mybir
    from concourse.bass_utils import run_bass_kernel_spmd as run

    g = {n: np.asarray(a) for n, a in inputs.items()}
    x = g["x"]
    time_major = x.transpose(1, 0, 2).reshape(TOKENS, D)
    gates = np.stack([g["L0_cond_Wz"], g["L0_cond_Wr"], g["L0_cond_Wh"]])
    gates = gates.reshape(3, 2, P, P).transpose(2, 1, 0, 3).reshape(P, 6 * P)

    def split_rows(w, parts):
        return w.reshape(parts, P, w.shape[-1]).transpose(1, 0, 2).reshape(P, -1)

    laid = {
        "x_t": time_major.T,
        "x_tok": split_rows(time_major, QUADS),
        "h0_t": g["cond_1024"].T,
        "gru_w": gates,
        "gru_b": np.concatenate([g["L0_cond_bz"], g["L0_cond_br"], g["L0_cond_bh"]])[None, :],
        "gru_wp": g["L0_cond_Wp"],
        "gru_bp": g["L0_cond_bp"][:, None],
        "we1": g["L0_ffn_We1"].transpose(1, 0, 2).reshape(P, -1),
        "we2": g["L0_ffn_We2"].reshape(E, 3, P, D).transpose(2, 0, 1, 3).reshape(P, -1),
        "ws1": g["L0_ffn_Ws1"],
        "ws2": split_rows(g["L0_ffn_Ws2"], 2),
        "wr": g["L0_ffn_Wr"],
        "br": g["L0_ffn_br"][None, :],
        "bias": np.concatenate([g["L0_ffn_be1"].ravel(), g["L0_ffn_be2"].ravel(), g["L0_ffn_bs1"],
                                g["L0_ffn_bs2"]]).reshape(BIAS_ROWS, P),
        "rnn_wx": g["L1_cond_Wx"],
        "rnn_wh": g["L1_cond_Wh"],
        "rnn_b": g["L1_cond_b"][:, None],
        "w1_t": g["L1_ffn_w1"].T,
        "w2_t": split_rows(g["L1_ffn_w2"].T, 4),
        "ln1_w": g["L1_ffn_ln1_w"][None, :],
        "ln1_b": g["L1_ffn_ln1_b"][None, :],
        "b1": g["L1_ffn_b1"][None, :],
        "ln2_w": g["L1_ffn_ln2_w"][None, :],
        "ln2_b": g["L1_ffn_ln2_b"][None, :],
        "b2": g["L1_ffn_b2"][None, :],
    }
    nc = bacc.Bacc("TRN2", target_bir_lowering=False, num_devices=1)
    arrays, args = {}, []
    for name, a in laid.items():
        a = np.ascontiguousarray(a)
        arrays[f"in_{name}"] = a
        args.append(nc.dram_tensor(f"in_{name}", a.shape, _mybir.dt.from_np(a.dtype), kind="ExternalInput").ap())
    args.append(nc.dram_tensor("out_0", (TOKENS, D), F32, kind="ExternalOutput").ap())
    build(nc, *args)
    r = run(nc, [arrays], core_ids=[0])
    got = r.results[0]["out_0"]
    return got.reshape(STEPS, BATCH, D).transpose(1, 0, 2)
```

```python
from contextlib import ExitStack

import concourse.bass as bass
from concourse import mybir

F32 = mybir.dt.float32
BF16 = mybir.dt.bfloat16
F16 = mybir.dt.float16
I32 = mybir.dt.int32
U32 = mybir.dt.uint32
ALU = mybir.AluOpType
ACT = mybir.ActivationFunctionType
AX_X = mybir.AxisListType.X

P = 128
BATCH, STEPS, D = 32, 128, 128
TOKENS = BATCH * STEPS
QUAD = 4
QUADS = STEPS // QUAD
PAIRS = QUADS // 2
E = 12
HS, HR = 2 * D, 3 * D
TAU = 1.5
HID = 512
EPS = 1e-5
MAGIC = 12582912.0
N_SLOT_TILES = 2 * TOKENS // P + E
N_SLOT_TILES += N_SLOT_TILES % 2
N_SLOTS = N_SLOT_TILES * P
B1_AT, B2_AT = 0, E * 2 * HR
BS1_AT = B2_AT + E * D
BS2_AT = BS1_AT + 2 * HS
BR_AT = BS2_AT + D
BG_AT = BR_AT + P
N_BIAS = BG_AT + 3 * P
BIAS_ROWS = N_BIAS // P
W_SCALE = 64.0
ds = bass.ds


def valid(q, lo=0, hi=QUADS):
    return lo <= q < hi if isinstance(q, int) else True


def build(nc, x_t, x_tok, h0_t, gru_w, gru_wp, gru_bp, we1, we2, ws1, ws2, wr, bias,
          rnn_wx, rnn_wh, rnn_b, w1_t, w2_t, ln1_w, ln1_b, b1, ln2_w, ln2_b, b2, out):
    with ExitStack() as ctx:
        def sb(name, shape, dt=F32):
            return ctx.enter_context(nc.sbuf_tensor(name, shape, dt))

        def sem(name):
            return ctx.enter_context(nc.semaphore(name))

        bank = [ctx.enter_context(nc.psum_tensor(f"bank{i}", [P, 512], F32)) for i in range(8)]

        slots_in = nc.dram_tensor("slots_in", (N_SLOTS, D), F32, kind="Internal").ap()
        slots_out = nc.dram_tensor("slots_out", (N_SLOTS, D), F32, kind="Internal").ap()

        ident = sb("ident", [P, P])
        ident_b = sb("ident_b", [P, P], BF16)
        ones_b = sb("ones_b", [P, P], BF16)
        ones_f = sb("ones_f", [P, P])
        before = sb("before", [P, P], BF16)
        iota_e = sb("iota_e", [P, E])
        iota_t = sb("iota_t", [1, N_SLOT_TILES])
        zeros = sb("zeros", [P, D])
        g_w = sb("g_w", [P, 2, 3, P])
        gx = sb("gx", [P, 3, P])
        w_new = sb("w_new", [P, 2, 4, P], F16)
        w_kept = sb("w_kept", [P, 2, 4, P], F16)
        w_prod = sb("w_prod", [P, 2, P], F16)
        scale_row = sb("scale_row", [3, P], BF16)
        wp_sb = sb("wp_sb", [P, P])
        bp_sb = sb("bp_sb", [P, 1])
        we1_sb = sb("we1_sb", [P, E * 2 * HR])
        we2_sb = sb("we2_sb", [P, E * HR])
        ws1_sb = sb("ws1_sb", [P, 2 * HS])
        ws2_sb = sb("ws2_sb", [P, 2, D])
        wr_sb = sb("wr_sb", [P, E])
        bias_in = sb("bias_in", [BIAS_ROWS, P])
        bias_r = sb("bias_r", [BIAS_ROWS, 2, P])
        bias_p = sb("bias_p", [BIAS_ROWS, 3, P], BF16)
        bias3 = sb("bias3", [3, N_BIAS], BF16)
        wx_sb = sb("wx_sb", [P, P])
        rwh_sb = sb("rwh_sb", [P, P])
        rb_sb = sb("rb_sb", [P, 1])
        w1_raw = sb("w1_raw", [P, HID])
        w2_raw = sb("w2_raw", [P, HID])
        w1_q = sb("w1_q", [P, HID], BF16)
        w2_q = sb("w2_q", [P, HID], BF16)
        w_abs = sb("w_abs", [P, 2])
        w_mean = sb("w_mean", [P, 2])
        w_inv = sb("w_inv", [P, 2])
        ln1w_sb = sb("ln1w_sb", [P, D])
        ln1b_sb = sb("ln1b_sb", [P, D])
        b1_sb = sb("b1_sb", [P, HID])
        ln2w_sb = sb("ln2w_sb", [P, HID])
        ln2b_sb = sb("ln2b_sb", [P, HID])
        b2_sb = sb("b2_sb", [P, D])

        xt_sb = sb("xt_sb", [P, TOKENS])
        res = sb("res", [P, QUADS, D])
        h_tok = sb("h_tok", [P, QUADS, D])

        h_prev = sb("h_prev", [P, BATCH])
        h_prev2 = sb("h_prev2", [P, BATCH])
        h_prev_p = sb("h_prev_p", [P, 2, BATCH], F16)
        g_r = sb("g_r", [P, BATCH])
        g_z = sb("g_z", [P, BATCH])
        g_rh = sb("g_rh", [P, BATCH])
        g_rh_p = sb("g_rh_p", [P, 2, BATCH], F16)
        g_na = sb("g_na", [P, BATCH])
        g_na_p = sb("g_na_p", [P, 2, BATCH], F16)
        g_c = sb("g_c", [P, BATCH])
        g_e = sb("g_e", [P, BATCH])
        g_e_p = sb("g_e_p", [P, 2, BATCH], F16)
        h2 = [sb(f"h2_{p}", [P, QUAD, BATCH]) for p in range(2)]

        lg = [sb(f"lg{p}", [P, E]) for p in range(2)]
        top = [sb(f"top{p}", [P, 8]) for p in range(2)]
        tix = [sb(f"tix{p}", [P, 8], U32) for p in range(2)]
        top_v = sb("top_v", [P, QUADS, 2])
        top_i = sb("top_i", [P, QUADS, 2])
        s_gl = sb("s_gl", [P, HS])
        s_act = sb("s_act", [P, HS])
        s_at = sb("s_at", [P, HS])

        hot = sb("hot", [P, 2, QUADS, E], BF16)
        hot_any = sb("hot_any", [P, QUADS, E], BF16)
        cnt = sb("cnt", [P, 4, E])
        ones_e = sb("ones_e", [P, E])
        ends = sb("ends", [P, E])
        base = sb("base", [P, E])
        where_e = sb("where_e", [P, QUADS, E])
        picked = sb("picked", [P, 2, QUADS, E])
        slot_f = sb("slot_f", [P, 2, QUADS])
        slot = sb("slot", [P, 2, QUADS], U32)
        past = sb("past", [1, N_SLOT_TILES, E])
        eid_f = sb("eid_f", [1, N_SLOT_TILES])
        eid_m = sb("eid_m", [1, N_SLOT_TILES])
        eid = sb("eid", [1, N_SLOT_TILES], I32)
        v_gap = sb("v_gap", [P, QUADS])
        th = sb("th", [P, QUADS])
        pick_w = sb("pick_w", [P, 2, QUADS])

        xg = [sb(f"xg{p}", [P, D]) for p in range(2)]
        xg_t = [sb(f"xg_t{p}", [P, P]) for p in range(2)]
        e_gl = [sb(f"e_gl{p}", [P, HR]) for p in range(2)]
        e_act = [sb(f"e_act{p}", [P, HR]) for p in range(2)]
        e_at = [sb(f"e_at{p}", [P, HR]) for p in range(2)]
        e_y = [sb(f"e_y{p}", [P, D]) for p in range(2)]

        late = [xt_sb[:, i * 2 * HID:(i + 1) * 2 * HID].rearrange("q (a n) -> q a n", a=2) for i in range(4)]
        hid, gel, n2, ln2 = late
        wq_tmp = gel

        y_got = sb("y_got", [P, 2, 2, D])
        y_sum = sb("y_sum", [P, 2, D])
        x1 = sb("x1", [P, 2, D])
        x1_t = sb("x1_t", [P, 2, P])
        r_t = [sb(f"r_t{p}", [P, QUAD, BATCH]) for p in range(2)]
        r_start = sb("r_start", [P, BATCH])
        touched = sb("touched", [P, 2])
        stats = sb("stats", [P, 4, 6])
        mv = sb("mv", [P, 4, 2])
        var_e = sb("var_e", [P, 4])
        half_bits = sb("half_bits", [P, 4], I32)
        rsq = [sb(f"rsq{i}", [P, 4]) for i in range(4)]
        rsq_t = sb("rsq_t", [P, 2, 4])
        amax = sb("amax", [P, 4])
        amax_e = sb("amax_e", [P, 4])
        inv = sb("inv", [P, 4])
        to_int = sb("to_int", [P, 4])
        step4 = sb("step4", [P, 4])
        dq = sb("dq", [P, 4])
        n1 = sb("n1", [P, 2, D])
        ln1 = sb("ln1", [P, 2, D])
        qm1 = sb("qm1", [P, 2, D])
        q1 = sb("q1", [P, 2, D], BF16)
        q1_t = sb("q1_t", [P, 2, P], BF16)
        q2 = sb("q2", [P, 2, HID], BF16)
        q2_t = sb("q2_t", [P, 2, HID], BF16)
        o_sb = [sb(f"o_sb{p}", [P, D]) for p in range(2)]

        gru_in = sem("gru_in")
        gru_x = sem("gru_x")
        ffn_in = sem("ffn_in")
        exp_in = sem("exp_in")
        l1_in = sem("l1_in")
        bias_loaded = sem("bias_loaded")
        bias_moved = sem("bias_moved")
        consts = sem("consts")
        consts_c = sem("consts_c")
        zeroed = sem("zeroed")
        w_scaled = sem("w_scaled")
        bias_chain = sem("bias_chain")
        bias_split = sem("bias_split")
        h0_in = sem("h0_in")
        w_split = sem("w_split")
        hp_ready = sem("hp_ready")
        r_gate = sem("r_gate")
        z_gate = sem("z_gate")
        r_tanhed = sem("r_tanhed")
        z_tanhed = sem("z_tanhed")
        rh_ready = sem("rh_ready")
        na_ready = sem("na_ready")
        c_done = sem("c_done")
        c_tanh = sem("c_tanh")
        e_ready = sem("e_ready")
        h_ready = sem("h_ready")
        prop_done = sem("prop_done")
        prop_tanh = sem("prop_tanh")
        hT_done = sem("hT_done")
        h_tok_ready = sem("h_tok_ready")
        lg_done = sem("lg_done")
        lg_read = sem("lg_read")
        rt = sem("rt")
        sh_done = sem("sh_done")
        s_gelu = sem("s_gelu")
        s_act_ready = sem("s_act_ready")
        sT_done = sem("sT_done")
        s_at_ready = sem("s_at_ready")
        sy_done = sem("sy_done")
        res_ready = sem("res_ready")
        sl = sem("sl")
        th_ready = sem("th_ready")
        rank_done = sem("rank_done")
        eid_ready = sem("eid_ready")
        slot_ready = sem("slot_ready")
        pw_ready = sem("pw_ready")
        scattered = sem("scattered")
        xg_in = [sem(f"xg_in{p}") for p in range(2)]
        xgT_done = sem("xgT_done")
        xg_t_ready = sem("xg_t_ready")
        up_done = sem("up_done")
        e_gelu = sem("e_gelu")
        e_act_ready = sem("e_act_ready")
        eT_done = sem("eT_done")
        e_at_ready = sem("e_at_ready")
        ey_done = sem("ey_done")
        e_y_ready = sem("e_y_ready")
        e_y_out = [sem(f"e_y_out{p}") for p in range(2)]
        gathered = sem("gathered")
        x1_ready = sem("x1_ready")
        x1_kept = sem("x1_kept")
        x1T_done = sem("x1T_done")
        x1_t_ready = sem("x1_t_ready")
        r_done = sem("r_done")
        r_tanh = sem("r_tanh")
        rT_done = sem("rT_done")
        dv = sem("dv")
        mv_init = sem("mv_init")
        n1_read = sem("n1_read")
        n2_read = sem("n2_read")
        qm1_ready = sem("qm1_ready")
        q1_ready = sem("q1_ready")
        q1T_done = sem("q1T_done")
        q1_t_ready = sem("q1_t_ready")
        m1_done = sem("m1_done")
        m1_scaled = sem("m1_scaled")
        hid_ready = sem("hid_ready")
        gel_ready = sem("gel_ready")
        qm2_ready = sem("qm2_ready")
        q2_ready = sem("q2_ready")
        q2T_done = sem("q2T_done")
        q2_t_ready = sem("q2_t_ready")
        m2_done = sem("m2_done")
        o_ready = sem("o_ready")
        o_out = [sem(f"o_out{p}") for p in range(2)]
        wq = sem("wq")
        wsum_ready = sem("wsum_ready")
        wsum_done = sem("wsum_done")
        wq_ready = sem("wq_ready")

        ROUTER_STEPS = 3

        r_ps, zc_ps = bank[0:2], bank[2:4]
        t_ps, a_ps, y_ps, l_ps = bank[4], bank[5], bank[6], bank[7]
        ea_ps, eg_ps = bank[0:2], bank[2:4]
        ex_ps, et_ps, ey_ps = bank[4], bank[5], bank[6]
        rank_ps = bank[7]
        rx_ps = bank[0:2]
        in_ps, rt_ps, m1_ps, out_ps = bank[2], bank[3], bank[4:6], bank[6]
        x1t_at, q1t_at = 0, 2 * P
        q2t_at, m2_at = 0, 2 * P

        def z_cols(s):
            return slice(s * BATCH, (s + 1) * BATCH)

        def c_cols(s):
            return slice(P + s * BATCH, P + (s + 1) * BATCH)

        prop_cols = slice(2 * P, 2 * P + BATCH)

        block = ctx.enter_context(nc.Block())

        @block.sync
        def _(sp):
            first = 4 * P
            sp.dma_start(g_w[:, :, :, :], gru_w.rearrange("k (i g n) -> k i g n", i=2, g=3)).then_inc(gru_in, 16)
            sp.dma_start(xt_sb[:, 0:first], x_t[:, 0:first]).then_inc(gru_in, 16)
            sp.dma_start(bias_in[:, :], bias).then_inc(bias_loaded, 16)
            sp.dma_start(wp_sb[:, :], gru_wp).then_inc(gru_in, 16)
            sp.dma_start(bp_sb[:, :], gru_bp).then_inc(gru_in, 16)
            sp.dma_start(h_prev[:, :], h0_t).then_inc(h0_in, 16)
            sp.dma_start(r_start[:, :], h0_t).then_inc(h0_in, 16)
            sp.dma_start(ws1_sb[:, :], ws1).then_inc(ffn_in, 16)
            sp.dma_start(ws2_sb[:, :, :], ws2.rearrange("k (c n) -> k c n", c=2)).then_inc(ffn_in, 16)
            sp.dma_start(wr_sb[:, :], wr).then_inc(ffn_in, 16)
            sp.dma_start(xt_sb[:, first:TOKENS], x_t[:, first:TOKENS]).then_inc(gru_x, 16)
            sp.dma_start(res[:, :, :], x_tok.rearrange("q (i n) -> q i n", i=QUADS)).then_inc(ffn_in, 16)
            sp.wait_ge(bias_split, 3)
            for part in range(3):
                sp.dma_start(bias3[part:part + 1, :].rearrange("a (r n) -> a r n", n=P),
                             bias_p[:, part, :]).then_inc(bias_moved, 16)
            sp.dma_start(we1_sb[:, :], we1).then_inc(exp_in, 16)
            sp.dma_start(we2_sb[:, :], we2).then_inc(exp_in, 16)
            for dst, src in ((wx_sb, rnn_wx), (rwh_sb, rnn_wh), (rb_sb, rnn_b), (w1_raw, w1_t), (w2_raw, w2_t)):
                sp.dma_start(dst[:, :], src).then_inc(l1_in, 16)
            for dst, src in ((ln1w_sb, ln1_w), (ln1b_sb, ln1_b), (b1_sb, b1), (ln2w_sb, ln2_w),
                             (ln2b_sb, ln2_b), (b2_sb, b2)):
                sp.dma_start(dst[:, :], src.to_broadcast([P, src.shape[1]])).then_inc(l1_in, 16)
            sp.wait_ge(consts, 7)
            for i in range(4):
                n = N_SLOTS // 4
                sp.dma_start(slots_in[i * n:(i + 1) * n, :].rearrange("(i p) d -> p i d", p=P),
                             zeros[:, :].unsqueeze(1).to_broadcast([P, n // P, D])).then_inc(zeroed, 16)

            sp.wait_ge(scattered, 16 * 2 * QUADS)
            for p in range(2):
                sp.dma_start(xg[p][:, :], slots_in[ds(p * P, P), :]).then_inc(xg_in[p], 16)

            def expert_io(k, p):
                i = 2 * k + p
                if valid(i + 2, 0, N_SLOT_TILES):
                    sp.wait_ge(xgT_done, i + 1)
                    sp.dma_start(xg[p][:, :], slots_in[ds((i + 2) * P, P), :]).then_inc(xg_in[p], 16)
                if valid(i - 2, 0, N_SLOT_TILES):
                    sp.wait_ge(e_y_ready, i - 1)
                    sp.dma_start(slots_out[ds((i - 2) * P, P), :], e_y[p][:, :]).then_inc(e_y_out[p], 16)

            expert_io(0, 0)
            expert_io(0, 1)
            with sp.Fori(1, N_SLOT_TILES // 2 - 1) as k:
                expert_io(k, 0)
                expert_io(k, 1)
            for i in range(N_SLOT_TILES - 2, N_SLOT_TILES + 2):
                expert_io(i // 2, i % 2)

            def store(k, p):
                i = 2 * k + p
                sp.wait_ge(o_ready, i + 1)
                sp.dma_start(out[ds(i * P, P), :], o_sb[p][:, :]).then_inc(o_out[p], 16)

            with sp.Fori(0, QUADS // 2) as k:
                store(k, 0)
                store(k, 1)
            for p in range(2):
                sp.wait_ge(o_out[p], 16 * (QUADS // 2))

        @block.gpsimd
        def _(pool):
            pool.memset(ident[:, :], 0.0).then_inc(consts_c, 1)
            pool.memset(ident_b[:, :], 0.0).then_inc(consts_c, 1)
            pool.memset(before[:, :], 0.0).then_inc(consts_c, 1)
            pool.memset(ones_f[:, :], 1.0).then_inc(consts, 1)
            pool.memset(ones_b[:, :], 1.0).then_inc(consts, 1)
            pool.memset(zeros[:, :], 0.0).then_inc(consts, 1)
            pool.memset(ones_e[:, :], 1.0).then_inc(consts, 1)
            pool.wait_ge(consts_c, 3)
            for m in (ident, ident_b):
                pool.affine_select(out=m[:, :], in_=m[:, :], compare_op=ALU.not_equal, fill=1.0, base=0,
                                   pattern=[[-1, P]], channel_multiplier=1).then_inc(consts, 1)
            pool.affine_select(out=before[:, :], in_=before[:, :], compare_op=ALU.is_ge, fill=1.0, base=0,
                               pattern=[[-1, P]], channel_multiplier=1).then_inc(consts, 1)
            pool.memset(scale_row[:, :], W_SCALE).then_inc(consts, 1)
            pool.wait_ge(gru_in, 16 * 4)
            pool.tensor_scalar(gx[:, :, :], g_w[:, 0, :, :], W_SCALE, None, ALU.mult).then_inc(w_scaled, 1)
            pool.iota(iota_e[:, :], [[1, E]], base=0, channel_multiplier=0,
                      allow_small_or_imprecise_dtypes=True).then_inc(consts, 1)
            pool.iota(iota_t[:, :], [[1, N_SLOT_TILES]], base=0, channel_multiplier=0,
                      allow_small_or_imprecise_dtypes=True).then_inc(consts, 1)
            pool.wait_ge(ffn_in, 16 * 4)
            pool.tensor_scalar(ws1_sb[:, :], ws1_sb[:, :], 0.5, None, ALU.mult).then_inc(w_scaled, 1)
            pool.tensor_scalar(wr_sb[:, :], wr_sb[:, :], 0.5, None, ALU.mult).then_inc(w_scaled, 1)

            pool.wait_ge(zeroed, 64)
            pool.wait_ge(slot_ready, 1)
            pool.wait_ge(h_tok_ready, QUADS)
            for j in range(QUADS):
                for k in range(2):
                    pool.indirect_dma_start(
                        out=slots_in, out_offset=bass.IndirectOffsetOnAxis(ap=slot[:, k, j:j + 1], axis=0),
                        in_=h_tok[:, j, :], in_offset=None).then_inc(scattered, 16)
            for p in range(2):
                pool.wait_ge(e_y_out[p], 16 * (N_SLOT_TILES // 2))
            def collect(m):
                for p in range(2):
                    for k in range(2):
                        pool.indirect_dma_start(
                            out=y_got[:, k, p, :], out_offset=None, in_=slots_out,
                            in_offset=bass.IndirectOffsetOnAxis(ap=slot[:, k, 2 * m + p:2 * m + p + 1], axis=0))\
                            .then_inc(gathered, 16)

            collect(0)
            pool.wait_ge(l1_in, 16 * 11)
            for m in range(-1, PAIRS + 2):
                if m + 1 < PAIRS:
                    pool.wait_ge(x1_ready, 2 * (m + 2))
                    if m + 2 < PAIRS:
                        collect(m + 2)
                    pool.tensor_tensor(res[:, 2 * (m + 1):2 * (m + 2), :], x1[:, :, :],
                                       b2_sb[:, :].unsqueeze(1).to_broadcast([P, 2, D]), ALU.add).then_inc(x1_kept, 1)
                if 0 <= m - 2 < PAIRS:
                    for p in range(2):
                        pool.wait_ge(m1_scaled, 2 * (m - 2) + p + 1)
                        pool.tensor_tensor(hid[:, p, :], hid[:, p, :], b1_sb[:, :], ALU.add).then_inc(hid_ready, 1)
                if 0 <= m - 1 < PAIRS:
                    pool.wait_ge(qm1_ready, m)
                    if m >= 2:
                        pool.wait_ge(q1T_done, m - 1)
                    pool.tensor_scalar(q1[:, :, :], qm1[:, :, :], MAGIC, None, ALU.subtract).then_inc(q1_ready, 1)

        @block.tensor
        def _(pe):
            pe.wait_ge(consts, 10)
            pe.wait_ge(gru_in, 16 * 4)
            pe.wait_ge(w_scaled, 3)
            pe.wait_ge(w_split, 7)
            pe.wait_ge(bias_moved, 48)

            def steps_of(ps, lo):
                return ps[:, lo:lo + P].rearrange("q (s b) -> q s b", s=QUAD)

            def x_part(q, p, g):
                ps, lo = ((zc_ps[p], 0), (r_ps[p], 0), (zc_ps[p], P))[g]
                pe.matmul(ps[:, lo:lo + P], gx[:, g, :], xt_sb[:, ds(q * P, P)],
                          start=(g != 2), stop=False, skip_group_check=True)
                pe.matmul(ps[:, lo:lo + P], bias3[:, BG_AT + g * P:BG_AT + (g + 1) * P], scale_row[:, :],
                          start=False, stop=False, skip_group_check=True)

            def add(dst, w, v):
                return pe.matmul(dst, w, v, start=False, stop=False, skip_group_check=True)

            def add_high(dst, w, g, v):
                add(dst, w[:, 0, g, :], v[:, 0, :])
                add(dst, w[:, 1, g, :], v[:, 0, :])

            def shared_up(p, half):
                pe.matmul(a_ps[:, half * HS:(half + 1) * HS], h2[p][:, :, :], ws1_sb[:, half * HS:(half + 1) * HS],
                          start=(half == 0), stop=False, skip_group_check=True)

            def logits(p):
                pe.matmul(l_ps[:, 0:E], h2[p][:, :, :], wr_sb[:, :], start=True, stop=False)
                pe.matmul(l_ps[:, 0:E], ones_b[0:3, :], bias3[:, BR_AT:BR_AT + E], start=False,
                          stop=True).then_inc(lg_done, 1)

            def shared_bias():
                add(a_ps[:, 0:2 * HS], ones_b[0:3, :], bias3[:, BS1_AT:BS1_AT + 2 * HS]).then_inc(sh_done, 1)

            def gru_quad(k, p, last=False):
                q = 2 * k + p
                side = valid(q - 1)
                o = 1 - p
                for s in range(QUAD):
                    n = 3 * (4 * q + s)
                    z_at, r_at = zc_ps[p][:, z_cols(s)], r_ps[p][:, 0:P][:, z_cols(s)]
                    c_at = zc_ps[p][:, c_cols(s)]
                    if s == 0:
                        pe.wait_ge(hp_ready, 3 * q + 1)
                        add_high(r_at, w_new, 1, h_prev_p)
                        add_high(z_at, w_new, 0, h_prev_p)
                        pe.wait_ge(hp_ready, 3 * q + 3)
                        add(r_at, w_new[:, 0, 1, :], h_prev_p[:, 1, :]).then_inc(r_gate, 1)
                        add(z_at, w_new[:, 0, 0, :], h_prev_p[:, 1, :]).then_inc(z_gate, 1)
                    else:
                        pe.wait_ge(e_ready, n - 2)
                        add_high(r_at, w_new, 1, g_e_p)
                        add_high(z_at, w_new, 0, g_e_p)
                        pe.wait_ge(e_ready, n)
                        add(r_at, w_new[:, 0, 1, :], g_e_p[:, 1, :]).then_inc(r_gate, 1)
                        add(z_at, w_new[:, 0, 0, :], g_e_p[:, 1, :]).then_inc(z_gate, 1)
                    if s == 0 and side:
                        pe.wait_ge(h_ready, 4 * q)
                        pe.transpose(t_ps[:, 0:P], h2[o][:, :, :], ident[:, :]).then_inc(hT_done, 1)
                    if s == 1 and side:
                        shared_up(o, 0)
                    if s == 2 and valid(q + 1):
                        x_part(q + 1, o, 0)
                    if s == 3 and valid(q + 1):
                        x_part(q + 1, o, 2)
                    pe.wait_ge(z_tanhed, 4 * q + s + 1)
                    pe.wait_ge(rh_ready, n + 1)
                    add(c_at, w_prod[:, 0, :], g_rh_p[:, 0, :])
                    add(c_at, w_prod[:, 1, :], g_rh_p[:, 0, :])
                    pe.wait_ge(rh_ready, n + 3)
                    add(c_at, w_prod[:, 0, :], g_rh_p[:, 1, :]).then_inc(c_done, 1)
                    if s == 0 and side:
                        logits(o)
                    if s == 1 and side:
                        shared_up(o, 1)
                        shared_bias()
                    if s == 2 and valid(q + 1):
                        x_part(q + 1, o, 1)
                    if s == 3 and side:
                        shared_turn(q - 1)
                    if s == QUAD - 1 and last:
                        continue
                    pe.wait_ge(c_tanh, 4 * q + s + 1)
                    pe.wait_ge(na_ready, n + 3)
                    if s < QUAD - 1:
                        for g, at in ((1, r_ps[p][:, z_cols(s + 1)]), (0, zc_ps[p][:, z_cols(s + 1)])):
                            add_high(at, w_kept, g, g_na_p)
                            add(at, w_kept[:, 0, g, :], g_na_p[:, 1, :])
                    else:
                        at = zc_ps[p][:, prop_cols]
                        add_high(at, w_kept, 3, g_na_p)
                        add(at, w_kept[:, 0, 3, :], g_na_p[:, 1, :])
                        pe.wait_ge(e_ready, n + 1)
                        add_high(at, w_new, 3, g_e_p)
                        pe.wait_ge(e_ready, n + 3)
                        add(at, w_new[:, 0, 3, :], g_e_p[:, 1, :]).then_inc(prop_done, 1)
                if side:
                    shared_down(q - 1)

            def shared_turn(j):
                pe.wait_ge(s_act_ready, j + 1)
                pe.wait_ge(h_tok_ready, j + 1)
                pe.transpose(t_ps[:, 0:P], s_act[:, 0:P], ident[:, :])
                pe.transpose(t_ps[:, P:2 * P], s_act[:, P:2 * P], ident[:, :]).then_inc(sT_done, 1)

            def shared_down(j):
                pe.wait_ge(s_at_ready, j + 1)
                if valid(j, 1):
                    pe.wait_ge(res_ready, j)
                pe.matmul(y_ps[:, 0:D], s_at[:, 0:P], ws2_sb[:, 0, :], start=True, stop=False)
                pe.matmul(y_ps[:, 0:D], s_at[:, P:2 * P], ws2_sb[:, 1, :], start=False, stop=False)
                pe.matmul(y_ps[:, 0:D], ones_b[0:3, :], bias3[:, BS2_AT:BS2_AT + D], start=False,
                          stop=True).then_inc(sy_done, 1)

            for g in range(3):
                x_part(0, 0, g)
            gru_quad(0, 0)
            pe.wait_ge(gru_x, 16)
            gru_quad(0, 1)
            with pe.Fori(1, QUADS // 2 - 1) as k:
                gru_quad(k, 0)
                gru_quad(k, 1)
            gru_quad(QUADS // 2 - 1, 0)
            gru_quad(QUADS // 2 - 1, 1, last=True)
            o = 1
            pe.wait_ge(h_ready, 4 * QUADS)
            pe.transpose(t_ps[:, 0:P], h2[o][:, :, :], ident[:, :]).then_inc(hT_done, 1)
            pe.wait_ge(lg_read, QUADS - 1)
            logits(o)
            pe.wait_ge(s_act_ready, QUADS - 1)
            shared_up(o, 0)
            shared_up(o, 1)
            shared_bias()
            shared_turn(QUADS - 1)
            shared_down(QUADS - 1)

            pe.wait_ge(sl, 3)
            pe.matmul(rank_ps[:, 0:QUADS * E], before[:, :], hot_any[:, :, :], start=True, stop=False,
                      skip_group_check=True)
            for j in range(QUADS):
                n = QUADS - j
                mm = pe.matmul(rank_ps[:, (j + 1) * E:(QUADS + 1) * E].rearrange("q (n e) -> q n e", e=E), ones_b[:, :],
                               hot_any[:, j:j + 1, :].to_broadcast([P, n, E]), start=False, stop=(j == QUADS - 1),
                               skip_group_check=True)
            mm.then_inc(rank_done, 1)
            pe.wait_ge(wsum_ready, 2)
            pe.matmul(y_ps[:, 256:258], ones_f[:, :], w_abs[:, :], start=True, stop=True).then_inc(wsum_done, 1)

            pe.wait_ge(exp_in, 32)
            pe.wait_ge(eid_ready, 1)

            def turn_in(k, p):
                i = 2 * k + p
                pe.wait_ge(xg_in[p], 16 * (k + 1))
                if valid(i, 1):
                    pe.wait_ge(xg_t_ready, i)
                pe.transpose(ex_ps[:, 0:P], xg[p][:, :], ident[:, :]).then_inc(xgT_done, 1)

            def expert(k, p):
                i = 2 * k + p
                if valid(i + 1, 0, N_SLOT_TILES):
                    turn_in(k + p, 1 - p)
                if valid(i - 2, 0, N_SLOT_TILES):
                    pe.wait_ge(e_act_ready, i - 1)
                    if valid(i - 3, 0, N_SLOT_TILES):
                        pe.wait_ge(e_at_ready, i - 2)
                    for c in range(3):
                        mm = pe.transpose(et_ps[:, c * P:(c + 1) * P], e_act[p][:, c * P:(c + 1) * P], ident[:, :])
                    mm.then_inc(eT_done, 1)
                if valid(i, 0, N_SLOT_TILES):
                    e = pe.value_load(eid[0:1, ds(i, 1)], min_val=0, max_val=E - 1)
                    pe.wait_ge(xg_t_ready, i + 1)
                    for half, ps in enumerate((eg_ps, ea_ps)):
                        at = (1 - half) * HR
                        pe.matmul(ps[p][:, 0:HR], xg_t[p][:, :], we1_sb[:, ds(e * (2 * HR) + at, HR)],
                                  start=True, stop=False)
                        mm = pe.matmul(ps[p][:, 0:HR], ones_b[0:3, :], bias3[:, ds(e * (2 * HR) + (B1_AT + at), HR)],
                                       start=False, stop=True)
                        mm.then_inc(up_done, 1)
                if valid(i - 2, 0, N_SLOT_TILES):
                    e = pe.value_load(eid[0:1, ds(i - 2, 1)], min_val=0, max_val=E - 1)
                    pe.wait_ge(e_at_ready, i - 1)
                    if valid(i - 3, 0, N_SLOT_TILES):
                        pe.wait_ge(e_y_ready, i - 2)
                    for c in range(3):
                        pe.matmul(ey_ps[:, 0:D], e_at[p][:, c * P:(c + 1) * P],
                                  we2_sb[:, ds(e * HR + c * D, D)], start=(c == 0), stop=False)
                    pe.matmul(ey_ps[:, 0:D], ones_b[0:3, :], bias3[:, ds(e * D + B2_AT, D)], start=False,
                              stop=True).then_inc(ey_done, 1)

            turn_in(0, 0)
            expert(0, 0)
            expert(0, 1)
            expert(1, 0)
            expert(1, 1)
            with pe.Fori(2, N_SLOT_TILES // 2 - 1) as k:
                expert(k, 0)
                expert(k, 1)
            for i in range(N_SLOT_TILES - 2, N_SLOT_TILES + 2):
                expert(i // 2, i % 2)

            pe.wait_ge(l1_in, 16 * 11)
            pe.wait_ge(h0_in, 32)
            pe.wait_ge(wq_ready, 2)

            def turn_x1(m):
                pe.wait_ge(x1_ready, 2 * m + 2)
                for p in range(2):
                    mm = pe.transpose(in_ps[:, x1t_at + p * P:x1t_at + (p + 1) * P], x1[:, p, :], ident[:, :])
                mm.then_inc(x1T_done, 1)

            def rnn_x(p):
                pe.matmul(rx_ps[p][:, 0:P], wx_sb[:, :], x1_t[:, p, :], start=True, stop=False, skip_group_check=True)

            def turn_r(p):
                pe.transpose(rt_ps[:, p * P:(p + 1) * P], r_t[p][:, :, :], ident[:, :]).then_inc(rT_done, 1)

            def turn_q2(m, p):
                for c in range(4):
                    mm = pe.transpose(out_ps[:, q2t_at + c * P // 2:q2t_at + (c + 1) * P // 2].bitcast(BF16),
                                      q2[:, p, c * P:(c + 1) * P], ident_b[:, :])
                mm.then_inc(q2T_done, 1)

            def layer1(m):
                for p in range(2):
                    for s in range(QUAD):
                        t = 8 * m + 4 * p + s
                        if valid(m, 0, PAIRS):
                            if s > 0:
                                prev = r_t[p][:, s - 1, :]
                            elif p == 0 and isinstance(m, int) and m == 0:
                                prev = r_start[:, :]
                            else:
                                prev = r_t[1 - p][:, QUAD - 1, :]
                            if valid(m, 1, PAIRS) or t > 0:
                                pe.wait_ge(r_tanh, t)
                            pe.matmul(rx_ps[p][:, s * BATCH:(s + 1) * BATCH], rwh_sb[:, :], prev, start=False,
                                      stop=False, skip_group_check=True).then_inc(r_done, 1)
                        at = (p, s)
                        if at == (0, 0) and valid(m - 1, 0, PAIRS):
                            pe.wait_ge(r_tanh, 8 * m)
                            turn_r(1)
                        if at == (0, 1) and valid(m - 2, 0, PAIRS):
                            pe.wait_ge(q1_ready, m - 1)
                            for i in range(2):
                                mm = pe.transpose(in_ps[:, q1t_at + i * P // 2:q1t_at + (i + 1) * P // 2].bitcast(BF16),
                                                  q1[:, i, :], ident_b[:, :])
                            mm.then_inc(q1T_done, 1)
                        if at == (0, 2) and valid(m - 4, 0, PAIRS):
                            pe.wait_ge(q2_ready, 2 * m - 6)
                            if valid(m - 5, 0, PAIRS):
                                pe.wait_ge(o_ready, 2 * m - 8)
                            turn_q2(m - 4, 0)
                        if at == (0, 3) and valid(m - 2, 0, PAIRS):
                            pe.wait_ge(q1_t_ready, m - 1)
                            for i in range(2):
                                pe.matmul(m1_ps[i][:, :], q1_t[:, i, :], w1_q[:, :], start=True,
                                          stop=True).then_inc(m1_done, 1)
                        if at == (1, 0) and valid(m - 4, 0, PAIRS):
                            pe.wait_ge(q2_t_ready, 2 * m - 7)
                            turn_q2(m - 4, 1)
                        if at == (1, 1) and valid(m + 1, 0, PAIRS):
                            if valid(m - 2, 0, PAIRS):
                                pe.wait_ge(q1_t_ready, m - 1)
                            turn_x1(m + 1)
                        if at == (1, 2) and valid(m, 0, PAIRS):
                            if valid(m - 1, 0, PAIRS):
                                pe.wait_ge(n1_read, m)
                            pe.wait_ge(r_tanh, 8 * m + 4)
                            turn_r(0)
                        if at == (1, 3) and valid(m - 4, 0, PAIRS):
                            pe.wait_ge(q2_t_ready, 2 * m - 6)
                            for i in range(2):
                                for c in range(4):
                                    mm = pe.matmul(out_ps[:, m2_at + i * P:m2_at + (i + 1) * P],
                                                   q2_t[:, i, c * P:(c + 1) * P], w2_q[:, c * P:(c + 1) * P],
                                                   start=(c == 0), stop=(c == 3), skip_group_check=True)
                            mm.then_inc(m2_done, 1)
                if valid(m + 1, 0, PAIRS):
                    pe.wait_ge(x1_t_ready, m + 2)
                    pe.wait_ge(r_tanh, 8 * m + 8)
                    rnn_x(0)
                    rnn_x(1)

            turn_x1(0)
            pe.wait_ge(x1_t_ready, 1)
            rnn_x(0)
            rnn_x(1)
            for m in range(5):
                layer1(m)
            with pe.Fori(5, PAIRS - 1) as m:
                layer1(m)
            for m in range(PAIRS - 1, PAIRS + 4):
                layer1(m)

        @block.scalar
        def _(act):
            act.wait_ge(gru_in, 16 * 4)

            def gru_quad(k, p, last=False):
                q = 2 * k + p
                side = valid(q - 1)
                for s in range(QUAD):
                    act.wait_ge(r_gate, 4 * q + s + 1)
                    act.activation(g_r[:, :], r_ps[p][:, z_cols(s)], ACT.Tanh, scale=0.5 / W_SCALE).then_inc(r_tanhed, 1)
                    act.wait_ge(z_gate, 4 * q + s + 1)
                    act.activation(g_z[:, :], zc_ps[p][:, z_cols(s)], ACT.Tanh, scale=0.5 / W_SCALE).then_inc(z_tanhed, 1)
                    act.wait_ge(c_done, 4 * q + s + 1)
                    act.activation(g_c[:, :], zc_ps[p][:, c_cols(s)], ACT.Tanh, scale=1.0 / W_SCALE).then_inc(c_tanh, 1)
                    if s == 0 and side:
                        keep_h(q - 1)
                    if s == 1 and side:
                        shared_gelu(q - 1)
                    if s == 3 and side:
                        shared_copy(q - 1)
                if not last:
                    act.wait_ge(prop_done, q + 1)
                    act.activation(h_prev[:, :], zc_ps[p][:, prop_cols], ACT.Tanh, scale=1.0 / W_SCALE,
                                   bias=bp_sb[:, :]).then_inc(prop_tanh, 1)

            def keep_h(j):
                act.wait_ge(hT_done, j + 1)
                act.activation(h_tok[:, ds(j, 1), :].rearrange("q a n -> q (a n)"), t_ps[:, 0:P], ACT.Copy,
                               scale=0.5).then_inc(h_tok_ready, 1)

            def shared_gelu(j):
                act.wait_ge(sh_done, j + 1)
                act.activation(s_gl[:, :], a_ps[:, HS:2 * HS], ACT.Gelu).then_inc(s_gelu, 1)

            def shared_copy(j):
                act.wait_ge(sT_done, j + 1)
                act.activation(s_at[:, :], t_ps[:, 0:HS], ACT.Copy).then_inc(s_at_ready, 1)

            gru_quad(0, 0)
            gru_quad(0, 1)
            with act.Fori(1, QUADS // 2 - 1) as k:
                gru_quad(k, 0)
                gru_quad(k, 1)
            gru_quad(QUADS // 2 - 1, 0)
            gru_quad(QUADS // 2 - 1, 1, last=True)
            keep_h(QUADS - 1)
            shared_gelu(QUADS - 1)
            shared_copy(QUADS - 1)
            act.wait_ge(sl, 4)
            act.activation(th[:, :], v_gap[:, :], ACT.Tanh, scale=0.5).then_inc(th_ready, 1)

            def copy_in(i, p):
                act.wait_ge(xgT_done, i + 1)
                act.activation(xg_t[p][:, :], ex_ps[:, 0:P], ACT.Copy).then_inc(xg_t_ready, 1)

            def expert(k, p):
                i = 2 * k + p
                if valid(i + 1, 0, N_SLOT_TILES):
                    if valid(i - 1, 0, N_SLOT_TILES):
                        act.wait_ge(up_done, 2 * i)
                    copy_in(i + 1, 1 - p)
                if valid(i - 2, 0, N_SLOT_TILES):
                    act.wait_ge(eT_done, i - 1)
                    if valid(i - 4, 0, N_SLOT_TILES):
                        act.wait_ge(ey_done, i - 3)
                    act.activation(e_at[p][:, :], et_ps[:, 0:HR], ACT.Copy).then_inc(e_at_ready, 1)
                if valid(i, 0, N_SLOT_TILES):
                    act.wait_ge(up_done, 2 * i + 1)
                    act.activation(e_gl[p][:, :], eg_ps[p][:, 0:HR], ACT.Gelu).then_inc(e_gelu, 1)

            copy_in(0, 0)
            for i in range(4):
                expert(i // 2, i % 2)
            with act.Fori(2, N_SLOT_TILES // 2 - 1) as k:
                expert(k, 0)
                expert(k, 1)
            for i in range(N_SLOT_TILES - 2, N_SLOT_TILES + 2):
                expert(i // 2, i % 2)

            act.wait_ge(l1_in, 16 * 11)

            def copy_x1(m):
                act.wait_ge(x1T_done, m + 1)
                act.activation(x1_t[:, :, :], in_ps[:, x1t_at:x1t_at + 2 * P].rearrange("q (a n) -> q a n", a=2),
                               ACT.Copy).then_inc(x1_t_ready, 1)

            def copy_q2(m, p):
                act.wait_ge(q2T_done, 2 * m + p + 1)
                act.activation(q2_t[:, p, :], out_ps[:, q2t_at:q2t_at + HID // 2].bitcast(BF16),
                               ACT.Copy).then_inc(q2_t_ready, 1)

            def scale_m1(m, p):
                act.wait_ge(m1_done, 2 * m + p + 1)
                act.activation(hid[:, p, :], m1_ps[p][:, :], ACT.Copy, scale=dq[:, p:p + 1]).then_inc(m1_scaled, 1)

            def gelu(m, p):
                act.wait_ge(hid_ready, 2 * m + p + 1)
                if p == 0 and valid(m - 1, 0, PAIRS):
                    act.wait_ge(n2_read, m)
                act.activation(gel[:, p, :], hid[:, p, :], ACT.Gelu).then_inc(gel_ready, 1)

            def layer1(m):
                for p in range(2):
                    for s in range(QUAD):
                        t = 8 * m + 4 * p + s
                        if valid(m, 0, PAIRS):
                            act.wait_ge(r_done, t + 1)
                            if s == 0 and valid(m - 1, 0, PAIRS):
                                act.wait_ge(rT_done, 2 * m - 1 + p)
                            act.activation(r_t[p][:, s, :], rx_ps[p][:, s * BATCH:(s + 1) * BATCH], ACT.Tanh,
                                           bias=rb_sb[:, :]).then_inc(r_tanh, 1)
                        at = (p, s)
                        if at == (0, 1) and valid(m - 2, 0, PAIRS):
                            act.wait_ge(q1T_done, m - 1)
                            act.activation(q1_t[:, :, :],
                                           in_ps[:, q1t_at:q1t_at + P].bitcast(BF16).rearrange("q (a n) -> q a n", a=2),
                                           ACT.Copy).then_inc(q1_t_ready, 1)
                        if at == (0, 2) and valid(m - 4, 0, PAIRS):
                            copy_q2(m - 4, 0)
                        if at == (0, 3) and valid(m - 2, 0, PAIRS):
                            scale_m1(m - 2, 0)
                        if at == (1, 0) and valid(m - 2, 0, PAIRS):
                            scale_m1(m - 2, 1)
                        if at == (1, 1) and valid(m - 4, 0, PAIRS):
                            copy_q2(m - 4, 1)
                        if at == (1, 2) and valid(m + 1, 0, PAIRS):
                            copy_x1(m + 1)
                if valid(m - 2, 0, PAIRS):
                    gelu(m - 2, 0)
                    gelu(m - 2, 1)
                if valid(m - 3, 0, PAIRS):
                    for p in range(2):
                        act.wait_ge(qm2_ready, 2 * m - 5 + p)
                        act.activation(q2[:, p, :], n2[:, p, :], ACT.Copy, bias=-MAGIC).then_inc(q2_ready, 1)

            copy_x1(0)
            for m in range(5):
                layer1(m)
            with act.Fori(5, PAIRS - 1) as m:
                layer1(m)
            for m in range(PAIRS - 1, PAIRS + 4):
                layer1(m)

        @block.vector
        def _(dve):
            dve.wait_ge(bias_loaded, 16)
            dve.tensor_copy(bias_p[:, 0, :], bias_in[:, :]).then_inc(bias_split, 1)
            dve.wait_ge(bias_split, 1)
            dve.tensor_tensor(bias_r[:, 0, :], bias_in[:, :], bias_p[:, 0, :], ALU.subtract).then_inc(bias_chain, 1)
            dve.wait_ge(bias_chain, 1)
            dve.tensor_copy(bias_p[:, 1, :], bias_r[:, 0, :]).then_inc(bias_split, 1)
            dve.wait_ge(bias_split, 2)
            dve.tensor_tensor(bias_r[:, 1, :], bias_r[:, 0, :], bias_p[:, 1, :], ALU.subtract).then_inc(bias_chain, 1)
            dve.wait_ge(bias_chain, 2)
            dve.tensor_copy(bias_p[:, 2, :], bias_r[:, 1, :]).then_inc(bias_split, 1)
            dve.memset(mv[:, :, :], 1.0).then_inc(mv_init, 1)
            dve.memset(amax[:, :], 1.0).then_inc(mv_init, 1)
            dve.wait_ge(gru_in, 16 * 4)
            for w, part, c in ((g_w[:, 1, :, :], slice(0, 3), 0.5), (wp_sb[:, :].unsqueeze(1), slice(3, 4), 0.5)):
                dve.tensor_scalar(w_new[:, 0, part, :], w, c * W_SCALE, None, ALU.mult).then_inc(w_split, 1)
            dve.tensor_scalar(w_prod[:, 0, :], g_w[:, 1, 2, :], 0.25 * W_SCALE, None, ALU.mult).then_inc(w_split, 1)
            dve.wait_ge(w_split, 3)
            for w, part, c in ((g_w[:, 1, :, :], slice(0, 3), 0.5), (wp_sb[:, :].unsqueeze(1), slice(3, 4), 0.5)):
                dve.scalar_tensor_tensor(w_new[:, 1, part, :], w, c * W_SCALE, w_new[:, 0, part, :], ALU.mult,
                                         ALU.subtract).then_inc(w_split, 1)
            dve.scalar_tensor_tensor(w_prod[:, 1, :], g_w[:, 1, 2, :], 0.25 * W_SCALE, w_prod[:, 0, :], ALU.mult,
                                     ALU.subtract).then_inc(w_split, 1)
            dve.wait_ge(w_split, 6)
            dve.tensor_scalar(w_kept[:, :, :, :], w_new[:, :, :, :], -0.5, None, ALU.mult).then_inc(w_split, 1)

            def gru_quad(k, p):
                q = 2 * k + p
                side = valid(q - 1)
                for s in range(QUAD):
                    t = 4 * q + s
                    n = 3 * t
                    if s == 0:
                        dve.wait_ge(prop_tanh, q)
                        dve.wait_ge(h_ready, t)
                        dve.tensor_scalar(h_prev_p[:, 0, :], h_prev[:, :], 2.0, None, ALU.mult).then_inc(hp_ready, 1)
                        dve.tensor_scalar(h_prev2[:, :], h_prev[:, :], 2.0, None, ALU.mult).then_inc(hp_ready, 1)
                        dve.wait_ge(hp_ready, 3 * q + 2)
                        dve.tensor_tensor(h_prev_p[:, 1, :], h_prev2[:, :], h_prev_p[:, 0, :], ALU.subtract)\
                           .then_inc(hp_ready, 1)
                    prev = h_prev2[:, :] if s == 0 else h2[p][:, s - 1, :]
                    dve.wait_ge(r_tanhed, t + 1)
                    if s > 0:
                        dve.wait_ge(h_ready, t)
                    dve.scalar_tensor_tensor(g_rh_p[:, 0, :], g_r[:, :], 1.0, prev, ALU.add, ALU.mult).then_inc(rh_ready, 1)
                    dve.scalar_tensor_tensor(g_rh[:, :], g_r[:, :], 1.0, prev, ALU.add, ALU.mult).then_inc(rh_ready, 1)
                    dve.wait_ge(rh_ready, n + 2)
                    dve.tensor_tensor(g_rh_p[:, 1, :], g_rh[:, :], g_rh_p[:, 0, :], ALU.subtract).then_inc(rh_ready, 1)
                    dve.wait_ge(z_tanhed, t + 1)
                    dve.scalar_tensor_tensor(g_na_p[:, 0, :], g_z[:, :], 1.0, prev, ALU.subtract, ALU.mult)\
                       .then_inc(na_ready, 1)
                    dve.scalar_tensor_tensor(g_na[:, :], g_z[:, :], 1.0, prev, ALU.subtract, ALU.mult).then_inc(na_ready, 1)
                    dve.wait_ge(na_ready, n + 2)
                    dve.tensor_tensor(g_na_p[:, 1, :], g_na[:, :], g_na_p[:, 0, :], ALU.subtract).then_inc(na_ready, 1)
                    if s == 1 and side:
                        router(q - 1, 1 - p, 0)
                    dve.wait_ge(c_tanh, t + 1)
                    dve.scalar_tensor_tensor(g_e_p[:, 0, :], g_z[:, :], 1.0, g_c[:, :], ALU.add, ALU.mult).then_inc(e_ready, 1)
                    dve.scalar_tensor_tensor(g_e[:, :], g_z[:, :], 1.0, g_c[:, :], ALU.add, ALU.mult).then_inc(e_ready, 1)
                    dve.wait_ge(e_ready, n + 2)
                    dve.tensor_tensor(g_e_p[:, 1, :], g_e[:, :], g_e_p[:, 0, :], ALU.subtract).then_inc(e_ready, 1)
                    if s == 0 and valid(q - 2):
                        dve.wait_ge(sh_done, q - 1)
                        dve.wait_ge(lg_done, q - 1)
                        dve.wait_ge(hT_done, q - 1)
                    dve.scalar_tensor_tensor(h2[p][:, s, :], g_na[:, :], -0.5, g_e[:, :],
                                             ALU.mult, ALU.add).then_inc(h_ready, 1)
                    if s == 1 and side:
                        router(q - 1, 1 - p, 1)
                    if s == 2 and side:
                        shared_act(q - 1)
                    if s == 0 and valid(q - 2):
                        add_shared(q - 2)

            def router(j, p, part):
                n = ROUTER_STEPS * j
                if part == 0:
                    dve.wait_ge(lg_done, j + 1)
                    dve.tensor_scalar(lg[p][:, :], l_ps[:, 0:E], 1.0 / TAU, None, ALU.mult).then_inc(lg_read, 1)
                    dve.wait_ge(lg_read, j + 1)
                    dve.tensor_copy(touched[:, 0:1], lg[p][:, 0:1])
                    dve.max(top[p][:, :], lg[p][:, :]).then_inc(rt, 1)
                else:
                    dve.wait_ge(rt, n + 1)
                    dve.tensor_copy(top_v[:, ds(j, 1), :].rearrange("q a n -> q (a n)"), top[p][:, 0:2])
                    dve.max_index(tix[p][:, :], top[p][:, :], lg[p][:, :]).then_inc(rt, 1)
                    dve.wait_ge(rt, n + 2)
                    dve.tensor_copy(top_i[:, ds(j, 1), :].rearrange("q a n -> q (a n)"), tix[p][:, 0:2]).then_inc(rt, 1)

            def shared_act(j):
                dve.wait_ge(s_gelu, j + 1)
                if valid(j, 1):
                    dve.wait_ge(sT_done, j)
                dve.tensor_tensor(s_act[:, :], a_ps[:, 0:HS], s_gl[:, :], ALU.mult).then_inc(s_act_ready, 1)

            def add_shared(j):
                dve.wait_ge(sy_done, j + 1)
                r = res[:, ds(j, 1), :].rearrange("q a n -> q (a n)")
                dve.tensor_tensor(r, r, y_ps[:, 0:D], ALU.add).then_inc(res_ready, 1)

            dve.wait_ge(ffn_in, 16 * 4)
            dve.wait_ge(h0_in, 32)
            gru_quad(0, 0)
            gru_quad(0, 1)
            with dve.Fori(1, QUADS // 2) as k:
                gru_quad(k, 0)
                gru_quad(k, 1)
            add_shared(QUADS - 2)
            router(QUADS - 1, 1, 0)
            router(QUADS - 1, 1, 1)
            shared_act(QUADS - 1)
            add_shared(QUADS - 1)

            dve.wait_ge(consts, 10)
            dve.wait_ge(rt, ROUTER_STEPS * QUADS)
            for k in range(2):
                dve.tensor_tensor(hot[:, k, :, :], iota_e[:, :].unsqueeze(1).to_broadcast([P, QUADS, E]),
                                  top_i[:, :, k:k + 1].to_broadcast([P, QUADS, E]), ALU.is_equal).then_inc(sl, 1)
            dve.wait_ge(sl, 2)
            dve.tensor_tensor(hot_any[:, :, :], hot[:, 0, :, :], hot[:, 1, :, :], ALU.add).then_inc(sl, 1)
            dve.tensor_tensor(v_gap[:, :], top_v[:, :, 0], top_v[:, :, 1], ALU.subtract).then_inc(sl, 1)
            dve.wait_ge(rank_done, 1)
            dve.tensor_scalar(cnt[:, 0, :], rank_ps[:, QUADS * E:(QUADS + 1) * E], 1.0 / P, 0.5 - 0.5 / P,
                              ALU.mult, ALU.add).then_inc(sl, 1)
            dve.wait_ge(sl, 5)
            dve.tensor_scalar(cnt[:, 1, :], cnt[:, 0, :], MAGIC, None, ALU.add).then_inc(sl, 1)
            dve.wait_ge(sl, 6)
            dve.tensor_scalar(cnt[:, 2, :], cnt[:, 1, :], MAGIC, None, ALU.subtract).then_inc(sl, 1)
            dve.wait_ge(sl, 7)
            dve.tensor_tensor_scan(ends[:, :], ones_e[:, :], cnt[:, 2, :], 0.0, ALU.mult, ALU.add).then_inc(sl, 1)
            dve.wait_ge(sl, 8)
            dve.tensor_tensor(cnt[:, 3, :], ends[:, :], cnt[:, 2, :], ALU.subtract).then_inc(sl, 1)
            dve.wait_ge(sl, 9)
            dve.tensor_scalar(base[:, :], cnt[:, 3, :], float(P), None, ALU.mult).then_inc(sl, 1)
            dve.wait_ge(sl, 10)
            dve.tensor_tensor(where_e[:, :, :], rank_ps[:, 0:QUADS * E].rearrange("q (j e) -> q j e", e=E),
                              base[:, :].unsqueeze(1).to_broadcast([P, QUADS, E]), ALU.add).then_inc(sl, 1)
            dve.wait_ge(sl, 11)
            for k in range(2):
                dve.tensor_tensor(picked[:, k, :, :], hot[:, k, :, :], where_e[:, :, :], ALU.mult).then_inc(sl, 1)
            dve.wait_ge(sl, 13)
            dve.tensor_reduce(slot_f[:, :, :], picked[:, :, :, :], AX_X, ALU.add).then_inc(sl, 1)
            dve.wait_ge(sl, 14)
            dve.tensor_copy(slot[:, :, :], slot_f[:, :, :]).then_inc(slot_ready, 1)
            dve.tensor_tensor(past[:, :, :], ends[0:1, :].unsqueeze(1).to_broadcast([1, N_SLOT_TILES, E]),
                              iota_t[:, :].unsqueeze(2).to_broadcast([1, N_SLOT_TILES, E]), ALU.is_le).then_inc(sl, 1)
            dve.wait_ge(sl, 15)
            dve.tensor_reduce(eid_f[:, :], past[:, :, :], AX_X, ALU.add).then_inc(sl, 1)
            dve.wait_ge(sl, 16)
            dve.tensor_scalar(eid_m[:, :], eid_f[:, :], float(E - 1), None, ALU.min).then_inc(sl, 1)
            dve.wait_ge(sl, 17)
            dve.tensor_copy(eid[:, :], eid_m[:, :]).then_inc(eid_ready, 1)
            dve.wait_ge(th_ready, 1)
            dve.tensor_scalar(pick_w[:, 0, :], th[:, :], 0.5, 0.5, ALU.mult, ALU.add).then_inc(pw_ready, 1)
            dve.tensor_scalar(pick_w[:, 1, :], th[:, :], -0.5, 0.5, ALU.mult, ALU.add).then_inc(pw_ready, 1)

            dve.wait_ge(l1_in, 16 * 11)
            for n, w in enumerate((w1_raw, w2_raw)):
                dve.tensor_reduce(w_abs[:, n:n + 1], w[:, :], AX_X, ALU.add, apply_absolute_value=True)\
                   .then_inc(wsum_ready, 1)
            dve.wait_ge(wsum_done, 1)
            dve.tensor_scalar(w_mean[:, :], y_ps[:, 256:258], 1.0 / (D * HID), EPS, ALU.mult, ALU.max).then_inc(wq, 1)
            dve.wait_ge(wq, 1)
            dve.reciprocal(w_inv[:, :], w_mean[:, :]).then_inc(wq, 1)
            for n in range(2):
                dve.tensor_scalar(step4[:, 2 * n:2 * n + 2], w_mean[:, n:n + 1].to_broadcast([P, 2]), 1.0 / 127.0, None,
                                  ALU.mult).then_inc(wq, 1)
            for n, (w, wq_out) in enumerate(((w1_raw, w1_q), (w2_raw, w2_q))):
                dve.wait_ge(wq, 4 + 2 * n)
                dve.tensor_scalar(wq_tmp[:, 0, :], w[:, :], w_inv[:, n:n + 1], MAGIC, ALU.mult, ALU.add).then_inc(wq, 1)
                dve.wait_ge(wq, 5 + 2 * n)
                dve.tensor_scalar(wq_tmp[:, 1, :], wq_tmp[:, 0, :], MAGIC + 1.0, MAGIC - 1.0, ALU.min, ALU.max)\
                   .then_inc(wq, 1)
                dve.wait_ge(wq, 6 + 2 * n)
                dve.tensor_scalar(wq_out[:, :], wq_tmp[:, 1, :], MAGIC, None, ALU.subtract).then_inc(wq_ready, 1)

            def expert(k, p):
                i = 2 * k + p
                if valid(i, 0, N_SLOT_TILES):
                    dve.wait_ge(e_gelu, i + 1)
                    dve.wait_ge(up_done, 2 * i + 2)
                    if valid(i - 2, 0, N_SLOT_TILES):
                        dve.wait_ge(eT_done, i - 1)
                    dve.tensor_tensor(e_act[p][:, :], ea_ps[p][:, 0:HR], e_gl[p][:, :], ALU.mult).then_inc(e_act_ready, 1)
                if valid(i - 2, 0, N_SLOT_TILES):
                    dve.wait_ge(ey_done, i - 1)
                    if valid(i - 4, 0, N_SLOT_TILES):
                        dve.wait_ge(e_y_out[p], 16 * (k - 1))
                    dve.tensor_copy(e_y[p][:, :], ey_ps[:, 0:D]).then_inc(e_y_ready, 1)

            for i in range(4):
                expert(i // 2, i % 2)
            with dve.Fori(2, N_SLOT_TILES // 2) as k:
                expert(k, 0)
                expert(k, 1)
            for i in range(N_SLOT_TILES, N_SLOT_TILES + 2):
                expert(i // 2, i % 2)

            dve.wait_ge(pw_ready, 2)
            dve.wait_ge(mv_init, 2)
            dve.wait_ge(res_ready, QUADS)

            def row(j):
                return res[:, ds(j, 1), :].rearrange("q a n -> q (a n)")

            def layer1(m, at):
                has_c, has_1, has_3, has_4 = (valid(m + i, 0, PAIRS) for i in (1, -1, -3, -4))
                done = [0]

                def sig(ins):
                    ins.then_inc(dv, 1)
                    done[0] += 1
                    return done[0]

                def after(n):
                    dve.wait_ge(dv, at + n)

                def summed(p):
                    if has_c:
                        if p == 0:
                            dve.wait_ge(gathered, 64 * (m + 2))
                        dve.scalar_tensor_tensor(y_sum[:, p, :], y_got[:, 0, p, :], pick_w[:, 0, ds(2 * (m + 1) + p, 1)],
                                                 row(2 * (m + 1) + p), ALU.mult, ALU.add)

                def combined(p):
                    if has_c:
                        if p == 0 and valid(m, 0, PAIRS):
                            dve.wait_ge(x1T_done, m + 1)
                            dve.wait_ge(x1_kept, m + 1)
                        dve.scalar_tensor_tensor(x1[:, p, :], y_got[:, 1, p, :], pick_w[:, 1, ds(2 * (m + 1) + p, 1)],
                                                 y_sum[:, p, :], ALU.mult, ALU.add).then_inc(x1_ready, 1)

                def centred1(p):
                    if has_1:
                        ins = dve.scalar_tensor_tensor(n1[:, p, :], rt_ps[:, p * P:(p + 1) * P], mv[:, p, 0:1],
                                                       ln1w_sb[:, :], ALU.subtract, ALU.mult)
                        if p == 1:
                            ins.then_inc(n1_read, 1)

                def centred2(p):
                    if has_3:
                        if p == 0 and valid(m - 4, 0, PAIRS):
                            dve.wait_ge(q2_ready, 2 * m - 6)
                        ins = dve.scalar_tensor_tensor(n2[:, p, :], gel[:, p, :], mv[:, 2 + p, 0:1], ln2w_sb[:, :],
                                                       ALU.subtract, ALU.mult)
                        if p == 1:
                            ins.then_inc(n2_read, 1)

                def result(p):
                    if has_4:
                        if p == 0:
                            dve.wait_ge(m2_done, m - 3)
                        if valid(m - 5, 0, PAIRS):
                            dve.wait_ge(o_out[p], 16 * (m - 4))
                        dve.scalar_tensor_tensor(o_sb[p][:, :], out_ps[:, m2_at + p * P:m2_at + (p + 1) * P],
                                                 dq[:, 2 + p:3 + p], row(2 * (m - 4) + p), ALU.mult,
                                                 ALU.add).then_inc(o_ready, 1)

                n = 0
                if has_1:
                    dve.wait_ge(rT_done, 2 * m)
                    for p in range(2):
                        n = sig(dve.bn_stats(stats[:, p, :], rt_ps[:, p * P:(p + 1) * P]))
                if has_3:
                    dve.wait_ge(gel_ready, 2 * m - 4)
                    for p in range(2):
                        n = sig(dve.bn_stats(stats[:, 2 + p, :], gel[:, p, :]))
                summed(0)
                if has_1 or has_3:
                    after(n)
                    sig(dve.tensor_copy(touched[:, 1:2], stats[:, 0, 0:1]))
                for i, has in ((0, has_1), (1, has_1), (2, has_3), (3, has_3)):
                    if has:
                        n = sig(dve.bn_aggr(mv[:, i, :], stats[:, i, :]))
                if has_1 or has_3:
                    summed(1)
                    after(n)
                    n = sig(dve.tensor_scalar(var_e[:, :], mv[:, :, 1], EPS, None, ALU.add))
                    centred1(0)
                    after(n)
                    n = sig(dve.tensor_scalar(half_bits[:, :], var_e[:, :].bitcast(I32), 1, None, ALU.logical_shift_right))
                    centred1(1)
                    after(n)
                    n = sig(dve.tensor_scalar(rsq[0][:, :].bitcast(I32), half_bits[:, :], -1.0, float(0x5F3759DF),
                                              ALU.mult, ALU.add))
                    wide = [lambda: combined(0), lambda: combined(1), lambda: centred2(0), lambda: centred2(1),
                            lambda: result(0), lambda: result(1)]
                    for i in range(3):
                        y = rsq[i][:, :]
                        after(n)
                        n = sig(dve.tensor_tensor(rsq_t[:, 0, :], y, y, ALU.mult))
                        wide[2 * i]()
                        after(n)
                        n = sig(dve.scalar_tensor_tensor(rsq_t[:, 1, :], rsq_t[:, 0, :], -0.5, var_e[:, :], ALU.mult,
                                                         ALU.mult))
                        wide[2 * i + 1]()
                        after(n)
                        n = sig(dve.scalar_tensor_tensor(rsq[i + 1][:, :], rsq_t[:, 1, :], 1.5, y, ALU.add, ALU.mult))
                    after(n)
                    for p in range(2):
                        if has_1:
                            n = sig(dve.scalar_tensor_tensor(ln1[:, p, :], n1[:, p, :], rsq[3][:, p:p + 1],
                                                             ln1b_sb[:, :], ALU.mult, ALU.add))
                    for p in range(2):
                        if has_3:
                            n = sig(dve.scalar_tensor_tensor(ln2[:, p, :], n2[:, p, :], rsq[3][:, 2 + p:3 + p],
                                                             ln2b_sb[:, :], ALU.mult, ALU.add))
                    after(n)
                    if has_1:
                        n = sig(dve.tensor_reduce(amax[:, 0:2], ln1[:, :, :], AX_X, ALU.max, apply_absolute_value=True))
                    if has_3:
                        n = sig(dve.tensor_reduce(amax[:, 2:4], ln2[:, :, :], AX_X, ALU.max, apply_absolute_value=True))
                    after(n)
                    n = sig(dve.tensor_scalar(amax_e[:, :], amax[:, :], EPS, None, ALU.max))
                    after(n)
                    n = sig(dve.reciprocal(inv[:, :], amax_e[:, :]))
                    if valid(m - 2, 0, PAIRS):
                        dve.wait_ge(m1_scaled, 2 * m - 2)
                    sig(dve.tensor_tensor(dq[:, :], amax_e[:, :], step4[:, :], ALU.mult))
                    after(n)
                    n = sig(dve.tensor_scalar(to_int[:, :], inv[:, :], 127.0, None, ALU.mult))
                    after(n)
                    if has_1 and valid(m - 2, 0, PAIRS):
                        dve.wait_ge(q1_ready, m - 1)
                    for p in range(2):
                        if has_1:
                            ins = dve.tensor_scalar(qm1[:, p, :], ln1[:, p, :], to_int[:, p:p + 1], MAGIC, ALU.mult,
                                                    ALU.add)
                            if p == 1:
                                ins.then_inc(qm1_ready, 1)
                    for p in range(2):
                        if has_3:
                            dve.tensor_scalar(n2[:, p, :], ln2[:, p, :], to_int[:, 2 + p:3 + p], MAGIC, ALU.mult,
                                              ALU.add).then_inc(qm2_ready, 1)
                else:
                    summed(1)
                    marker = dve.memset(touched[:, 0:1], 0.0)
                    n = sig(marker)
                    after(n)
                    combined(0)
                    combined(1)
                    result(0)
                    result(1)
                return done[0]

            at = 0
            for m in range(-1, 5):
                full = layer1(m, at)
                at += full
            with dve.Fori(5, PAIRS - 1) as m:
                layer1(m, at + (m - 5) * full)
            at += (PAIRS - 6) * full
            for m in range(PAIRS - 1, PAIRS + 4):
                at += layer1(m, at)




def kernel(**inputs):
    import numpy as np
    import concourse.bacc as bacc
    from concourse import mybir as _mybir
    from concourse.bass_utils import run_bass_kernel_spmd as run

    g = {n: np.asarray(a) for n, a in inputs.items()}
    x = g["x"]
    time_major = x.transpose(1, 0, 2).reshape(TOKENS, D)
    gates = np.stack([g["L0_cond_Wz"], g["L0_cond_Wr"], g["L0_cond_Wh"]])
    gates = gates.reshape(3, 2, P, P).transpose(2, 1, 0, 3).reshape(P, 6 * P)

    def split_rows(w, parts):
        return w.reshape(parts, P, w.shape[-1]).transpose(1, 0, 2).reshape(P, -1)

    laid = {
        "x_t": time_major.T,
        "x_tok": split_rows(time_major, QUADS),
        "h0_t": g["cond_1024"].T,
        "gru_w": gates,
        "gru_wp": g["L0_cond_Wp"],
        "gru_bp": g["L0_cond_bp"][:, None],
        "we1": g["L0_ffn_We1"].transpose(1, 0, 2).reshape(P, -1),
        "we2": g["L0_ffn_We2"].reshape(E, 3, P, D).transpose(2, 0, 1, 3).reshape(P, -1),
        "ws1": g["L0_ffn_Ws1"],
        "ws2": split_rows(g["L0_ffn_Ws2"], 2),
        "wr": g["L0_ffn_Wr"],
        "bias": np.concatenate([g["L0_ffn_be1"].ravel(), g["L0_ffn_be2"].ravel(), g["L0_ffn_bs1"],
                                g["L0_ffn_bs2"], np.pad(g["L0_ffn_br"], (0, P - E)), g["L0_cond_bz"],
                                g["L0_cond_br"], g["L0_cond_bh"]]).reshape(BIAS_ROWS, P),
        "rnn_wx": g["L1_cond_Wx"],
        "rnn_wh": g["L1_cond_Wh"],
        "rnn_b": g["L1_cond_b"][:, None],
        "w1_t": g["L1_ffn_w1"].T,
        "w2_t": split_rows(g["L1_ffn_w2"].T, 4),
        "ln1_w": g["L1_ffn_ln1_w"][None, :],
        "ln1_b": g["L1_ffn_ln1_b"][None, :],
        "b1": g["L1_ffn_b1"][None, :],
        "ln2_w": g["L1_ffn_ln2_w"][None, :],
        "ln2_b": g["L1_ffn_ln2_b"][None, :],
        "b2": g["L1_ffn_b2"][None, :],
    }
    nc = bacc.Bacc("TRN2", target_bir_lowering=False, num_devices=1)
    arrays, args = {}, []
    for name, a in laid.items():
        a = np.ascontiguousarray(a)
        arrays[f"in_{name}"] = a
        args.append(nc.dram_tensor(f"in_{name}", a.shape, _mybir.dt.from_np(a.dtype), kind="ExternalInput").ap())
    args.append(nc.dram_tensor("out_0", (TOKENS, D), F32, kind="ExternalOutput").ap())
    build(nc, *args)
    r = run(nc, [arrays], core_ids=[0])
    got = r.results[0]["out_0"]
    return got.reshape(STEPS, BATCH, D).transpose(1, 0, 2)
```

```python
from contextlib import ExitStack

import concourse.bass as bass
from concourse import mybir

F32 = mybir.dt.float32
BF16 = mybir.dt.bfloat16
F16 = mybir.dt.float16
I32 = mybir.dt.int32
U32 = mybir.dt.uint32
ALU = mybir.AluOpType
ACT = mybir.ActivationFunctionType
AX_X = mybir.AxisListType.X

P = 128
BATCH, STEPS, D = 32, 128, 128
TOKENS = BATCH * STEPS
QUAD = 4
QUADS = STEPS // QUAD
PAIRS = QUADS // 2
E = 12
HS, HR = 2 * D, 3 * D
TAU = 1.5
HID = 512
EPS = 1e-5
MAGIC = 12582912.0
N_SLOT_TILES = 2 * TOKENS // P + E - 1
N_TABLE = N_SLOT_TILES + -N_SLOT_TILES % 4
REGION = TOKENS + P
N_ROWS = E * REGION + P
B1_AT, B2_AT = 0, E * 2 * HR
BS1_AT = B2_AT + E * D
BS2_AT = BS1_AT + 2 * HS
BR_AT = BS2_AT + D
BG_AT = BR_AT + P
N_BIAS = BG_AT + 3 * P
BIAS_ROWS = N_BIAS // P
W_SCALE = 64.0
ds = bass.ds


def valid(q, lo=0, hi=QUADS):
    return lo <= q < hi if isinstance(q, int) else True


def build(nc, x_t, x_tok, h0_t, gru_w, gru_wp, gru_bp, we1, we2, ws1, ws2, wr, bias,
          rnn_wx, rnn_wh, rnn_b, w1_t, w2_t, ln1_w, ln1_b, b1, ln2_w, ln2_b, b2, out):
    with ExitStack() as ctx:
        def sb(name, shape, dt=F32):
            return ctx.enter_context(nc.sbuf_tensor(name, shape, dt))

        def sem(name):
            return ctx.enter_context(nc.semaphore(name))

        bank = [ctx.enter_context(nc.psum_tensor(f"bank{i}", [P, 512], F32)) for i in range(8)]

        slots_in = nc.dram_tensor("slots_in", (N_ROWS, D), F32, kind="Internal").ap()
        slots_out = nc.dram_tensor("slots_out", (N_SLOT_TILES * P, D), F32, kind="Internal").ap()

        ident = sb("ident", [P, P])
        ident_b = sb("ident_b", [P, P], BF16)
        ones_b = sb("ones_b", [P, P], BF16)
        ones_f = sb("ones_f", [P, P])
        before = sb("before", [P, P], BF16)
        iota_e = sb("iota_e", [P, E])
        iota_t = sb("iota_t", [1, N_TABLE])
        zeros = sb("zeros", [P, D])
        g_w = sb("g_w", [P, 2, 3, P])
        gx = sb("gx", [P, 3, P])
        w_new = sb("w_new", [P, 2, 4, P], F16)
        w_kept = sb("w_kept", [P, 2, 4, P], F16)
        w_prod = sb("w_prod", [P, 2, P], F16)
        scale_row = sb("scale_row", [3, P], BF16)
        wp_sb = sb("wp_sb", [P, P])
        bp_sb = sb("bp_sb", [P, 1])
        we1_sb = sb("we1_sb", [P, E * 2 * HR])
        we1_p = we1_sb[:, :].bitcast(F16)
        we2_sb = sb("we2_sb", [P, E * HR])
        ws1_sb = sb("ws1_sb", [P, 2 * HS])
        ws2_sb = sb("ws2_sb", [P, 2, D])
        wr_sb = sb("wr_sb", [P, E])
        bias_in = sb("bias_in", [BIAS_ROWS, P])
        bias_r = sb("bias_r", [BIAS_ROWS, 2, P])
        bias_p = sb("bias_p", [BIAS_ROWS, 3, P], BF16)
        bias3 = sb("bias3", [3, N_BIAS], BF16)
        wx_sb = sb("wx_sb", [P, P])
        rwh_sb = sb("rwh_sb", [P, P])
        rb_sb = sb("rb_sb", [P, 1])
        w1_raw = sb("w1_raw", [P, HID])
        w2_raw = sb("w2_raw", [P, HID])
        w1_q = sb("w1_q", [P, HID], BF16)
        w2_q = sb("w2_q", [P, HID], BF16)
        w_abs = sb("w_abs", [P, 2])
        w_mean = sb("w_mean", [P, 2])
        w_inv = sb("w_inv", [P, 2])
        ln1w_sb = sb("ln1w_sb", [P, D])
        ln1b_sb = sb("ln1b_sb", [P, D])
        b1_sb = sb("b1_sb", [P, HID])
        ln2w_sb = sb("ln2w_sb", [P, HID])
        ln2b_sb = sb("ln2b_sb", [P, HID])
        b2_sb = sb("b2_sb", [P, D])

        xt_sb = sb("xt_sb", [P, TOKENS])
        res = sb("res", [P, QUADS, D])
        h_tok = sb("h_tok", [P, QUADS, D])

        h_prev = sb("h_prev", [P, BATCH])
        h_prev2 = sb("h_prev2", [P, BATCH])
        h_prev_p = sb("h_prev_p", [P, 2, BATCH], F16)
        g_r = sb("g_r", [P, BATCH])
        g_z = sb("g_z", [P, BATCH])
        g_rh = sb("g_rh", [P, BATCH])
        g_rh_p = sb("g_rh_p", [P, 2, BATCH], F16)
        g_na = sb("g_na", [P, BATCH])
        g_na_p = sb("g_na_p", [P, 2, BATCH], F16)
        g_c = sb("g_c", [P, BATCH])
        g_e = sb("g_e", [P, BATCH])
        g_e_p = sb("g_e_p", [P, 2, BATCH], F16)
        h2 = [sb(f"h2_{p}", [P, QUAD, BATCH]) for p in range(2)]

        lg = [sb(f"lg{p}", [P, E]) for p in range(2)]
        top = [sb(f"top{p}", [P, 8]) for p in range(2)]
        tix = [sb(f"tix{p}", [P, 8], U32) for p in range(2)]
        top_v = sb("top_v", [P, QUADS, 2])
        top_i = sb("top_i", [P, QUADS, 2])
        s_gl = sb("s_gl", [P, HS])
        s_act = sb("s_act", [P, HS])
        s_at = sb("s_at", [P, HS])

        region_at = sb("region_at", [P, E])
        acc = sb("acc", [P, E], BF16)
        hot_q = sb("hot_q", [P, 2, E])
        any_q = sb("any_q", [P, E], BF16)
        where_q = sb("where_q", [P, E])
        pick12 = sb("pick12", [P, 2, E])
        pick6 = sb("pick6", [P, 2, E // 2])
        pick3 = sb("pick3", [P, 2, E // 4])
        pick1 = sb("pick1", [P, 2, 1])
        sent_f = sb("sent_f", [P, 2, QUADS])
        sent = sb("sent", [P, 2, QUADS], U32)
        hot = sb("hot", [P, 2, QUADS, E], BF16)
        cnt = sb("cnt", [P, 4, E])
        ones_e = sb("ones_e", [P, E])
        ends = sb("ends", [P, E])
        tail_f = sb("tail_f", [1, E])
        tail = sb("tail", [1, E], I32)
        spare = sb("spare", [1, E])
        shift = sb("shift", [P, E])
        picked = sb("picked", [P, 2, QUADS, E])
        shift_f = sb("shift_f", [P, 2, QUADS])
        slot_f = sb("slot_f", [P, 2, QUADS])
        slot = sb("slot", [P, 2, QUADS], U32)
        past = sb("past", [1, N_TABLE, E])
        past_spare = sb("past_spare", [1, N_TABLE, E])
        eid_f = sb("eid_f", [1, N_TABLE])
        eid_m = sb("eid_m", [1, N_TABLE])
        eid = sb("eid", [1, N_TABLE], I32)
        start_s = sb("start_s", [1, N_TABLE])
        start_f = sb("start_f", [1, N_TABLE])
        start_m = sb("start_m", [1, N_TABLE])
        start_row = sb("start_row", [1, N_TABLE], I32)
        v_gap = sb("v_gap", [P, QUADS])
        th = sb("th", [P, QUADS])
        pick_w = sb("pick_w", [P, 2, QUADS])

        xg = [sb(f"xg{p}", [P, D]) for p in range(2)]
        xg_t = [sb(f"xg_t{p}", [P, 2, P], F16) for p in range(2)]
        e_gl = [sb(f"e_gl{p}", [P, HR]) for p in range(2)]
        e_act = [sb(f"e_act{p}", [P, HR]) for p in range(2)]
        e_at = [sb(f"e_at{p}", [P, HR]) for p in range(2)]
        e_y = [sb(f"e_y{p}", [P, D]) for p in range(2)]

        w_stage, w_scl = e_gl, e_act

        late = [xt_sb[:, i * 2 * HID:(i + 1) * 2 * HID].rearrange("q (a n) -> q a n", a=2) for i in range(4)]
        hid, gel, n2, ln2 = late
        wq_tmp = gel

        y_got = we1_sb[:, 0:2 * QUADS * D].rearrange("q (k j n) -> q k j n", k=2, j=QUADS)
        y_sum = sb("y_sum", [P, 2, D])
        x1 = sb("x1", [P, 2, D])
        x1_t = sb("x1_t", [P, 2, P])
        r_t = [sb(f"r_t{p}", [P, QUAD, BATCH]) for p in range(2)]
        r_start = sb("r_start", [P, BATCH])
        touched = sb("touched", [P, 2])
        stats = sb("stats", [P, 4, 6])
        mv = sb("mv", [P, 4, 2])
        var_e = sb("var_e", [P, 4])
        half_bits = sb("half_bits", [P, 4], I32)
        guess = sb("guess", [P, 4])
        better = sb("better", [P, 4])
        rsq = sb("rsq", [P, 4])
        rsq_t = sb("rsq_t", [P, 5, 4])
        amax = sb("amax", [P, 4])
        amax_e = sb("amax_e", [P, 4])
        inv = sb("inv", [P, 4])
        to_int = sb("to_int", [P, 4])
        step4 = sb("step4", [P, 4])
        dq = sb("dq", [P, 4])
        dq_out = sb("dq_out", [P, 2])
        n1 = sb("n1", [P, 2, D])
        ln1 = sb("ln1", [P, 2, D])
        qm1 = sb("qm1", [P, 2, D])
        q1 = sb("q1", [P, 2, D], BF16)
        q1_t = sb("q1_t", [P, 2, P], BF16)
        q2 = sb("q2", [P, 2, HID], BF16)
        q2_t = sb("q2_t", [P, 2, HID], BF16)
        o_sb = [sb(f"o_sb{p}", [P, D]) for p in range(2)]

        gru_in = sem("gru_in")
        gru_x = sem("gru_x")
        ffn_in = sem("ffn_in")
        res_in = sem("res_in")
        exp_in = sem("exp_in")
        w1_in = [sem(f"w1_in{p}") for p in range(2)]
        w1_split = sem("w1_split")
        l1_in = sem("l1_in")
        bias_loaded = sem("bias_loaded")
        bias_moved = sem("bias_moved")
        consts = sem("consts")
        consts_c = sem("consts_c")
        zeroed = sem("zeroed")
        hot_ready = sem("hot_ready")
        any_ready = sem("any_ready")
        acc_ready = sem("acc_ready")
        rank_ready = sem("rank_ready")
        picks = sem("picks")
        tail_ready = sem("tail_ready")
        start_ready = sem("start_ready")
        w_scaled = sem("w_scaled")
        bias_chain = sem("bias_chain")
        bias_split = sem("bias_split")
        h0_in = sem("h0_in")
        w_split = sem("w_split")
        hp_ready = sem("hp_ready")
        r_gate = sem("r_gate")
        z_gate = sem("z_gate")
        r_tanhed = sem("r_tanhed")
        z_tanhed = sem("z_tanhed")
        rh_ready = sem("rh_ready")
        na_ready = sem("na_ready")
        c_done = sem("c_done")
        c_tanh = sem("c_tanh")
        e_ready = sem("e_ready")
        h_ready = sem("h_ready")
        prop_done = sem("prop_done")
        prop_tanh = sem("prop_tanh")
        hT_done = sem("hT_done")
        h_tok_ready = sem("h_tok_ready")
        lg_done = sem("lg_done")
        lg_read = sem("lg_read")
        rt = sem("rt")
        sh_done = sem("sh_done")
        s_gelu = sem("s_gelu")
        s_act_ready = sem("s_act_ready")
        sT_done = sem("sT_done")
        s_at_ready = sem("s_at_ready")
        sy_done = sem("sy_done")
        res_ready = sem("res_ready")
        sl = sem("sl")
        gap_ready = sem("gap_ready")
        th_ready = sem("th_ready")
        count_done = sem("count_done")
        rank_done = sem("rank_done")
        eid_ready = sem("eid_ready")
        slot_ready = sem("slot_ready")
        pw_ready = sem("pw_ready")
        scattered = sem("scattered")
        xg_in = [sem(f"xg_in{p}") for p in range(2)]
        xgT_done = sem("xgT_done")
        xg_hi_ready = sem("xg_hi_ready")
        xg_t_ready = sem("xg_t_ready")
        up_done = sem("up_done")
        e_gelu = sem("e_gelu")
        e_act_ready = sem("e_act_ready")
        eT_done = sem("eT_done")
        e_at_ready = sem("e_at_ready")
        ey_done = sem("ey_done")
        e_y_ready = sem("e_y_ready")
        e_y_out = [sem(f"e_y_out{p}") for p in range(2)]
        gathered = sem("gathered")
        x1_ready = sem("x1_ready")
        x1_kept = sem("x1_kept")
        x1T_done = sem("x1T_done")
        x1_t_ready = sem("x1_t_ready")
        r_done = sem("r_done")
        r_tanh = sem("r_tanh")
        rT_done = sem("rT_done")
        dv = sem("dv")
        mv_init = sem("mv_init")
        n1_read = sem("n1_read")
        n2_read = sem("n2_read")
        qm1_ready = sem("qm1_ready")
        q1_ready = sem("q1_ready")
        q1T_done = sem("q1T_done")
        q1_t_ready = sem("q1_t_ready")
        m1_done = sem("m1_done")
        m1_scaled = sem("m1_scaled")
        hid_ready = sem("hid_ready")
        gel_ready = sem("gel_ready")
        qm2_ready = sem("qm2_ready")
        q2_ready = sem("q2_ready")
        q2T_done = sem("q2T_done")
        q2_t_ready = sem("q2_t_ready")
        m2_done = sem("m2_done")
        to_int_ready = sem("to_int_ready")
        dq_ready = sem("dq_ready")
        o_ready = sem("o_ready")
        o_out = [sem(f"o_out{p}") for p in range(2)]
        wq = sem("wq")
        wsum_ready = sem("wsum_ready")
        wsum_done = sem("wsum_done")
        wq_ready = sem("wq_ready")

        ROUTER_STEPS = 3
        W_CHUNKS = 2 * E
        PICK_STEPS = 6

        r_ps, zc_ps = bank[0:2], bank[2:4]
        t_ps, a_ps, y_ps, l_ps = bank[4], bank[5], bank[6], bank[7]
        ea_ps, eg_ps = bank[0:2], bank[2:4]
        ex_ps, et_ps, ey_ps = bank[4], bank[5], bank[6:8]
        rank_at = D
        count_at, wsum_at = 2 * E, 3 * E
        rx_ps = bank[0:2]
        in_ps, rt_ps, m1_ps, m2_ps, q2t_ps = bank[2], bank[3], bank[4:6], bank[6], bank[7]
        x1t_at, q1t_at = 0, 2 * P

        def z_cols(s):
            return slice(s * BATCH, (s + 1) * BATCH)

        def c_cols(s):
            return slice(P + s * BATCH, P + (s + 1) * BATCH)

        prop_cols = slice(2 * P, 2 * P + BATCH)

        block = ctx.enter_context(nc.Block())

        def zero_tails(eng, lo, hi):
            tails = [eng.alloc_register(f"tail{e}") for e in range(lo, hi)]
            eng.wait_ge(tail_ready, 1)
            eng.load(tails, tail[0:1, lo:hi])
            for e in range(lo, hi):
                row = eng.snap(tails[e - lo], min_val=e * REGION, max_val=e * REGION + TOKENS)
                eng.dma_start(slots_in[ds(row, P), :], zeros[:, :]).then_inc(zeroed, 16)

        @block.sync
        def _(sp):
            first = 4 * P
            sp.dma_start(g_w[:, :, :, :], gru_w.rearrange("k (i g n) -> k i g n", i=2, g=3)).then_inc(gru_in, 16)
            sp.dma_start(xt_sb[:, 0:first], x_t[:, 0:first]).then_inc(gru_in, 16)
            sp.dma_start(bias_in[:, :], bias).then_inc(bias_loaded, 16)
            sp.dma_start(wp_sb[:, :], gru_wp).then_inc(gru_in, 16)
            sp.dma_start(bp_sb[:, :], gru_bp).then_inc(gru_in, 16)
            sp.dma_start(h_prev[:, :], h0_t).then_inc(h0_in, 16)
            sp.dma_start(r_start[:, :], h0_t).then_inc(h0_in, 16)
            sp.dma_start(ws1_sb[:, :], ws1).then_inc(ffn_in, 16)
            sp.dma_start(ws2_sb[:, :, :], ws2.rearrange("k (c n) -> k c n", c=2)).then_inc(ffn_in, 16)
            sp.dma_start(wr_sb[:, :], wr).then_inc(ffn_in, 16)
            sp.wait_ge(bias_split, 3)
            for part in range(3):
                sp.dma_start(bias3[part:part + 1, :].rearrange("a (r n) -> a r n", n=P),
                             bias_p[:, part, :]).then_inc(bias_moved, 16)
            sp.dma_start(xt_sb[:, first:TOKENS], x_t[:, first:TOKENS]).then_inc(gru_x, 16)
            sp.dma_start(res[:, :, :], x_tok.rearrange("q (i n) -> q i n", i=QUADS)).then_inc(res_in, 16)
            sp.dma_start(we2_sb[:, :], we2).then_inc(exp_in, 16)
            for dst, src in ((wx_sb, rnn_wx), (rwh_sb, rnn_wh), (rb_sb, rnn_b), (w1_raw, w1_t), (w2_raw, w2_t)):
                sp.dma_start(dst[:, :], src).then_inc(l1_in, 16)
            for dst, src in ((ln1w_sb, ln1_w), (ln1b_sb, ln1_b), (b1_sb, b1), (ln2w_sb, ln2_w),
                             (ln2b_sb, ln2_b), (b2_sb, b2)):
                sp.dma_start(dst[:, :], src.to_broadcast([P, src.shape[1]])).then_inc(l1_in, 16)
            for c in range(W_CHUNKS):
                if c >= 2:
                    sp.wait_ge(w1_split, 3 * (c - 1))
                sp.dma_start(w_stage[c % 2][:, :], we1[:, c * HR:(c + 1) * HR]).then_inc(w1_in[c % 2], 16)
            sp.wait_ge(consts, 7)
            sp.dma_start(slots_in[E * REGION:N_ROWS, :], zeros[:, :]).then_inc(zeroed, 16)
            zero_tails(sp, 0, E // 2)

            def start_of(i):
                return sp.value_load(start_row[0:1, ds(i, 1)], min_val=0, max_val=E * REGION)

            def load_slots(row, p):
                sp.dma_start(xg[p][:, :], slots_in[ds(row, P), :]).then_inc(xg_in[p], 16)

            sp.wait_ge(start_ready, 1)
            first_rows = [start_of(p) for p in range(2)]
            sp.wait_ge(scattered, 16 * 2 * QUADS)
            sp.wait_ge(zeroed, 16 * (E + 1))
            for p in range(2):
                load_slots(first_rows[p], p)

            def expert_io(k, p):
                i = 2 * k + p
                if valid(i + 2, 0, N_SLOT_TILES):
                    sp.wait_ge(xgT_done, i + 1)
                    load_slots(start_of(i + 2), p)
                if valid(i - 3, 0, N_SLOT_TILES):
                    sp.wait_ge(e_y_ready, i - 2)
                    sp.dma_start(slots_out[ds((i - 3) * P, P), :], e_y[1 - p][:, :]).then_inc(e_y_out[1 - p], 16)

            for i in range(4):
                expert_io(i // 2, i % 2)
            with sp.Fori(2, N_SLOT_TILES // 2 - 1) as k:
                expert_io(k, 0)
                expert_io(k, 1)
            for i in range(N_SLOT_TILES // 2 * 2 - 2, N_SLOT_TILES + 3):
                expert_io(i // 2, i % 2)

            def store(k, p):
                i = 2 * k + p
                sp.wait_ge(o_ready, i + 1)
                sp.dma_start(out[ds(i * P, P), :], o_sb[p][:, :]).then_inc(o_out[p], 16)

            with sp.Fori(0, QUADS // 2) as k:
                store(k, 0)
                store(k, 1)
            for p in range(2):
                sp.wait_ge(o_out[p], 16 * (QUADS // 2))

        @block.gpsimd
        def _(pool):
            pool.memset(ident[:, :], 0.0).then_inc(consts_c, 1)
            pool.memset(ident_b[:, :], 0.0).then_inc(consts_c, 1)
            pool.memset(before[:, :], 0.0).then_inc(consts_c, 1)
            pool.memset(ones_f[:, :], 1.0).then_inc(consts, 1)
            pool.memset(ones_b[:, :], 1.0).then_inc(consts, 1)
            pool.memset(zeros[:, :], 0.0).then_inc(consts, 1)
            pool.memset(ones_e[:, :], 1.0).then_inc(consts, 1)
            pool.wait_ge(consts_c, 3)
            for m in (ident, ident_b):
                pool.affine_select(out=m[:, :], in_=m[:, :], compare_op=ALU.not_equal, fill=1.0, base=0,
                                   pattern=[[-1, P]], channel_multiplier=1).then_inc(consts, 1)
            pool.affine_select(out=before[:, :], in_=before[:, :], compare_op=ALU.is_ge, fill=1.0, base=0,
                               pattern=[[-1, P]], channel_multiplier=1).then_inc(consts, 1)
            pool.memset(scale_row[:, :], W_SCALE).then_inc(consts, 1)
            pool.wait_ge(gru_in, 16 * 4)
            pool.tensor_scalar(gx[:, :, :], g_w[:, 0, :, :], W_SCALE, None, ALU.mult).then_inc(w_scaled, 1)
            pool.iota(iota_e[:, :], [[1, E]], base=0, channel_multiplier=0,
                      allow_small_or_imprecise_dtypes=True).then_inc(consts, 1)
            pool.iota(iota_t[:, :], [[1, N_TABLE]], base=0, channel_multiplier=0,
                      allow_small_or_imprecise_dtypes=True).then_inc(consts, 1)
            pool.iota(region_at[:, :], [[REGION, E]], base=0, channel_multiplier=0,
                      allow_small_or_imprecise_dtypes=True).then_inc(consts, 1)
            pool.memset(acc[:, :], 0.0).then_inc(acc_ready, 1)
            pool.wait_ge(ffn_in, 16 * 3)
            pool.tensor_scalar(ws1_sb[:, :], ws1_sb[:, :], 0.5, None, ALU.mult).then_inc(w_scaled, 1)
            pool.tensor_scalar(wr_sb[:, :], wr_sb[:, :], 0.5, None, ALU.mult).then_inc(w_scaled, 1)

            def experts_of(j):
                pool.wait_ge(rt, ROUTER_STEPS * j + 2)
                for k in range(2):
                    pool.tensor_scalar(hot_q[:, k, :], iota_e[:, :], tix[j % 2][:, k:k + 1], None,
                                       ALU.is_equal).then_inc(hot_ready, 1)
                pool.wait_ge(hot_ready, 2 * j + 2)
                pool.tensor_tensor(any_q[:, :], hot_q[:, 0, :], hot_q[:, 1, :], ALU.add).then_inc(any_ready, 1)

            def rows_of(j):
                n = PICK_STEPS * j
                pool.wait_ge(rank_ready, j + 1)
                pool.tensor_tensor(pick12[:, :, :], hot_q[:, :, :],
                                   where_q[:, :].unsqueeze(1).to_broadcast([P, 2, E]), ALU.mult).then_inc(picks, 1)
                if j < QUADS - 1:
                    pool.tensor_tensor(acc[:, :], acc[:, :], any_q[:, :], ALU.add).then_inc(acc_ready, 1)
                pool.wait_ge(picks, n + 1)
                pool.tensor_tensor(pick6[:, :, :], pick12[:, :, 0:6], pick12[:, :, 6:12], ALU.add).then_inc(picks, 1)
                pool.wait_ge(picks, n + 2)
                pool.tensor_tensor(pick3[:, :, :], pick6[:, :, 0:3], pick6[:, :, 3:6], ALU.add).then_inc(picks, 1)
                pool.wait_ge(picks, n + 3)
                pool.tensor_tensor(pick1[:, :, :], pick3[:, :, 0:1], pick3[:, :, 1:2], ALU.add).then_inc(picks, 1)
                pool.wait_ge(picks, n + 4)
                pool.tensor_tensor(sent_f[:, :, j:j + 1], pick1[:, :, :], pick3[:, :, 2:3], ALU.add).then_inc(picks, 1)
                pool.wait_ge(picks, n + 5)
                pool.tensor_scalar(sent[:, :, j:j + 1], sent_f[:, :, j:j + 1], 1.0, 0.0, ALU.mult,
                                   ALU.add).then_inc(picks, 1)

            def send(j):
                pool.wait_ge(picks, PICK_STEPS * (j + 1))
                pool.wait_ge(h_tok_ready, j + 1)
                for k in range(2):
                    pool.indirect_dma_start(
                        out=slots_in, out_offset=bass.IndirectOffsetOnAxis(ap=sent[:, k, j:j + 1], axis=0),
                        in_=h_tok[:, j, :], in_offset=None).then_inc(scattered, 16)

            def split_weights(c):
                hi, lo = (we1_p[:, (2 * c + part) * HR:(2 * c + part + 1) * HR] for part in range(2))
                pool.wait_ge(w1_in[c % 2], 16 * (c // 2 + 1))
                pool.tensor_scalar(hi, w_stage[c % 2][:, :], W_SCALE, 1.0, ALU.mult, ALU.mult).then_inc(w1_split, 1)
                if c >= 2:
                    pool.wait_ge(w1_split, 3 * (c - 1))
                pool.tensor_scalar(w_scl[c % 2][:, :], w_stage[c % 2][:, :], W_SCALE, 1.0, ALU.mult,
                                   ALU.mult).then_inc(w1_split, 1)
                pool.wait_ge(w1_split, 3 * c + 2)
                pool.tensor_tensor(lo, w_scl[c % 2][:, :], hi, ALU.subtract).then_inc(w1_split, 1)

            experts_of(0)
            for j in range(QUADS):
                rows_of(j)
                if j + 1 < QUADS:
                    experts_of(j + 1)
                send(j)
                if j < W_CHUNKS:
                    split_weights(j)
            pool.wait_ge(slot_ready, 1)
            for p in range(2):
                pool.wait_ge(e_y_out[p], 16 * ((N_SLOT_TILES + 1 - p) // 2))
            def collect(m, k):
                if m > 0 and k == 0:
                    pool.wait_ge(gathered, 64 * m)
                for p in range(2):
                    pool.indirect_dma_start(
                        out=y_got[:, k, 2 * m + p, :], out_offset=None, in_=slots_out,
                        in_offset=bass.IndirectOffsetOnAxis(ap=slot[:, k, 2 * m + p:2 * m + p + 1], axis=0))\
                        .then_inc(gathered, 16)

            for m in range(2):
                for k in range(2):
                    collect(m, k)
            pool.wait_ge(l1_in, 16 * 11)
            for m in range(-1, PAIRS + 2):
                if 2 <= m < PAIRS - 3:
                    collect(m + 3, 0)
                if m + 1 < PAIRS:
                    pool.wait_ge(x1_ready, 2 * (m + 2))
                    pool.tensor_tensor(res[:, 2 * (m + 1):2 * (m + 2), :], x1[:, :, :],
                                       b2_sb[:, :].unsqueeze(1).to_broadcast([P, 2, D]), ALU.add).then_inc(x1_kept, 1)
                if m < 2:
                    collect(m + 3, 0)
                if 0 <= m - 2 < PAIRS:
                    for p in range(2):
                        pool.wait_ge(m1_scaled, 2 * (m - 2) + p + 1)
                        pool.tensor_tensor(hid[:, p, :], hid[:, p, :], b1_sb[:, :], ALU.add).then_inc(hid_ready, 1)
                if m + 3 < PAIRS:
                    collect(m + 3, 1)
                if 0 <= m - 1 < PAIRS:
                    pool.wait_ge(qm1_ready, 2 * m)
                    if m >= 2:
                        pool.wait_ge(q1T_done, m - 1)
                    pool.tensor_scalar(q1[:, :, :], qm1[:, :, :], -MAGIC, 1.0, ALU.add, ALU.mult).then_inc(q1_ready, 1)

        @block.tensor
        def _(pe):
            pe.wait_ge(consts, 11)
            pe.wait_ge(gru_in, 16 * 4)
            pe.wait_ge(w_scaled, 1)
            pe.wait_ge(w_split, 7)
            pe.wait_ge(bias_moved, 48)

            def steps_of(ps, lo):
                return ps[:, lo:lo + P].rearrange("q (s b) -> q s b", s=QUAD)

            def gate_input(p, g):
                ps, lo = ((zc_ps[p], 0), (r_ps[p], 0), (zc_ps[p], P))[g]
                return ps[:, lo:lo + P]

            def x_product(q, p, g):
                pe.matmul(gate_input(p, g), gx[:, g, :], xt_sb[:, ds(q * P, P)],
                          start=(g != 2), stop=False, skip_group_check=True)

            def x_bias(p, g):
                pe.matmul(gate_input(p, g), bias3[:, BG_AT + g * P:BG_AT + (g + 1) * P], scale_row[:, :],
                          start=False, stop=False, skip_group_check=True)

            def x_part(q, p, g):
                x_product(q, p, g)
                x_bias(p, g)

            def add(dst, w, v):
                return pe.matmul(dst, w, v, start=False, stop=False, skip_group_check=True)

            def add_high(dst, w, g, v):
                add(dst, w[:, 0, g, :], v[:, 0, :])
                add(dst, w[:, 1, g, :], v[:, 0, :])

            def shared_up(p, part):
                at = slice(part * HS // 2, (part + 1) * HS // 2)
                return pe.matmul(a_ps[:, at], h2[p][:, :, :], ws1_sb[:, at], start=(part == 0), stop=False,
                                 skip_group_check=True)

            def turn_h(p):
                pe.transpose(t_ps[:, 0:P], h2[p][:, :, :], ident[:, :]).then_inc(hT_done, 1)

            def logits(p):
                pe.matmul(l_ps[:, 0:E], h2[p][:, :, :], wr_sb[:, :], start=True, stop=False)
                pe.matmul(l_ps[:, 0:E], ones_b[0:3, :], bias3[:, BR_AT:BR_AT + E], start=False,
                          stop=True).then_inc(lg_done, 1)

            def shared_bias(half):
                add(a_ps[:, half * HS:(half + 1) * HS], ones_b[0:3, :],
                    bias3[:, BS1_AT + half * HS:BS1_AT + (half + 1) * HS])

            def gru_quad(k, p, last=False):
                q = 2 * k + p
                side = valid(q - 1)
                o = 1 - p
                for s in range(QUAD):
                    n = 3 * (4 * q + s)
                    z_at, r_at = zc_ps[p][:, z_cols(s)], r_ps[p][:, 0:P][:, z_cols(s)]
                    c_at = zc_ps[p][:, c_cols(s)]
                    if s == 0:
                        pe.wait_ge(hp_ready, 3 * q + 1)
                        add_high(r_at, w_new, 1, h_prev_p)
                        add_high(z_at, w_new, 0, h_prev_p)
                        pe.wait_ge(hp_ready, 3 * q + 3)
                        add(r_at, w_new[:, 0, 1, :], h_prev_p[:, 1, :]).then_inc(r_gate, 1)
                        add(z_at, w_new[:, 0, 0, :], h_prev_p[:, 1, :]).then_inc(z_gate, 1)
                    else:
                        pe.wait_ge(e_ready, n - 2)
                        add_high(r_at, w_new, 1, g_e_p)
                        add_high(z_at, w_new, 0, g_e_p)
                        pe.wait_ge(e_ready, n)
                        add(r_at, w_new[:, 0, 1, :], g_e_p[:, 1, :]).then_inc(r_gate, 1)
                        add(z_at, w_new[:, 0, 0, :], g_e_p[:, 1, :]).then_inc(z_gate, 1)
                    if s == 0 and valid(q - 2):
                        shared_down(q - 2)
                    if s == 1 and side:
                        shared_up(o, 1)
                        shared_bias(0)
                    if s == 2 and side:
                        shared_up(o, 3).then_inc(sh_done, 1)
                    if s == 2 and valid(q + 1):
                        x_bias(o, 1)
                    if s == 3 and valid(q + 1):
                        x_part(q + 1, o, 2)
                    pe.wait_ge(z_tanhed, 4 * q + s + 1)
                    pe.wait_ge(rh_ready, n + 1)
                    add(c_at, w_prod[:, 0, :], g_rh_p[:, 0, :])
                    add(c_at, w_prod[:, 1, :], g_rh_p[:, 0, :])
                    pe.wait_ge(rh_ready, n + 3)
                    add(c_at, w_prod[:, 0, :], g_rh_p[:, 1, :]).then_inc(c_done, 1)
                    if s == 0 and side:
                        shared_up(o, 0)
                    if s == 0 and valid(q + 1):
                        x_product(q + 1, o, 1)
                    if s == 1 and side:
                        shared_up(o, 2)
                        shared_bias(1)
                    if s == 2 and valid(q + 1):
                        x_part(q + 1, o, 0)
                    if s == 3 and side:
                        if valid(q - 2):
                            pe.wait_ge(rank_ready, q - 1)
                        ranks(q - 1)
                        down_bias()
                        shared_turn(q - 1)
                    if s == QUAD - 1 and last:
                        continue
                    pe.wait_ge(c_tanh, 4 * q + s + 1)
                    pe.wait_ge(na_ready, n + 3)
                    if s < QUAD - 1:
                        for g, at in ((1, r_ps[p][:, z_cols(s + 1)]), (0, zc_ps[p][:, z_cols(s + 1)])):
                            add_high(at, w_kept, g, g_na_p)
                            add(at, w_kept[:, 0, g, :], g_na_p[:, 1, :])
                    else:
                        at = zc_ps[p][:, prop_cols]
                        add_high(at, w_kept, 3, g_na_p)
                        add(at, w_kept[:, 0, 3, :], g_na_p[:, 1, :])
                        pe.wait_ge(e_ready, n + 1)
                        add_high(at, w_new, 3, g_e_p)
                        pe.wait_ge(e_ready, n + 3)
                        add(at, w_new[:, 0, 3, :], g_e_p[:, 1, :]).then_inc(prop_done, 1)
                        pe.wait_ge(h_ready, 4 * q + 4)
                        if not side:
                            pe.wait_ge(ffn_in, 16 * 3)
                            pe.wait_ge(w_scaled, 3)
                        if side:
                            pe.wait_ge(lg_read, q)
                        logits(p)
                        if side:
                            pe.wait_ge(s_at_ready, q)
                        turn_h(p)

            def shared_turn(j):
                pe.wait_ge(s_act_ready, j + 1)
                pe.wait_ge(h_tok_ready, j + 1)
                pe.transpose(t_ps[:, 0:P], s_act[:, 0:P], ident[:, :])
                pe.transpose(t_ps[:, P:2 * P], s_act[:, P:2 * P], ident[:, :]).then_inc(sT_done, 1)

            def ranks(j):
                pe.wait_ge(any_ready, j + 1)
                at = y_ps[:, rank_at:rank_at + E]
                pe.matmul(at, before[:, :], any_q[:, :], start=True, stop=False, skip_group_check=True)
                return pe.matmul(at, ones_b[:, :], acc[:, :], start=False, stop=True, skip_group_check=True)

            def down_bias():
                pe.matmul(y_ps[:, 0:D], ones_b[0:3, :], bias3[:, BS2_AT:BS2_AT + D], start=True, stop=False,
                          skip_group_check=True)

            def shared_down(j):
                pe.wait_ge(s_at_ready, j + 1)
                add(y_ps[:, 0:D], s_at[:, 0:P], ws2_sb[:, 0, :])
                add(y_ps[:, 0:D], s_at[:, P:2 * P], ws2_sb[:, 1, :]).then_inc(sy_done, 1)

            for g in range(3):
                x_part(0, 0, g)
            gru_quad(0, 0)
            pe.wait_ge(gru_x, 16)
            gru_quad(0, 1)
            with pe.Fori(1, QUADS // 2 - 1) as k:
                gru_quad(k, 0)
                gru_quad(k, 1)
            gru_quad(QUADS // 2 - 1, 0)
            gru_quad(QUADS // 2 - 1, 1, last=True)
            o = 1
            pe.wait_ge(h_ready, 4 * QUADS)
            pe.wait_ge(lg_read, QUADS - 1)
            logits(o)
            shared_down(QUADS - 2)
            turn_h(o)
            pe.wait_ge(s_act_ready, QUADS - 1)
            shared_up(o, 0)
            shared_bias(0)
            shared_bias(1)
            for part in range(1, 4):
                mm = shared_up(o, part)
            mm.then_inc(sh_done, 1)
            pe.wait_ge(wsum_ready, 2)
            pe.matmul(l_ps[:, wsum_at:wsum_at + 2], ones_f[:, :], w_abs[:, :], start=True, stop=True)\
              .then_inc(wsum_done, 1)
            pe.wait_ge(rank_ready, QUADS - 1)
            ranks(QUADS - 1).then_inc(rank_done, 1)
            pe.matmul(l_ps[:, count_at:count_at + E], ones_b[:, :], any_q[:, :], start=True, stop=False)
            pe.matmul(l_ps[:, count_at:count_at + E], ones_b[:, :], acc[:, :], start=False,
                      stop=True).then_inc(count_done, 1)
            shared_turn(QUADS - 1)
            pe.wait_ge(rank_ready, QUADS)
            down_bias()
            shared_down(QUADS - 1)

            pe.wait_ge(exp_in, 16)
            pe.wait_ge(w1_split, 3 * W_CHUNKS)
            pe.wait_ge(eid_ready, 1)

            e_regs = [[pe.alloc_register(f"expert{n}_{p}") for p in range(2)] for n in range(2)]

            def load_experts(n, i):
                pe.load(e_regs[n], eid[0:1, ds(i, 2)])

            def expert_of(n, p):
                return pe.snap(e_regs[n][p], min_val=0, max_val=E - 1)

            def turn_in(i, p):
                pe.wait_ge(xg_in[p], 16 * (i // 2 + 1) if isinstance(i, int) else 8 * (i - p) + 16)
                pe.transpose(ex_ps[:, 0:P], xg[p][:, :], ident[:, :]).then_inc(xgT_done, 1)

            def expert(i, p, n):
                if valid(i - 2, 0, N_SLOT_TILES):
                    pe.wait_ge(e_act_ready, i - 1)
                    for c in range(3):
                        mm = pe.transpose(et_ps[:, c * P:(c + 1) * P], e_act[p][:, c * P:(c + 1) * P], ident[:, :])
                        if c == 0 and valid(i - 4, 0, N_SLOT_TILES):
                            pe.wait_ge(e_y_ready, i - 3)
                        if c == 1 and valid(i, 0, N_SLOT_TILES):
                            pe.wait_ge(xg_t_ready, i + 1)
                    mm.then_inc(eT_done, 1)
                elif valid(i, 0, N_SLOT_TILES):
                    pe.wait_ge(xg_t_ready, i + 1)
                if valid(i + 1, 0, N_SLOT_TILES):
                    turn_in(i + 1, 1 - p)
                if valid(i, 0, N_SLOT_TILES):
                    e = expert_of(n, p)
                    for half, ps in enumerate((eg_ps, ea_ps)):
                        at = (1 - half) * HR
                        for x_part, w_part in ((0, 0), (1, 0), (0, 1)):
                            pe.matmul(ps[p][:, 0:HR], xg_t[p][:, x_part, :],
                                      we1_p[:, ds(e * (4 * HR) + (2 * at + w_part * HR), HR)],
                                      start=(x_part == 0 and w_part == 0), stop=False)
                        mm = pe.matmul(ps[p][:, 0:HR], scale_row[:, :], bias3[:, ds(e * (2 * HR) + (B1_AT + at), HR)],
                                       start=False, stop=True)
                        mm.then_inc(up_done, 1)
                if valid(i - 2, 0, N_SLOT_TILES):
                    e = expert_of(1 - n, p)
                    pe.wait_ge(e_at_ready, i - 1)
                    for c in range(3):
                        pe.matmul(ey_ps[p][:, 0:D], e_at[p][:, c * P:(c + 1) * P],
                                  we2_sb[:, ds(e * HR + c * D, D)], start=(c == 0), stop=False)
                    pe.matmul(ey_ps[p][:, 0:D], ones_b[0:3, :], bias3[:, ds(e * D + B2_AT, D)], start=False,
                              stop=True).then_inc(ey_done, 1)

            def four_experts(i):
                expert(i, 0, 0)
                expert(i + 1, 1, 0)
                if valid(i + 2, 0, N_SLOT_TILES):
                    load_experts(1, i + 2)
                    expert(i + 2, 0, 1)
                    expert(i + 3, 1, 1)
                if valid(i + 4, 0, N_SLOT_TILES):
                    load_experts(0, i + 4)

            load_experts(0, 0)
            turn_in(0, 0)
            four_experts(0)
            with pe.Fori(1, N_TABLE // 4 - 1) as k:
                four_experts(4 * k)
            four_experts(N_TABLE - 4)
            four_experts(N_TABLE)

            pe.wait_ge(l1_in, 16 * 11)
            pe.wait_ge(h0_in, 32)
            pe.wait_ge(wq_ready, 2)

            def turn_x1(m):
                pe.wait_ge(x1_ready, 2 * m + 2)
                for p in range(2):
                    mm = pe.transpose(in_ps[:, x1t_at + p * P:x1t_at + (p + 1) * P], x1[:, p, :], ident[:, :])
                mm.then_inc(x1T_done, 1)

            def rnn_x(p):
                pe.matmul(rx_ps[p][:, 0:P], wx_sb[:, :], x1_t[:, p, :], start=True, stop=False, skip_group_check=True)

            def turn_r(p):
                pe.transpose(rt_ps[:, p * P:(p + 1) * P], r_t[p][:, :, :], ident[:, :]).then_inc(rT_done, 1)

            def turn_q2(m, p):
                for c in range(4):
                    lo = (4 * p + c) * P // 2
                    mm = pe.transpose(q2t_ps[:, lo:lo + P // 2].bitcast(BF16), q2[:, p, c * P:(c + 1) * P],
                                      ident_b[:, :])
                mm.then_inc(q2T_done, 1)

            def up(i):
                pe.matmul(m1_ps[i][:, :], q1_t[:, i, :], w1_q[:, :], start=True, stop=True).then_inc(m1_done, 1)

            def down(i):
                for c in range(4):
                    mm = pe.matmul(m2_ps[:, i * P:(i + 1) * P], q2_t[:, i, c * P:(c + 1) * P],
                                   w2_q[:, c * P:(c + 1) * P], start=(c == 0), stop=(c == 3), skip_group_check=True)
                mm.then_inc(m2_done, 1)

            def layer1(m):
                for p in range(2):
                    for s in range(QUAD):
                        t = 8 * m + 4 * p + s
                        if valid(m, 0, PAIRS):
                            if s > 0:
                                prev = r_t[p][:, s - 1, :]
                            elif p == 0 and isinstance(m, int) and m == 0:
                                prev = r_start[:, :]
                            else:
                                prev = r_t[1 - p][:, QUAD - 1, :]
                            if valid(m, 1, PAIRS) or t > 0:
                                pe.wait_ge(r_tanh, t)
                            pe.matmul(rx_ps[p][:, s * BATCH:(s + 1) * BATCH], rwh_sb[:, :], prev, start=False,
                                      stop=False, skip_group_check=True).then_inc(r_done, 1)
                        at = (p, s)
                        if at == (0, 0) and valid(m - 1, 0, PAIRS):
                            pe.wait_ge(r_tanh, 8 * m)
                            turn_r(1)
                        if at in ((0, 0), (0, 1)) and valid(m - 5, 0, PAIRS):
                            pe.wait_ge(q2_ready, 2 * m - 9 + s)
                            turn_q2(m - 5, s)
                        if at == (0, 2) and valid(m, 0, PAIRS):
                            rnn_x(1)
                        if at == (0, 3) and valid(m - 2, 0, PAIRS):
                            pe.wait_ge(q1_ready, m - 1)
                            for i in range(2):
                                mm = pe.transpose(in_ps[:, q1t_at + i * P // 2:q1t_at + (i + 1) * P // 2].bitcast(BF16),
                                                  q1[:, i, :], ident_b[:, :])
                            mm.then_inc(q1T_done, 1)
                        if at == (1, 1) and valid(m - 2, 0, PAIRS):
                            pe.wait_ge(q1_t_ready, m - 1)
                            up(0)
                        if at == (1, 1) and valid(m + 1, 0, PAIRS):
                            turn_x1(m + 1)
                        if at == (1, 2) and valid(m - 2, 0, PAIRS):
                            up(1)
                        if at == (1, 2) and valid(m, 0, PAIRS):
                            if valid(m - 1, 0, PAIRS):
                                pe.wait_ge(n1_read, m)
                            turn_r(0)
                        if at == (1, 3) and valid(m + 1, 0, PAIRS):
                            pe.wait_ge(x1_t_ready, m + 2)
                            rnn_x(0)
                        if at == (1, 3) and valid(m - 5, 0, PAIRS):
                            if valid(m - 6, 0, PAIRS):
                                pe.wait_ge(o_ready, 2 * m - 10)
                            pe.wait_ge(q2_t_ready, 2 * m - 8)
                            down(0)
                            down(1)

            turn_x1(0)
            pe.wait_ge(x1_t_ready, 1)
            rnn_x(0)
            for m in range(6):
                layer1(m)
            with pe.Fori(6, PAIRS - 1) as m:
                layer1(m)
            for m in range(PAIRS - 1, PAIRS + 5):
                layer1(m)

        @block.scalar
        def _(act):
            act.wait_ge(gru_in, 16 * 4)

            def gru_quad(k, p, last=False):
                q = 2 * k + p
                side = valid(q - 1)
                for s in range(QUAD):
                    act.wait_ge(r_gate, 4 * q + s + 1)
                    act.activation(g_r[:, :], r_ps[p][:, z_cols(s)], ACT.Tanh, scale=0.5 / W_SCALE).then_inc(r_tanhed, 1)
                    act.wait_ge(z_gate, 4 * q + s + 1)
                    act.activation(g_z[:, :], zc_ps[p][:, z_cols(s)], ACT.Tanh, scale=0.5 / W_SCALE).then_inc(z_tanhed, 1)
                    act.wait_ge(c_done, 4 * q + s + 1)
                    act.activation(g_c[:, :], zc_ps[p][:, c_cols(s)], ACT.Tanh, scale=1.0 / W_SCALE).then_inc(c_tanh, 1)
                    if s == 0 and side:
                        keep_h(q - 1)
                    if s == 2 and side:
                        shared_gelu(q - 1)
                    if s == 3 and side:
                        shared_copy(q - 1)
                if not last:
                    act.wait_ge(prop_done, q + 1)
                    act.activation(h_prev[:, :], zc_ps[p][:, prop_cols], ACT.Tanh, scale=1.0 / W_SCALE,
                                   bias=bp_sb[:, :]).then_inc(prop_tanh, 1)

            def keep_h(j):
                act.wait_ge(hT_done, j + 1)
                act.activation(h_tok[:, ds(j, 1), :].rearrange("q a n -> q (a n)"), t_ps[:, 0:P], ACT.Copy,
                               scale=0.5).then_inc(h_tok_ready, 1)

            def shared_gelu(j):
                act.wait_ge(sh_done, j + 1)
                act.activation(s_gl[:, :], a_ps[:, HS:2 * HS], ACT.Gelu).then_inc(s_gelu, 1)

            def shared_copy(j):
                act.wait_ge(sT_done, j + 1)
                act.activation(s_at[:, :], t_ps[:, 0:HS], ACT.Copy).then_inc(s_at_ready, 1)

            gru_quad(0, 0)
            gru_quad(0, 1)
            with act.Fori(1, QUADS // 2 - 1) as k:
                gru_quad(k, 0)
                gru_quad(k, 1)
            gru_quad(QUADS // 2 - 1, 0)
            gru_quad(QUADS // 2 - 1, 1, last=True)
            keep_h(QUADS - 1)
            shared_gelu(QUADS - 1)
            shared_copy(QUADS - 1)
            act.wait_ge(consts, 7)
            zero_tails(act, E // 2, E)
            act.wait_ge(gap_ready, 1)
            act.activation(th[:, :], v_gap[:, :], ACT.Tanh, scale=0.5).then_inc(th_ready, 1)

            def copy_in(i, p):
                act.wait_ge(xgT_done, i + 1)
                act.activation(xg_t[p][:, 0, :], ex_ps[:, 0:P], ACT.Copy).then_inc(xg_hi_ready, 1)

            def expert(k, p):
                i = 2 * k + p
                if valid(i - 2, 0, N_SLOT_TILES):
                    act.wait_ge(eT_done, i - 1)
                    if valid(i - 4, 0, N_SLOT_TILES):
                        act.wait_ge(ey_done, i - 3)
                    act.activation(e_at[p][:, :], et_ps[:, 0:HR], ACT.Copy).then_inc(e_at_ready, 1)
                if valid(i + 1, 0, N_SLOT_TILES):
                    if valid(i - 1, 0, N_SLOT_TILES):
                        act.wait_ge(up_done, 2 * i)
                    copy_in(i + 1, 1 - p)
                if valid(i, 0, N_SLOT_TILES):
                    act.wait_ge(up_done, 2 * i + 1)
                    act.activation(e_gl[p][:, :], eg_ps[p][:, 0:HR], ACT.Gelu,
                                   scale=1.0 / W_SCALE).then_inc(e_gelu, 1)

            copy_in(0, 0)
            for i in range(4):
                expert(i // 2, i % 2)
            with act.Fori(2, N_SLOT_TILES // 2) as k:
                expert(k, 0)
                expert(k, 1)
            for i in range(N_SLOT_TILES // 2 * 2, N_SLOT_TILES + 2):
                expert(i // 2, i % 2)

            act.wait_ge(l1_in, 16 * 11)

            def copy_x1(m):
                act.wait_ge(x1T_done, m + 1)
                act.activation(x1_t[:, :, :], in_ps[:, x1t_at:x1t_at + 2 * P].rearrange("q (a n) -> q a n", a=2),
                               ACT.Copy).then_inc(x1_t_ready, 1)

            def copy_q2(m, p):
                act.wait_ge(q2T_done, 2 * m + 2)
                act.activation(q2_t[:, p, :], q2t_ps[:, p * HID // 2:(p + 1) * HID // 2].bitcast(BF16),
                               ACT.Copy).then_inc(q2_t_ready, 1)

            def round1(m, p):
                act.wait_ge(to_int_ready, m + 1)
                if p == 0 and valid(m - 1, 0, PAIRS):
                    act.wait_ge(q1_ready, m)
                act.activation(qm1[:, p, :], ln1[:, p, :], ACT.Copy, bias=MAGIC,
                               scale=to_int[:, p:p + 1]).then_inc(qm1_ready, 1)

            def round2(m, p):
                act.wait_ge(to_int_ready, m + 3)
                act.activation(ln2[:, p, :], ln2[:, p, :], ACT.Copy, bias=MAGIC,
                               scale=to_int[:, 2 + p:3 + p]).then_inc(qm2_ready, 1)

            def integers2(m, p):
                act.wait_ge(qm2_ready, 2 * m + 1 + p)
                if p == 0 and valid(m - 1, 0, PAIRS):
                    act.wait_ge(q2T_done, 2 * m)
                act.activation(q2[:, p, :], ln2[:, p, :], ACT.Copy, bias=-MAGIC).then_inc(q2_ready, 1)

            def scale_m1(m, p):
                act.wait_ge(m1_done, 2 * m + p + 1)
                if p == 0:
                    act.wait_ge(dq_ready, m + 1)
                act.activation(hid[:, p, :], m1_ps[p][:, :], ACT.Copy, scale=dq[:, p:p + 1]).then_inc(m1_scaled, 1)

            def gelu(m, p):
                act.wait_ge(hid_ready, 2 * m + p + 1)
                if p == 0 and valid(m - 1, 0, PAIRS):
                    act.wait_ge(n2_read, m)
                act.activation(gel[:, p, :], hid[:, p, :], ACT.Gelu).then_inc(gel_ready, 1)

            def layer1(m):
                for p in range(2):
                    for s in range(QUAD):
                        t = 8 * m + 4 * p + s
                        if valid(m, 0, PAIRS):
                            act.wait_ge(r_done, t + 1)
                            if s == 0 and valid(m - 1, 0, PAIRS):
                                act.wait_ge(rT_done, 2 * m - 1 + p)
                            act.activation(r_t[p][:, s, :], rx_ps[p][:, s * BATCH:(s + 1) * BATCH], ACT.Tanh,
                                           bias=rb_sb[:, :]).then_inc(r_tanh, 1)
                        at = (p, s)
                        if at in ((0, 0), (0, 1)) and valid(m - 3, 0, PAIRS):
                            gelu(m - 3, s)
                        if at == (0, 3) and valid(m - 2, 0, PAIRS):
                            round1(m - 2, 0)
                            round1(m - 2, 1)
                        if at == (0, 3) and valid(m - 4, 0, PAIRS):
                            round2(m - 4, 0)
                            round2(m - 4, 1)
                        if at == (1, 0) and valid(m - 2, 0, PAIRS):
                            act.wait_ge(q1T_done, m - 1)
                            act.activation(q1_t[:, :, :],
                                           in_ps[:, q1t_at:q1t_at + P].bitcast(BF16).rearrange("q (a n) -> q a n", a=2),
                                           ACT.Copy).then_inc(q1_t_ready, 1)
                        if at in ((1, 0), (1, 1)) and valid(m - 5, 0, PAIRS):
                            copy_q2(m - 5, s)
                        if at == (1, 1) and valid(m - 2, 0, PAIRS):
                            scale_m1(m - 2, 0)
                        if at == (1, 2) and valid(m + 1, 0, PAIRS):
                            copy_x1(m + 1)
                        if at == (1, 2) and valid(m - 2, 0, PAIRS):
                            scale_m1(m - 2, 1)
                        if at == (1, 3) and valid(m - 4, 0, PAIRS):
                            integers2(m - 4, 0)
                            integers2(m - 4, 1)

            copy_x1(0)
            for m in range(6):
                layer1(m)
            with act.Fori(6, PAIRS - 1) as m:
                layer1(m)
            for m in range(PAIRS - 1, PAIRS + 5):
                layer1(m)

        @block.vector
        def _(dve):
            dve.wait_ge(bias_loaded, 16)
            dve.tensor_copy(bias_p[:, 0, :], bias_in[:, :]).then_inc(bias_split, 1)
            dve.wait_ge(bias_split, 1)
            dve.tensor_tensor(bias_r[:, 0, :], bias_in[:, :], bias_p[:, 0, :], ALU.subtract).then_inc(bias_chain, 1)
            dve.wait_ge(bias_chain, 1)
            dve.tensor_copy(bias_p[:, 1, :], bias_r[:, 0, :]).then_inc(bias_split, 1)
            dve.wait_ge(bias_split, 2)
            dve.tensor_tensor(bias_r[:, 1, :], bias_r[:, 0, :], bias_p[:, 1, :], ALU.subtract).then_inc(bias_chain, 1)
            dve.wait_ge(bias_chain, 2)
            dve.tensor_copy(bias_p[:, 2, :], bias_r[:, 1, :]).then_inc(bias_split, 1)
            dve.memset(mv[:, :, :], 1.0).then_inc(mv_init, 1)
            dve.memset(amax[:, :], 1.0).then_inc(mv_init, 1)
            dve.memset(dq[:, :], 0.0).then_inc(mv_init, 1)
            dve.wait_ge(gru_in, 16 * 4)
            for w, part, c in ((g_w[:, 1, :, :], slice(0, 3), 0.5), (wp_sb[:, :].unsqueeze(1), slice(3, 4), 0.5)):
                dve.tensor_scalar(w_new[:, 0, part, :], w, c * W_SCALE, None, ALU.mult).then_inc(w_split, 1)
            dve.tensor_scalar(w_prod[:, 0, :], g_w[:, 1, 2, :], 0.25 * W_SCALE, None, ALU.mult).then_inc(w_split, 1)
            dve.wait_ge(w_split, 3)
            for w, part, c in ((g_w[:, 1, :, :], slice(0, 3), 0.5), (wp_sb[:, :].unsqueeze(1), slice(3, 4), 0.5)):
                dve.scalar_tensor_tensor(w_new[:, 1, part, :], w, c * W_SCALE, w_new[:, 0, part, :], ALU.mult,
                                         ALU.subtract).then_inc(w_split, 1)
            dve.scalar_tensor_tensor(w_prod[:, 1, :], g_w[:, 1, 2, :], 0.25 * W_SCALE, w_prod[:, 0, :], ALU.mult,
                                     ALU.subtract).then_inc(w_split, 1)
            dve.wait_ge(w_split, 6)
            dve.tensor_scalar(w_kept[:, :, :, :], w_new[:, :, :, :], -0.5, None, ALU.mult).then_inc(w_split, 1)

            def gru_quad(k, p):
                q = 2 * k + p
                side = valid(q - 1)
                for s in range(QUAD):
                    t = 4 * q + s
                    n = 3 * t
                    if s == 0:
                        dve.wait_ge(prop_tanh, q)
                        dve.wait_ge(h_ready, t)
                        dve.tensor_scalar(h_prev_p[:, 0, :], h_prev[:, :], 2.0, None, ALU.mult).then_inc(hp_ready, 1)
                        dve.tensor_scalar(h_prev2[:, :], h_prev[:, :], 2.0, None, ALU.mult).then_inc(hp_ready, 1)
                        dve.wait_ge(hp_ready, 3 * q + 2)
                        dve.tensor_tensor(h_prev_p[:, 1, :], h_prev2[:, :], h_prev_p[:, 0, :], ALU.subtract)\
                           .then_inc(hp_ready, 1)
                    prev = h_prev2[:, :] if s == 0 else h2[p][:, s - 1, :]
                    dve.wait_ge(r_tanhed, t + 1)
                    if s > 0:
                        dve.wait_ge(h_ready, t)
                    dve.scalar_tensor_tensor(g_rh_p[:, 0, :], g_r[:, :], 1.0, prev, ALU.add, ALU.mult).then_inc(rh_ready, 1)
                    dve.scalar_tensor_tensor(g_rh[:, :], g_r[:, :], 1.0, prev, ALU.add, ALU.mult).then_inc(rh_ready, 1)
                    dve.wait_ge(rh_ready, n + 2)
                    dve.tensor_tensor(g_rh_p[:, 1, :], g_rh[:, :], g_rh_p[:, 0, :], ALU.subtract).then_inc(rh_ready, 1)
                    dve.wait_ge(z_tanhed, t + 1)
                    dve.scalar_tensor_tensor(g_na_p[:, 0, :], g_z[:, :], 1.0, prev, ALU.subtract, ALU.mult)\
                       .then_inc(na_ready, 1)
                    dve.scalar_tensor_tensor(g_na[:, :], g_z[:, :], 1.0, prev, ALU.subtract, ALU.mult).then_inc(na_ready, 1)
                    dve.wait_ge(na_ready, n + 2)
                    dve.tensor_tensor(g_na_p[:, 1, :], g_na[:, :], g_na_p[:, 0, :], ALU.subtract).then_inc(na_ready, 1)
                    if s == 1 and side:
                        router(q - 1, 1 - p, 0)
                    dve.wait_ge(c_tanh, t + 1)
                    dve.scalar_tensor_tensor(g_e_p[:, 0, :], g_z[:, :], 1.0, g_c[:, :], ALU.add, ALU.mult).then_inc(e_ready, 1)
                    dve.scalar_tensor_tensor(g_e[:, :], g_z[:, :], 1.0, g_c[:, :], ALU.add, ALU.mult).then_inc(e_ready, 1)
                    dve.wait_ge(e_ready, n + 2)
                    dve.tensor_tensor(g_e_p[:, 1, :], g_e[:, :], g_e_p[:, 0, :], ALU.subtract).then_inc(e_ready, 1)
                    if s == 0 and valid(q - 2):
                        dve.wait_ge(sh_done, q - 1)
                        dve.wait_ge(lg_done, q - 1)
                        dve.wait_ge(hT_done, q - 1)
                    dve.scalar_tensor_tensor(h2[p][:, s, :], g_na[:, :], -0.5, g_e[:, :],
                                             ALU.mult, ALU.add).then_inc(h_ready, 1)
                    if s == 1 and side:
                        router(q - 1, 1 - p, 1)
                    if s == 2 and side:
                        shared_act(q - 1)
                    if s == 0 and valid(q - 2):
                        add_shared(q - 2)
                        place()

            def router(j, p, part):
                n = ROUTER_STEPS * j
                if part == 0:
                    dve.wait_ge(lg_done, j + 1)
                    dve.tensor_scalar(lg[p][:, :], l_ps[:, 0:E], 1.0 / TAU, None, ALU.mult).then_inc(lg_read, 1)
                    dve.wait_ge(lg_read, j + 1)
                    dve.tensor_copy(touched[:, 0:1], lg[p][:, 0:1])
                    dve.max(top[p][:, :], lg[p][:, :]).then_inc(rt, 1)
                else:
                    dve.wait_ge(rt, n + 1)
                    dve.tensor_copy(top_v[:, ds(j, 1), :].rearrange("q a n -> q (a n)"), top[p][:, 0:2])
                    dve.max_index(tix[p][:, :], top[p][:, :], lg[p][:, :]).then_inc(rt, 1)
                    dve.wait_ge(rt, n + 2)
                    dve.tensor_copy(top_i[:, ds(j, 1), :].rearrange("q a n -> q (a n)"), tix[p][:, 0:2]).then_inc(rt, 1)

            def shared_act(j):
                dve.wait_ge(s_gelu, j + 1)
                if valid(j, 1):
                    dve.wait_ge(sT_done, j)
                dve.tensor_tensor(s_act[:, :], a_ps[:, 0:HS], s_gl[:, :], ALU.mult).then_inc(s_act_ready, 1)

            def add_shared(j):
                dve.wait_ge(sy_done, j + 1)
                r = res[:, ds(j, 1), :].rearrange("q a n -> q (a n)")
                dve.tensor_tensor(r, r, y_ps[:, 0:D], ALU.add).then_inc(res_ready, 1)

            def place():
                dve.tensor_tensor(where_q[:, :], y_ps[:, rank_at:rank_at + E], region_at[:, :],
                                  ALU.add).then_inc(rank_ready, 1)

            dve.wait_ge(h0_in, 32)
            dve.wait_ge(consts, 11)
            gru_quad(0, 0)
            gru_quad(0, 1)
            dve.wait_ge(res_in, 16)
            with dve.Fori(1, QUADS // 2) as k:
                gru_quad(k, 0)
                gru_quad(k, 1)
            add_shared(QUADS - 2)
            place()
            router(QUADS - 1, 1, 0)
            router(QUADS - 1, 1, 1)
            dve.wait_ge(l1_in, 16 * 11)
            for n, w in enumerate((w1_raw, w2_raw)):
                dve.tensor_reduce(w_abs[:, n:n + 1], w[:, :], AX_X, ALU.add, apply_absolute_value=True)\
                   .then_inc(wsum_ready, 1)
            shared_act(QUADS - 1)
            dve.wait_ge(rank_done, 1)
            place()
            dve.wait_ge(count_done, 1)
            count = l_ps[:, count_at:count_at + E]
            dve.tensor_tensor(tail_f[:, :], l_ps[0:1, count_at:count_at + E], region_at[0:1, :], ALU.add).then_inc(sl, 1)
            dve.tensor_scalar(cnt[:, 0, :], count, 1.0 / P, 0.5 - 0.5 / P, ALU.mult, ALU.add).then_inc(sl, 1)
            dve.wait_ge(sl, 1)
            dve.tensor_copy(tail[:, :], tail_f[:, :]).then_inc(tail_ready, 1)
            dve.wait_ge(sl, 2)
            dve.tensor_scalar(cnt[:, 1, :], cnt[:, 0, :], MAGIC, None, ALU.add).then_inc(sl, 1)
            dve.wait_ge(sl, 3)
            dve.tensor_scalar(cnt[:, 2, :], cnt[:, 1, :], MAGIC, None, ALU.subtract).then_inc(sl, 1)
            dve.wait_ge(sl, 4)
            dve.tensor_tensor_scan(ends[:, :], ones_e[:, :], cnt[:, 2, :], 0.0, ALU.mult, ALU.add).then_inc(sl, 1)
            dve.tensor_scalar(spare[:, :], cnt[0:1, 2, :], -float(P), float(REGION), ALU.mult, ALU.add).then_inc(sl, 1)
            dve.wait_ge(sl, 6)
            dve.tensor_tensor(past[:, :, :], ends[0:1, :].unsqueeze(1).to_broadcast([1, N_TABLE, E]),
                              iota_t[:, :].unsqueeze(2).to_broadcast([1, N_TABLE, E]), ALU.is_le).then_inc(sl, 1)
            dve.wait_ge(sl, 7)
            dve.tensor_tensor(past_spare[:, :, :], past[:, :, :],
                              spare[:, :].unsqueeze(1).to_broadcast([1, N_TABLE, E]), ALU.mult).then_inc(sl, 1)
            dve.wait_ge(sl, 8)
            dve.tensor_reduce(start_s[:, :], past_spare[:, :, :], AX_X, ALU.add).then_inc(sl, 1)
            dve.wait_ge(sl, 9)
            dve.scalar_tensor_tensor(start_f[:, :], iota_t[:, :], float(P), start_s[:, :], ALU.mult, ALU.add)\
               .then_inc(sl, 1)
            dve.wait_ge(sl, 10)
            dve.tensor_scalar(start_m[:, :], start_f[:, :], float(E * REGION), None, ALU.min).then_inc(sl, 1)
            dve.wait_ge(sl, 11)
            dve.tensor_copy(start_row[:, :], start_m[:, :]).then_inc(start_ready, 1)
            dve.tensor_reduce(eid_f[:, :], past[:, :, :], AX_X, ALU.add).then_inc(sl, 1)
            dve.wait_ge(sl, 12)
            dve.tensor_scalar(eid_m[:, :], eid_f[:, :], float(E - 1), None, ALU.min).then_inc(sl, 1)
            dve.wait_ge(sl, 13)
            dve.tensor_copy(eid[:, :], eid_m[:, :]).then_inc(eid_ready, 1)
            add_shared(QUADS - 1)
            dve.tensor_tensor(cnt[:, 3, :], ends[:, :], cnt[:, 2, :], ALU.subtract).then_inc(sl, 1)
            dve.wait_ge(sl, 14)
            dve.scalar_tensor_tensor(shift[:, :], cnt[:, 3, :], float(P), region_at[:, :], ALU.mult,
                                     ALU.subtract).then_inc(sl, 1)
            dve.wait_ge(rt, ROUTER_STEPS * QUADS)
            for k in range(2):
                dve.tensor_tensor(hot[:, k, :, :], iota_e[:, :].unsqueeze(1).to_broadcast([P, QUADS, E]),
                                  top_i[:, :, k:k + 1].to_broadcast([P, QUADS, E]), ALU.is_equal).then_inc(sl, 1)
            dve.wait_ge(sl, 17)
            for k in range(2):
                dve.tensor_tensor(picked[:, k, :, :], hot[:, k, :, :],
                                  shift[:, :].unsqueeze(1).to_broadcast([P, QUADS, E]), ALU.mult).then_inc(sl, 1)
            dve.tensor_tensor(v_gap[:, :], top_v[:, :, 0], top_v[:, :, 1], ALU.subtract).then_inc(gap_ready, 1)
            dve.wait_ge(wsum_done, 1)
            dve.tensor_scalar(w_mean[:, :], l_ps[:, wsum_at:wsum_at + 2], 1.0 / (D * HID), EPS, ALU.mult, ALU.max).then_inc(wq, 1)
            dve.wait_ge(wq, 1)
            dve.reciprocal(w_inv[:, :], w_mean[:, :]).then_inc(wq, 1)
            for n in range(2):
                dve.tensor_scalar(step4[:, 2 * n:2 * n + 2], w_mean[:, n:n + 1].to_broadcast([P, 2]), 1.0 / 127.0, None,
                                  ALU.mult).then_inc(wq, 1)

            def slot_rows():
                dve.wait_ge(sl, 19)
                dve.tensor_reduce(shift_f[:, :, :], picked[:, :, :, :], AX_X, ALU.add).then_inc(sl, 1)
                dve.wait_ge(sl, 20)
                dve.wait_ge(picks, PICK_STEPS * QUADS)
                dve.tensor_tensor(slot_f[:, :, :], shift_f[:, :, :], sent_f[:, :, :], ALU.add).then_inc(sl, 1)
                dve.wait_ge(sl, 21)
                dve.tensor_copy(slot[:, :, :], slot_f[:, :, :]).then_inc(slot_ready, 1)
                dve.wait_ge(th_ready, 1)
                dve.tensor_scalar(pick_w[:, 0, :], th[:, :], 0.5, 0.5, ALU.mult, ALU.add).then_inc(pw_ready, 1)
                dve.tensor_scalar(pick_w[:, 1, :], th[:, :], -0.5, 0.5, ALU.mult, ALU.add).then_inc(pw_ready, 1)

            def ternary(n):
                w, wq_out = ((w1_raw, w1_q), (w2_raw, w2_q))[n]
                dve.wait_ge(wq, 4 + 2 * n)
                dve.tensor_scalar(wq_tmp[:, 0, :], w[:, :], w_inv[:, n:n + 1], MAGIC, ALU.mult, ALU.add).then_inc(wq, 1)
                dve.wait_ge(wq, 5 + 2 * n)
                dve.tensor_scalar(wq_tmp[:, 1, :], wq_tmp[:, 0, :], MAGIC + 1.0, MAGIC - 1.0, ALU.min, ALU.max)\
                   .then_inc(wq, 1)
                dve.wait_ge(wq, 6 + 2 * n)
                dve.tensor_scalar(wq_out[:, :], wq_tmp[:, 1, :], MAGIC, None, ALU.subtract).then_inc(wq_ready, 1)

            def low_part(i, p):
                dve.wait_ge(xg_hi_ready, i + 1)
                dve.tensor_tensor(xg_t[p][:, 1, :], ex_ps[:, 0:P], xg_t[p][:, 0, :], ALU.subtract)\
                   .then_inc(xg_t_ready, 1)

            def expert(k, p):
                i = 2 * k + p
                if valid(i + 1, 0, N_SLOT_TILES):
                    low_part(i + 1, 1 - p)
                if valid(i, 0, N_SLOT_TILES):
                    dve.wait_ge(e_gelu, i + 1)
                    dve.wait_ge(up_done, 2 * i + 2)
                    if valid(i - 2, 0, N_SLOT_TILES):
                        dve.wait_ge(eT_done, i - 1)
                    dve.scalar_tensor_tensor(e_act[p][:, :], ea_ps[p][:, 0:HR], 1.0 / W_SCALE, e_gl[p][:, :], ALU.mult,
                                             ALU.mult).then_inc(e_act_ready, 1)
                if valid(i - 2, 0, N_SLOT_TILES):
                    dve.wait_ge(ey_done, i - 1)
                    if valid(i - 4, 0, N_SLOT_TILES):
                        dve.wait_ge(e_y_out[p], 16 * (k - 1))
                    dve.tensor_copy(e_y[p][:, :], ey_ps[p][:, 0:D]).then_inc(e_y_ready, 1)

            low_part(0, 0)
            expert(0, 0)
            slot_rows()
            expert(0, 1)
            ternary(0)
            expert(1, 0)
            ternary(1)
            expert(1, 1)
            with dve.Fori(2, N_SLOT_TILES // 2) as k:
                expert(k, 0)
                expert(k, 1)
            for i in range(N_SLOT_TILES // 2 * 2, N_SLOT_TILES + 2):
                expert(i // 2, i % 2)

            dve.wait_ge(pw_ready, 2)
            dve.wait_ge(mv_init, 3)
            dve.wait_ge(res_ready, QUADS)

            def row(j):
                return res[:, ds(j, 1), :].rearrange("q a n -> q (a n)")

            def layer1(m, at):
                has_c, has_1, has_3, has_5 = (valid(m + i, 0, PAIRS) for i in (1, -1, -3, -5))
                done = [0]

                def sig(ins):
                    ins.then_inc(dv, 1)
                    done[0] += 1
                    return done[0]

                def after(n):
                    dve.wait_ge(dv, at + n)

                def picked_row(k, p):
                    return y_got[:, k, ds(2 * (m + 1) + p, 1), :].rearrange("q a n -> q (a n)")

                def summed(p):
                    if has_c:
                        if p == 0:
                            dve.wait_ge(gathered, 64 * (m + 2))
                        dve.scalar_tensor_tensor(y_sum[:, p, :], picked_row(0, p), pick_w[:, 0, ds(2 * (m + 1) + p, 1)],
                                                 row(2 * (m + 1) + p), ALU.mult, ALU.add)

                def combined(p):
                    if has_c:
                        if p == 0 and valid(m, 0, PAIRS):
                            dve.wait_ge(x1T_done, m + 1)
                            dve.wait_ge(x1_kept, m + 1)
                        dve.scalar_tensor_tensor(x1[:, p, :], picked_row(1, p), pick_w[:, 1, ds(2 * (m + 1) + p, 1)],
                                                 y_sum[:, p, :], ALU.mult, ALU.add).then_inc(x1_ready, 1)

                def centred1(p):
                    if has_1:
                        ins = dve.scalar_tensor_tensor(n1[:, p, :], rt_ps[:, p * P:(p + 1) * P], mv[:, p, 0:1],
                                                       ln1w_sb[:, :], ALU.subtract, ALU.mult)
                        if p == 1:
                            ins.then_inc(n1_read, 1)

                def centred2(p):
                    if has_3:
                        ins = dve.scalar_tensor_tensor(n2[:, p, :], gel[:, p, :], mv[:, 2 + p, 0:1], ln2w_sb[:, :],
                                                       ALU.subtract, ALU.mult)
                        if p == 1:
                            ins.then_inc(n2_read, 1)

                def results_can_go():
                    if has_5:
                        dve.wait_ge(m2_done, 2 * m - 8)
                        if valid(m - 6, 0, PAIRS):
                            for p in range(2):
                                dve.wait_ge(o_out[p], 16 * (m - 5))

                def result(p):
                    if has_5:
                        dve.scalar_tensor_tensor(o_sb[p][:, :], m2_ps[:, p * P:(p + 1) * P],
                                                 dq_out[:, p:p + 1], row(2 * (m - 5) + p), ALU.mult,
                                                 ALU.add).then_inc(o_ready, 1)

                n = 0
                if has_1:
                    dve.wait_ge(rT_done, 2 * m)
                    for p in range(2):
                        n = sig(dve.bn_stats(stats[:, p, :], rt_ps[:, p * P:(p + 1) * P]))
                if has_3:
                    dve.wait_ge(gel_ready, 2 * m - 4)
                    for p in range(2):
                        n = sig(dve.bn_stats(stats[:, 2 + p, :], gel[:, p, :]))
                if has_1 or has_3:
                    summed(0)
                    after(n)
                    sig(dve.tensor_copy(touched[:, 1:2], stats[:, 0, 0:1]))
                    for i, has in ((0, has_1), (1, has_1), (2, has_3), (3, has_3)):
                        if has:
                            n = sig(dve.bn_aggr(mv[:, i, :], stats[:, i, :]))
                    summed(1)
                    after(n)
                    n = sig(dve.tensor_scalar(var_e[:, :], mv[:, :, 1], EPS, None, ALU.add))
                    combined(0)
                    after(n)
                    n = sig(dve.tensor_scalar(half_bits[:, :], var_e[:, :].bitcast(I32), 1, None, ALU.logical_shift_right))
                    combined(1)
                    after(n)
                    n = sig(dve.tensor_scalar(guess[:, :].bitcast(I32), half_bits[:, :], -1.0, float(0x5F3759DF),
                                              ALU.mult, ALU.add))
                    centred1(0)
                    after(n)
                    n = sig(dve.tensor_tensor(rsq_t[:, 0, :], guess[:, :], guess[:, :], ALU.mult))
                    centred1(1)
                    after(n)
                    n = sig(dve.tensor_tensor(rsq_t[:, 1, :], rsq_t[:, 0, :], var_e[:, :], ALU.mult))
                    if has_1 and valid(m - 2, 0, PAIRS):
                        dve.wait_ge(qm1_ready, 2 * m - 2)
                    centred2(0)
                    after(n)
                    n = sig(dve.scalar_tensor_tensor(rsq_t[:, 2, :], rsq_t[:, 1, :], -10.0 / 3.0, rsq_t[:, 1, :],
                                                     ALU.add, ALU.mult))
                    centred2(1)
                    after(n)
                    n = sig(dve.scalar_tensor_tensor(better[:, :], rsq_t[:, 2, :], 5.0, guess[:, :], ALU.add, ALU.mult))
                    after(n)
                    n = sig(dve.tensor_tensor(rsq_t[:, 3, :], better[:, :], better[:, :], ALU.mult))
                    after(n)
                    n = sig(dve.scalar_tensor_tensor(rsq_t[:, 4, :], rsq_t[:, 3, :], -27.0 / 1024.0, var_e[:, :], ALU.mult,
                                                     ALU.mult))
                    after(n)
                    n = sig(dve.scalar_tensor_tensor(rsq[:, :], rsq_t[:, 4, :], 0.5625, better[:, :], ALU.add, ALU.mult))
                    after(n)
                    for p in range(2):
                        if has_1:
                            n = n_ln1 = sig(dve.scalar_tensor_tensor(ln1[:, p, :], n1[:, p, :], rsq[:, p:p + 1],
                                                                     ln1b_sb[:, :], ALU.mult, ALU.add))
                    if has_3 and valid(m - 4, 0, PAIRS):
                        dve.wait_ge(q2_ready, 2 * m - 6)
                    for p in range(2):
                        if has_3:
                            n = sig(dve.scalar_tensor_tensor(ln2[:, p, :], n2[:, p, :], rsq[:, 2 + p:3 + p],
                                                             ln2b_sb[:, :], ALU.mult, ALU.add))
                    if has_1:
                        after(n_ln1)
                        n_max = sig(dve.tensor_reduce(amax[:, 0:2], ln1[:, :, :], AX_X, ALU.max,
                                                      apply_absolute_value=True))
                    if has_3:
                        after(n)
                        n_max = sig(dve.tensor_reduce(amax[:, 2:4], ln2[:, :, :], AX_X, ALU.max,
                                                      apply_absolute_value=True))
                    results_can_go()
                    after(n_max)
                    n = sig(dve.tensor_scalar(amax_e[:, :], amax[:, :], EPS, None, ALU.max))
                    result(0)
                    after(n)
                    n = sig(dve.reciprocal(inv[:, :], amax_e[:, :]))
                    result(1)
                    after(n)
                    n = sig(dve.tensor_scalar(to_int[:, :], inv[:, :], 127.0, None, ALU.mult))
                    after(n)
                    dve.tensor_copy(touched[:, 0:1], to_int[:, 0:1]).then_inc(to_int_ready, 1)
                    n = sig(dve.tensor_copy(dq_out[:, :], dq[:, 2:4]))
                    if valid(m - 2, 0, PAIRS):
                        dve.wait_ge(m1_scaled, 2 * m - 2)
                    after(n)
                    dve.tensor_tensor(dq[:, :], amax_e[:, :], step4[:, :], ALU.mult).then_inc(dq_ready, 1)
                else:
                    if has_c and valid(m, 0, PAIRS):
                        dve.wait_ge(x1_ready, 2 * (m + 1))
                    summed(0)
                    summed(1)
                    n = sig(dve.memset(touched[:, 0:1], 0.0))
                    after(n)
                    combined(0)
                    combined(1)
                    results_can_go()
                    result(0)
                    result(1)
                    if has_5:
                        dve.wait_ge(o_ready, 2 * m - 8)
                        n = sig(dve.tensor_copy(dq_out[:, :], dq[:, 2:4]))
                        after(n)
                return done[0]

            at = 0
            for m in range(-1, 6):
                full = layer1(m, at)
                at += full
            with dve.Fori(2, (PAIRS - 1) // 3) as k:
                for i in range(3):
                    layer1(3 * k + i, at + (3 * k + i - 6) * full)
            at += (PAIRS - 7) * full
            for m in range(PAIRS - 1, PAIRS + 5):
                at += layer1(m, at)




def kernel(**inputs):
    import numpy as np
    import concourse.bacc as bacc
    from concourse import mybir as _mybir
    from concourse.bass_utils import run_bass_kernel_spmd as run

    g = {n: np.asarray(a) for n, a in inputs.items()}
    x = g["x"]
    time_major = x.transpose(1, 0, 2).reshape(TOKENS, D)
    gates = np.stack([g["L0_cond_Wz"], g["L0_cond_Wr"], g["L0_cond_Wh"]])
    gates = gates.reshape(3, 2, P, P).transpose(2, 1, 0, 3).reshape(P, 6 * P)

    def split_rows(w, parts):
        return w.reshape(parts, P, w.shape[-1]).transpose(1, 0, 2).reshape(P, -1)

    laid = {
        "x_t": time_major.T,
        "x_tok": split_rows(time_major, QUADS),
        "h0_t": g["cond_1024"].T,
        "gru_w": gates,
        "gru_wp": g["L0_cond_Wp"],
        "gru_bp": g["L0_cond_bp"][:, None],
        "we1": g["L0_ffn_We1"].transpose(1, 0, 2).reshape(P, -1),
        "we2": g["L0_ffn_We2"].reshape(E, 3, P, D).transpose(2, 0, 1, 3).reshape(P, -1),
        "ws1": g["L0_ffn_Ws1"],
        "ws2": split_rows(g["L0_ffn_Ws2"], 2),
        "wr": g["L0_ffn_Wr"],
        "bias": np.concatenate([g["L0_ffn_be1"].ravel(), g["L0_ffn_be2"].ravel(), g["L0_ffn_bs1"],
                                g["L0_ffn_bs2"], np.pad(g["L0_ffn_br"], (0, P - E)), g["L0_cond_bz"],
                                g["L0_cond_br"], g["L0_cond_bh"]]).reshape(BIAS_ROWS, P),
        "rnn_wx": g["L1_cond_Wx"],
        "rnn_wh": g["L1_cond_Wh"],
        "rnn_b": g["L1_cond_b"][:, None],
        "w1_t": g["L1_ffn_w1"].T,
        "w2_t": split_rows(g["L1_ffn_w2"].T, 4),
        "ln1_w": g["L1_ffn_ln1_w"][None, :],
        "ln1_b": g["L1_ffn_ln1_b"][None, :],
        "b1": g["L1_ffn_b1"][None, :],
        "ln2_w": g["L1_ffn_ln2_w"][None, :],
        "ln2_b": g["L1_ffn_ln2_b"][None, :],
        "b2": g["L1_ffn_b2"][None, :],
    }
    nc = bacc.Bacc("TRN2", target_bir_lowering=False, num_devices=1)
    arrays, args = {}, []
    for name, a in laid.items():
        a = np.ascontiguousarray(a)
        arrays[f"in_{name}"] = a
        args.append(nc.dram_tensor(f"in_{name}", a.shape, _mybir.dt.from_np(a.dtype), kind="ExternalInput").ap())
    args.append(nc.dram_tensor("out_0", (TOKENS, D), F32, kind="ExternalOutput").ap())
    build(nc, *args)
    r = run(nc, [arrays], core_ids=[0])
    got = r.results[0]["out_0"]
    return got.reshape(STEPS, BATCH, D).transpose(1, 0, 2)
```
